# Optimizing a Trainium2 kernel written in Bass

```python
import numpy as np
import jax
import jax.numpy as jnp

def _softmax(x, axis=-1):
    return jax.nn.softmax(x, axis=axis)
def _gelu(x):
    return jax.nn.gelu(x, approximate=True)
def _silu(x):
    return jax.nn.silu(x)
def _sigmoid(x):
    return jax.nn.sigmoid(x)
def _layernorm(x, axis=-1, eps=1e-5):
    m = jnp.mean(x, axis=axis, keepdims=True)
    v = jnp.var(x, axis=axis, keepdims=True)
    return (x - m) / jnp.sqrt(v + eps)
def _scatter_add(tgt, idx, src, axis=0):
    return tgt.at[idx].add(src)
def _segment_sum(src, seg, n):
    return jax.ops.segment_sum(src, seg, n)

kernel_name = 'mk_conv_attn_hybrid_d2_conv_nhwc256_5f5611'

def setup_inputs(seed: int = 0):
    np.random.seed(seed)
    _w = jnp.asarray
    def _rec_inputs():
        import jax
        import jax.numpy as jnp
        _gk = jax.random.key(seed)
        x = -0.0005207 + 1.001 * jax.random.normal(jax.random.fold_in(_gk, 1), (8, 32, 32, 256), jnp.float32)
        return x
    x = _rec_inputs()
    def _L0_conv_setup():
        import jax, jax.numpy as jnp
        import numpy as np
        B, N1, N2, E = (8, 32, 32, 256)
        H = 8
        KD = E // H
        HD = E // H
        L = N1 * N2
        SCALING = KD ** (-0.5)
        LN_EPS = 1e-05

        def _rel_pos_2d():
            half = 1.0 / 10000.0 ** jnp.linspace(0.0, 1.0, KD // 2)
            angle = jnp.repeat(half, 2)
            decay = jnp.log(1.0 - 2.0 ** (-2.0 - 5.0 * jnp.arange(H, dtype=jnp.float32) / H))
            i1 = jnp.arange(N1, dtype=jnp.float32)
            i2 = jnp.arange(N2, dtype=jnp.float32)
            index_k = (i1[:, None] + i2[None, :]).reshape(L)
            sin_k = jnp.sin(index_k[:, None] * angle[None, :])
            cos_k = jnp.cos(index_k[:, None] * angle[None, :])
            sin_q = sin_k[None, None]
            cos_q = cos_k[None, None]
            d = (jnp.abs(i1[:, None, None, None] - i1[None, None, :, None]) + jnp.abs(i2[None, :, None, None] - i2[None, None, None, :])).reshape(L, L)
            mask = jnp.exp(d[None, :, :] * decay[:, None, None])
            mask = jnp.nan_to_num(mask)
            mask = mask / jnp.sqrt(mask.sum(-1, keepdims=True))
            return (sin_q, cos_q, sin_k, cos_k, mask)

        def rotate_every_two(x):
            x1 = x[..., ::2]
            x2 = x[..., 1::2]
            return jnp.stack((-x2, x1), axis=-1).reshape(x.shape)

        def theta_shift(x, sin, cos):
            return x * cos + rotate_every_two(x) * sin
        key = jax.random.key(seed)
        ks = jax.random.split(key, 5)
        gain_qkv = 2.0 ** (-2.5) * (6.0 / (E + E)) ** 0.5
        gain_o = 2.0 ** (-1) * (6.0 / (E + E)) ** 0.5
        x = jax.random.normal(ks[0], (B, N1, N2, E), dtype=jnp.float32)
        Wq = jax.random.uniform(ks[1], (E, E), jnp.float32, -gain_qkv, gain_qkv)
        Wk = jax.random.uniform(ks[2], (E, E), jnp.float32, -gain_qkv, gain_qkv)
        Wv = jax.random.uniform(ks[3], (E, E), jnp.float32, -gain_qkv, gain_qkv)
        Wo = jax.random.uniform(ks[4], (E, E), jnp.float32, -gain_o, gain_o)
        ln_g = jnp.ones((HD,), jnp.float32)
        ln_b = jnp.zeros((HD,), jnp.float32)
        return {'x': x, 'Wq': Wq, 'Wk': Wk, 'Wv': Wv, 'Wo': Wo, 'ln_g': ln_g, 'ln_b': ln_b}
    _L0_conv_all = _L0_conv_setup()
    _L0_conv_in = {k: v for k, v in _L0_conv_all.items() if k in ('Wq', 'Wk', 'Wv', 'Wo', 'ln_g', 'ln_b', )}
    del _L0_conv_all

    def _L1_attn_setup():
        import jax, jax.numpy as jnp
        import numpy as np
        N_EMBD = 256
        B, T, H = (8, 4096, 256)
        key = jax.random.key(seed)
        k1, k2, k3, k4 = jax.random.split(key, 4)
        x = jax.random.normal(k1, (B, T, N_EMBD), dtype=jnp.float32)
        s = 1.0 / np.sqrt(N_EMBD)
        Wk = jax.random.normal(k2, (N_EMBD, H), dtype=jnp.float32) * s
        Wq = jax.random.normal(k3, (N_EMBD, H), dtype=jnp.float32) * s
        Wv = jax.random.normal(k4, (N_EMBD, H), dtype=jnp.float32) * s
        return {'x': x, 'Wk': Wk, 'Wq': Wq, 'Wv': Wv}
    _L1_attn_all = _L1_attn_setup()
    _L1_attn_in = {k: v for k, v in _L1_attn_all.items() if k in ('Wk', 'Wq', 'Wv', )}
    del _L1_attn_all

    def _L1_ffn_setup():
        import jax, jax.numpy as jnp
        import numpy as np
        BN_EPS = 0.001

        def _bn(h, g, b, m, v):
            return g * (h - m) * jax.lax.rsqrt(v + BN_EPS) + b
        key = jax.random.key(seed)
        ks = jax.random.split(key, 8)
        B, F, Df = (256, 64, 256)
        E, H, D = (8, 256, 256)
        s1 = 1.0 / np.sqrt(Df)
        s2 = 1.0 / np.sqrt(H)
        return {'x': jax.random.normal(ks[0], (B, F, Df), jnp.float32), 'Wr': jax.random.normal(ks[1], (Df, E), jnp.float32) * s1, 'br': jnp.zeros((E,), jnp.float32), 'W1': jax.random.normal(ks[2], (E, Df, H), jnp.float32) * s1, 'b1': jnp.zeros((E, H), jnp.float32), 'g1': jnp.ones((E, H), jnp.float32), 'be1': jnp.zeros((E, H), jnp.float32), 'm1': jnp.zeros((E, H), jnp.float32), 'v1': jnp.ones((E, H), jnp.float32), 'W2': jax.random.normal(ks[3], (E, H, H), jnp.float32) * s2, 'b2': jnp.zeros((E, H), jnp.float32), 'g2': jnp.ones((E, H), jnp.float32), 'be2': jnp.zeros((E, H), jnp.float32), 'm2': jnp.zeros((E, H), jnp.float32), 'v2': jnp.ones((E, H), jnp.float32), 'Wo': jax.random.normal(ks[4], (E, H, D), jnp.float32) * s2, 'bo': jnp.zeros((E, D), jnp.float32)}
    _L1_ffn_all = _L1_ffn_setup()
    _L1_ffn_in = {k: v for k, v in _L1_ffn_all.items() if k in ('Wr', 'br', 'W1', 'b1', 'g1', 'be1', 'm1', 'v1', 'W2', 'b2', 'g2', 'be2', 'm2', 'v2', 'Wo', 'bo', )}
    del _L1_ffn_all

    return {
        "x": x,
        "L0_conv_Wq": _L0_conv_in["Wq"],
        "L0_conv_Wk": _L0_conv_in["Wk"],
        "L0_conv_Wv": _L0_conv_in["Wv"],
        "L0_conv_Wo": _L0_conv_in["Wo"],
        "L0_conv_ln_g": _L0_conv_in["ln_g"],
        "L0_conv_ln_b": _L0_conv_in["ln_b"],
        "L1_attn_Wk": _L1_attn_in["Wk"],
        "L1_attn_Wq": _L1_attn_in["Wq"],
        "L1_attn_Wv": _L1_attn_in["Wv"],
        "L1_ffn_Wr": _L1_ffn_in["Wr"],
        "L1_ffn_br": _L1_ffn_in["br"],
        "L1_ffn_W1": _L1_ffn_in["W1"],
        "L1_ffn_b1": _L1_ffn_in["b1"],
        "L1_ffn_g1": _L1_ffn_in["g1"],
        "L1_ffn_be1": _L1_ffn_in["be1"],
        "L1_ffn_m1": _L1_ffn_in["m1"],
        "L1_ffn_v1": _L1_ffn_in["v1"],
        "L1_ffn_W2": _L1_ffn_in["W2"],
        "L1_ffn_b2": _L1_ffn_in["b2"],
        "L1_ffn_g2": _L1_ffn_in["g2"],
        "L1_ffn_be2": _L1_ffn_in["be2"],
        "L1_ffn_m2": _L1_ffn_in["m2"],
        "L1_ffn_v2": _L1_ffn_in["v2"],
        "L1_ffn_Wo": _L1_ffn_in["Wo"],
        "L1_ffn_bo": _L1_ffn_in["bo"],
    }

def reference(x, L0_conv_Wq, L0_conv_Wk, L0_conv_Wv, L0_conv_Wo, L0_conv_ln_g, L0_conv_ln_b, L1_attn_Wk, L1_attn_Wq, L1_attn_Wv, L1_ffn_Wr, L1_ffn_br, L1_ffn_W1, L1_ffn_b1, L1_ffn_g1, L1_ffn_be1, L1_ffn_m1, L1_ffn_v1, L1_ffn_W2, L1_ffn_b2, L1_ffn_g2, L1_ffn_be2, L1_ffn_m2, L1_ffn_v2, L1_ffn_Wo, L1_ffn_bo):
    import jax
    import jax.numpy as jnp
    def _L0_conv_ref(x, Wq, Wk, Wv, Wo, ln_g, ln_b):
        import jax, jax.numpy as jnp
        import numpy as np
        B, N1, N2, E = (8, 32, 32, 256)
        H = 8
        KD = E // H
        HD = E // H
        L = N1 * N2
        SCALING = KD ** (-0.5)
        LN_EPS = 1e-05

        def _rel_pos_2d():
            half = 1.0 / 10000.0 ** jnp.linspace(0.0, 1.0, KD // 2)
            angle = jnp.repeat(half, 2)
            decay = jnp.log(1.0 - 2.0 ** (-2.0 - 5.0 * jnp.arange(H, dtype=jnp.float32) / H))
            i1 = jnp.arange(N1, dtype=jnp.float32)
            i2 = jnp.arange(N2, dtype=jnp.float32)
            index_k = (i1[:, None] + i2[None, :]).reshape(L)
            sin_k = jnp.sin(index_k[:, None] * angle[None, :])
            cos_k = jnp.cos(index_k[:, None] * angle[None, :])
            sin_q = sin_k[None, None]
            cos_q = cos_k[None, None]
            d = (jnp.abs(i1[:, None, None, None] - i1[None, None, :, None]) + jnp.abs(i2[None, :, None, None] - i2[None, None, None, :])).reshape(L, L)
            mask = jnp.exp(d[None, :, :] * decay[:, None, None])
            mask = jnp.nan_to_num(mask)
            mask = mask / jnp.sqrt(mask.sum(-1, keepdims=True))
            return (sin_q, cos_q, sin_k, cos_k, mask)

        def rotate_every_two(x):
            x1 = x[..., ::2]
            x2 = x[..., 1::2]
            return jnp.stack((-x2, x1), axis=-1).reshape(x.shape)

        def theta_shift(x, sin, cos):
            return x * cos + rotate_every_two(x) * sin
        sin_q, cos_q, sin_k, cos_k, mask = _rel_pos_2d()
        xf = x.reshape(B, L, E)
        q = (xf @ Wq.T).reshape(B, L, H, KD).transpose(0, 2, 1, 3)
        k = (xf @ Wk.T * SCALING).reshape(B, L, H, KD).transpose(0, 2, 1, 3)
        vr = (xf @ Wv.T).reshape(B, L, H, HD).transpose(0, 2, 1, 3)
        qr = theta_shift(q, sin_q, cos_q)
        kr = theta_shift(k, sin_k[None, None], cos_k[None, None])
        qk = jnp.einsum('bhqd,bhkd->bhqk', qr, kr) * mask[None]
        den = jnp.clip(jax.lax.stop_gradient(jnp.abs(qk)).sum(-1, keepdims=True), 1.0, 50000.0)
        qk = qk / den
        out = jnp.einsum('bhqk,bhkd->bhqd', qk, vr).transpose(0, 2, 1, 3)
        mu = out.mean(-1, keepdims=True)
        var = out.var(-1, keepdims=True)
        out = (out - mu) / jnp.sqrt(var + LN_EPS) * ln_g + ln_b
        out = jax.nn.gelu(out.reshape(B, L, H * HD), approximate=False)
        out = out @ Wo.T
        return out.reshape(B, N1, N2, E)

    def _L1_attn_ref(x, Wk, Wq, Wv):
        import jax, jax.numpy as jnp
        import numpy as np
        N_EMBD = 256
        B, T, H = (8, 4096, 256)
        Bb, Tt, C = x.shape
        k = x @ Wk
        q = x @ Wq
        v = x @ Wv
        scores = jnp.einsum('bth,bsh->bts', q, k) * C ** (-0.5)
        causal = jnp.tril(jnp.ones((Tt, Tt), dtype=bool))
        scores = jnp.where(causal, scores, -jnp.inf)
        wei = jax.nn.softmax(scores, axis=-1)
        return jnp.einsum('bts,bsh->bth', wei, v)

    def _L1_ffn_ref(x, Wr, br, W1, b1, g1, be1, m1, v1, W2, b2, g2, be2, m2, v2, Wo, bo):
        import jax, jax.numpy as jnp
        import numpy as np
        BN_EPS = 0.001

        def _bn(h, g, b, m, v):
            return g * (h - m) * jax.lax.rsqrt(v + BN_EPS) + b
        feat = jnp.mean(x, axis=0)
        w = jax.nn.softmax(feat @ Wr + br, axis=-1)
        h = jnp.einsum('bfd,edh->bfeh', x, W1) + b1
        h = jax.nn.relu(_bn(h, g1, be1, m1, v1))
        h = jnp.einsum('bfeh,ehk->bfek', h, W2) + b2
        h = jax.nn.relu(_bn(h, g2, be2, m2, v2))
        y = jnp.einsum('bfeh,ehd->bfed', h, Wo) + bo
        return jnp.einsum('bfed,fe->bfd', y, w)

    def _gn(v, G=32, eps=1e-5):
        B_, H_, W_, C_ = v.shape
        g = v.reshape(B_, H_, W_, G, C_ // G)
        m = jnp.mean(g, axis=(1, 2, 4), keepdims=True)
        s = jnp.var(g, axis=(1, 2, 4), keepdims=True)
        return ((g - m) / jnp.sqrt(s + eps)).reshape(v.shape)

    def _ln_c(v, eps=1e-6):
        m = jnp.mean(v, axis=-1, keepdims=True)
        s = jnp.var(v, axis=-1, keepdims=True)
        return (v - m) / jnp.sqrt(s + eps)

    def _ln_t(v, eps=1e-5):
        m = jnp.mean(v, axis=-1, keepdims=True)
        s = jnp.var(v, axis=-1, keepdims=True)
        return (v - m) / jnp.sqrt(s + eps)

    def _to_tokens(v):
        B_, H_, W_, C_ = v.shape
        return v.reshape(B_, H_ * W_, C_)
    def _from_tokens(t, like):
        return t.reshape(like.shape)

    x = x + _L0_conv_ref(_gn(x), L0_conv_Wq, L0_conv_Wk, L0_conv_Wv, L0_conv_Wo, L0_conv_ln_g, L0_conv_ln_b)
    t = _to_tokens(x)
    t = t + _L1_attn_ref(_ln_t(t), L1_attn_Wk, L1_attn_Wq, L1_attn_Wv)
    t = t + _L1_ffn_ref(_ln_t(t), L1_ffn_Wr, L1_ffn_br, L1_ffn_W1, L1_ffn_b1, L1_ffn_g1, L1_ffn_be1, L1_ffn_m1, L1_ffn_v1, L1_ffn_W2, L1_ffn_b2, L1_ffn_g2, L1_ffn_be2, L1_ffn_m2, L1_ffn_v2, L1_ffn_Wo, L1_ffn_bo)
    x = _from_tokens(t, x)
    return x


_drawn_inputs = setup_inputs


def setup_inputs(seed=0):
    import zlib

    import numpy as np

    out = dict(_drawn_inputs(seed))
    spreads = {'L0_conv_ln_g': (1.0, 0.2),
     'L0_conv_ln_b': (0.0, 0.1),
     'L1_ffn_br': (0.0, 0.555),
     'L1_ffn_b1': (0.0, 0.414),
     'L1_ffn_g1': (1.0, 0.2),
     'L1_ffn_be1': (0.0, 0.456),
     'L1_ffn_m1': (0.0, 0.431),
     'L1_ffn_v1': (1.0, 0.6),
     'L1_ffn_b2': (0.0, 0.303),
     'L1_ffn_g2': (1.0, 0.2),
     'L1_ffn_be2': (0.0, 0.348),
     'L1_ffn_m2': (0.0, 0.299),
     'L1_ffn_v2': (1.0, 0.6),
     'L1_ffn_bo': (0.0, 0.1)}
    factors = {}
    for name, (base, spread) in spreads.items():
        noise = np.random.default_rng([zlib.crc32(name.encode()), seed]).standard_normal(out[name].shape)
        drawn = base * np.exp(spread * noise) if base else spread * noise
        out[name] = jnp.asarray(drawn.astype(out[name].dtype))
    for name, factor in factors.items():
        out[name] = (out[name] * factor).astype(out[name].dtype)
    return out
```

```python
from contextlib import ExitStack

import numpy as np

import concourse.bass as bass
from concourse import mybir

ALU = mybir.AluOpType
ACT = mybir.ActivationFunctionType
AX = mybir.AxisListType
F32 = mybir.dt.float32
F32R = mybir.dt.float32r


def layer0(nc, x, xT, wqT, wkT, wvT, woT, lng, lnb, window, rowscale, cosT, sinT, avg8, ident, headpick, x1):
    B, L, E = x.shape
    H, HD = 8, E // 8
    QC = 512
    KT = L // 128
    STEPS, PHASES = 4 * KT, 4
    ROWS = L // 32
    CROWS = QC // 32
    LN_EPS, GN_EPS = 1e-5, 1e-5
    SCALING = float(HD) ** -0.5
    STACK = 16 * 16

    A_HEAD = ["gn1", "gn2", "k", "k'", "v", "v'", "q"]
    A_MID = ["q0", "dT3'", "k0", "v0", "q1", "dT0", "k1", "v1", "q2", "dT1", "gn1", "gn2", "k2", "v2",
             "q3", "dT2", "k3", "v3"]
    A_FIRST = [t for t in A_MID if t != "dT3'"]
    A_LAST = [t for t in A_MID if t not in ("gn1", "gn2", "k2", "v2", "q3", "k3", "v3")] + ["dT3'"]
    B_MID = ["nT3'", "zT3'", "o2'", "o3'", "nT0", "zT0", "nT1", "zT1", "nT2", "zT2", "o0", "o1"]
    B_FIRST = B_MID[4:]
    B_LAST = B_MID + B_MID[:4]

    def order(name, b, first, last, lists, head):
        one, mid, end = lists
        if first:
            return head + one.index(name)
        if last:
            n = len(end) - 1 - end[::-1].index(name) if last == "after" else end.index(name)
            return head + len(one) + len(mid) * (B - 2) + n
        return head + len(one) + len(mid) * (b - 1) + mid.index(name)

    def a_order(name, b, first, last):
        return order(name, b, first, last, (A_FIRST, A_MID, A_LAST), len(A_HEAD))

    def b_order(name, b, first, last):
        return order(name, b, first, last, (B_FIRST, B_MID, B_LAST), 0)

    def prep_order(name, b):
        return 3 + 8 * b + ["q0", "k0", "q1", "k1", "q2", "k2", "q3", "k3"].index(name)

    with ExitStack() as ctx:
        def sb(name, shape, dt=F32):
            return ctx.enter_context(nc.sbuf_tensor("l0_" + name, shape, dt))

        def sem(name):
            return ctx.enter_context(nc.semaphore("l0_" + name))

        win = sb("window", [128, H, (2 * ROWS - 4) * 32])
        rsc = sb("rowscale", [128, 2, ROWS])
        cos_sb, sin_sb = sb("cos", [128, L]), sb("sin", [128, L])
        wq, wk, wv, wo = (sb(n, [128, 2, E]) for n in ("wq", "wk", "wv", "wo"))
        avg, idn, pick = sb("avg8", [128, 128]), sb("ident", [128, 128]), sb("pick", [128, 4])
        ones = sb("ones", [128, HD])
        lngb = sb("lngb", [128, 2])
        raw, xn = sb("raw", [128, 2, L]), sb("xn", [128, 2, L])
        t1, t2 = sb("t1", [128, QC]), sb("t2", [128, QC])
        hi, lo = sb("hi", [128, QC], F32R), sb("lo", [128, QC], F32R)
        kst = [sb(f"kst{g}", [128, 4, L], F32R) for g in range(2)]
        qst = [sb(f"qst{c}", [128, 4, QC], F32R) for c in range(2)]
        vsb = [sb(f"v{g}", [128, KT, 128]) for g in range(2)]
        prod = [sb(f"prod{n}", [128, 2, QC]) for n in range(4)]
        absp = [sb(f"absp{n}", [128, 2, QC]) for n in range(4)]
        tA, tB = sb("tA", [128, 4, 128]), sb("tB", [128, 4, 128])
        z = sb("z", [128, 2, L])
        xo = [sb(f"xo{n}", [128, 2, E]) for n in range(2)]
        stats, mv = sb("stats", [128, 2, 2, 6]), sb("mv", [128, 2, 2])
        gmean, dmean, gvar, grstd = (sb(n, [128, 2]) for n in ("gmean", "dmean", "gvar", "grstd"))
        mhalf = sb("mhalf", [128, 16])
        nsum, nmean, rden, sqs, var, rstd, fac = (sb(n, [128, 16]) for n in
                                                  ("nsum", "nmean", "rden", "sqs", "var", "rstd", "fac"))

        def bank(name, shape):
            return ctx.enter_context(nc.psum_tensor("l0_" + name, shape, F32))

        sc = [bank(f"scores{j}", [128, 2, QC]) for j in range(2)]
        num, den = bank("num", [128, QC]), bank("den", [128, QC])
        pA, pB = bank("bankA", [128, QC]), bank("bankB", [128, QC])

        def sems(names):
            return (sem(n) for n in names.split())

        consts, made, x_in, waited = sems("consts made x_in waited")
        stats_done, agg_done, gmean_ready, gvar_ready = sems("stats_done agg_done gmean_ready gvar_ready")
        geps_ready, grstd_ready, xn_ready = sems("geps_ready grstd_ready xn_ready")
        scores_ready, prod_ready, abs_ready, av_done, den_done = sems("scores_ready prod_ready abs_ready av_done den_done")
        a_ready, a_free, b_ready, b_free = sems("a_ready a_free b_ready b_free")
        t1_ready, shuffled, rot_ready, sum_ready = sems("t1_ready shuffled rot_ready sum_ready")
        hi_ready, lo_ready, q_stacked, v_ready = sems("hi_ready lo_ready q_stacked v_ready")
        n_taken, d_taken, nsum_ready, nmean_ready, centred = sems("n_taken d_taken nsum_ready nmean_ready centred")
        sq_ready, rden_ready, u_step, u_ready, rstd_ready = sems("sq_ready rden_ready u_step u_ready rstd_ready")
        fac_ready, on_ready, z_ready, o_added = sems("fac_ready on_ready z_ready o_added")
        k_stacked = [sem(f"k_stacked{c}") for c in range(2)]
        xo_in = [sem(f"xo_in{n}") for n in range(2)]
        xo_out = [sem(f"xo_out{n}") for n in range(2)]

        NCONST = 13

        def nphase(b, p, prev):
            return 4 * b - 1 if prev else 4 * b + p

        block = ctx.enter_context(nc.Block())

        @block.sync
        def _(sp):
            sp.dma_start(raw[:], xT[0].rearrange("(k p) t -> p k t", p=128)).then_inc(x_in, 16)
            for dst, src in ((avg[:], avg8), (wk[:], wkT.rearrange("(k p) n -> p k n", p=128)),
                             (wq[:], wqT.rearrange("(k p) n -> p k n", p=128)),
                             (wv[:], wvT.rearrange("(k p) n -> p k n", p=128)),
                             (cos_sb[:], cosT), (sin_sb[:], sinT), (rsc[:], rowscale),
                             (win[:], window), (idn[:], ident), (pick[:], headpick),
                             (wo[:], woT.rearrange("(k p) n -> p k n", p=128)),
                             (lngb[:, 0:1], lng), (lngb[:, 1:2], lnb)):
                sp.dma_start(dst, src).then_inc(consts, 16)

            def stack(n, dst, quads, done):
                sp.wait_ge(hi_ready, n + 1)
                for part, tile, ready in (("hi", hi, None), ("lo", lo, lo_ready)):
                    if ready is not None:
                        sp.wait_ge(ready, n + 1)
                    for quad in range(4):
                        if quads[quad] == part:
                            for h in range(4):
                                sp.dma_start(dst[32 * quad:32 * quad + 32, h, :].bitcast(F32),
                                             tile[32 * h:32 * h + 32, :].bitcast(F32)).then_inc(done, 16)

            QUADS = {"q": ("hi", "hi", "lo", "lo"), "k": ("hi", "lo", "hi", "lo")}
            stack(0, kst[0][:, :, 0:QC], QUADS["k"], k_stacked[0])
            stack(1, kst[0][:, :, QC:L], QUADS["k"], k_stacked[1])
            stack(2, qst[0][:, :, :], QUADS["q"], q_stacked)

            def load_x(n, bb, t0, count):
                if count is not None:
                    sp.wait_ge(xo_out[n], count)
                sp.dma_start(xo[n][:], x[bb, t0:t0 + 256, :].rearrange("(t p) e -> p t e", p=128)).then_inc(xo_in[n], 16)

            def store_x(n, bb, t0, added):
                sp.wait_ge(o_added, added)
                sp.dma_start(x1[bb, t0:t0 + 256, :].rearrange("(t p) e -> p t e", p=128), xo[n][:]).then_inc(xo_out[n], 16)

            def body(b, first, last):
                if not last:
                    sp.wait_ge(xn_ready, 2 * b + 2)
                    sp.dma_start(raw[:], xT[b + 1].rearrange("(k p) t -> p k t", p=128)).then_inc(x_in, 16)
                if not first:
                    for n in range(2):
                        load_x(n, b - 1, QC + 256 * n, 16 * (2 * b - 1))
                stack(prep_order("q0", b), qst[1][:, :, :], QUADS["q"], q_stacked)
                stack(prep_order("k0", b), kst[1][:, :, 0:QC], QUADS["k"], k_stacked[0])
                if not first:
                    store_x(0, b - 1, QC, 4 * b - 1)
                    store_x(1, b - 1, QC + 256, 4 * b)
                stack(prep_order("q1", b), qst[0][:, :, :], QUADS["q"], q_stacked)
                stack(prep_order("k1", b), kst[1][:, :, QC:L], QUADS["k"], k_stacked[1])
                stack(prep_order("q2", b), qst[1][:, :, :], QUADS["q"], q_stacked)
                if not last:
                    stack(prep_order("k2", b), kst[0][:, :, 0:QC], QUADS["k"], k_stacked[0])
                for n in range(2):
                    load_x(n, b, 256 * n, None if first else 32 * b)
                if not last:
                    stack(prep_order("q3", b), qst[0][:, :, :], QUADS["q"], q_stacked)
                    stack(prep_order("k3", b), kst[0][:, :, QC:L], QUADS["k"], k_stacked[1])
                store_x(0, b, 0, 4 * b + 1)
                store_x(1, b, 256, 4 * b + 2)

            body(0, True, False)
            with sp.Fori(1, B - 1) as b:
                body(b, False, False)
            body(B - 1, False, True)
            for n in range(2):
                load_x(n, B - 1, QC + 256 * n, 16 * (2 * B - 1))
            for n in range(2):
                store_x(n, B - 1, QC + 256 * n, 4 * B - 1 + n)
            for n in range(2):
                sp.wait_ge(xo_out[n], 32 * B)

        @block.tensor
        def _(pe):
            pe.wait_ge(consts, 16 * NCONST)
            pe.wait_ge(made, 2)

            def a_begin(n):
                if not isinstance(n, int) or n > 0:
                    pe.wait_ge(a_free, n)

            def b_begin(n):
                if not isinstance(n, int) or n > 0:
                    pe.wait_ge(b_free, n)

            def project(n, w, g, c):
                a_begin(n)
                for k in range(2):
                    mm = nc.tensor.matmul(pA[:], w[:, k, 128 * g:128 * g + 128], xn[:, k, QC * c:QC * c + QC],
                                          start=(k == 0), stop=(k == 1))
                mm.then_inc(a_ready, 1)

            def project_v(n, g, half):
                a_begin(n)
                for t in range(4):
                    tok = QC * half + 128 * t
                    for k in range(2):
                        mm = nc.tensor.matmul(pA[:, 128 * t:128 * t + 128], xn[:, k, tok:tok + 128],
                                              wv[:, k, 128 * g:128 * g + 128], start=(k == 0), stop=(k == 1))
                mm.then_inc(a_ready, 1)

            def group_sums(n, rhs, sem_, count):
                a_begin(n)
                pe.wait_ge(sem_, count)
                nc.tensor.matmul(pA[:, 0:2], avg[:], rhs, start=True, stop=True).then_inc(a_ready, 1)

            def transpose_n(n, phase):
                b_begin(n)
                pe.wait_ge(n_taken, phase + 1)
                for t in range(4):
                    mm = nc.tensor.transpose(pB[:, 128 * t:128 * t + 128], tA[:, t, :], idn[:])
                mm.then_inc(b_ready, 1)

            def transpose_d(n, phase):
                a_begin(n)
                pe.wait_ge(d_taken, phase + 1)
                for t in range(4):
                    mm = nc.tensor.matmul(pA[:, 4 * t:4 * t + 4], tB[:, t, :], pick[:], start=True, stop=True)
                mm.then_inc(a_ready, 1)

            def transpose_z(n, phase):
                b_begin(n)
                pe.wait_ge(on_ready, phase + 1)
                for t in range(4):
                    mm = nc.tensor.transpose(pB[:, 128 * t:128 * t + 128], tA[:, t, :], idn[:])
                mm.then_inc(b_ready, 1)

            def out_proj(n, c, half, phases):
                b_begin(n)
                pe.wait_ge(z_ready, phases)
                for t in range(2):
                    tok = QC * c + 256 * half + 128 * t
                    for g in range(2):
                        mm = nc.tensor.matmul(pB[:, 256 * t:256 * t + 256], z[:, g, tok:tok + 128], wo[:, g, :],
                                              start=(g == 0), stop=(g == 1))
                mm.then_inc(b_ready, 1)

            def scores(b, i):
                p, kt = i // KT, i % KT
                g, c = p // 2, p % 2
                if kt == 0:
                    pe.wait_ge(q_stacked, STACK * (4 * b + p + 1))
                if c == 0 and kt % 4 == 0:
                    pe.wait_ge(k_stacked[kt // 4], STACK * (2 * b + g + 1))
                for j in range(2):
                    n = 2 * i + j
                    if n >= 2:
                        pe.wait_ge(prod_ready, 2 * STEPS * b + n - 1)
                    elif not isinstance(b, int) or b > 0:
                        pe.wait_ge(prod_ready, 2 * STEPS * b + n - 1)
                    for s in range(2):
                        h = 2 * j + s
                        mm = nc.tensor.matmul(sc[j][:, s, :], kst[g][:, h, 128 * kt:128 * kt + 128], qst[c][:, h, :],
                                              start=True, stop=True)
                    mm.then_inc(scores_ready, 1)

            def weighted(b, i, first):
                p, kt = i // KT, i % KT
                g = p // 2
                pe.wait_ge(prod_ready, 2 * STEPS * b + 2 * i + 2)
                if p % 2 == 0 and kt % 4 == 0:
                    pe.wait_ge(v_ready, 4 * b + 2 * g + kt // 4 + 1)
                if kt == 0 and not (first and p == 0):
                    pe.wait_ge(n_taken, 4 * b + p)
                for h in range(4):
                    mm = nc.tensor.matmul(num[32 * h:32 * h + 32, :], vsb[g][:, kt, 32 * h:32 * h + 32],
                                          prod[2 * (i % 2) + h // 2][:, h % 2, :], start=(kt == 0), stop=(kt == KT - 1))
                mm.then_inc(av_done, 1)
                pe.wait_ge(abs_ready, 2 * STEPS * b + 2 * i + 2)
                if kt == 0 and not (first and p == 0):
                    pe.wait_ge(d_taken, 4 * b + p)
                for h in range(4):
                    mm = nc.tensor.matmul(den[32 * h:32 * h + 32, :], ones[:],
                                          absp[2 * (i % 2) + h // 2][:, h % 2, :], start=(kt == 0), stop=(kt == KT - 1))
                mm.then_inc(den_done, 1)

            group_sums(0, mv[:, :, 0], agg_done, 1)
            group_sums(1, gvar[:], gvar_ready, 1)
            pe.wait_ge(xn_ready, 2)
            project(2, wk, 0, 0)
            project(3, wk, 0, 1)
            project_v(4, 0, 0)
            project_v(5, 0, 1)
            project(6, wq, 0, 0)
            scores(0, 0)

            def body(b, first, last):
                A = lambda name: a_order(name, b, first, last)
                Bn = lambda name: b_order(name, b, first, last)
                for i in range(STEPS):
                    p, kt = i // KT, i % KT
                    if i + 1 < STEPS:
                        scores(b, i + 1)
                    elif not last:
                        scores(b + 1, 0)
                    weighted(b, i, first)
                    prev = p == 0
                    post = not (prev and first)
                    tag = "3'" if prev else str(p - 1)
                    ph = nphase(b, p - 1, prev)
                    if kt == 0:
                        if post:
                            transpose_n(Bn("nT" + tag), ph)
                        if p < 3 or not last:
                            g, c = ((p + 1) // 2 % 2, (p + 1) % 2)
                            project(A(f"q{p}"), wq, g, c)
                    if kt == 1 and post:
                        transpose_d(A("dT" + tag), ph)
                    if p == 2 and not last:
                        if kt == 2:
                            group_sums(A("gn1"), mv[:, :, 0], agg_done, b + 2)
                        if kt == 3:
                            group_sums(A("gn2"), gvar[:], gvar_ready, b + 2)
                    if p < 2 or not last:
                        if kt == (5 if p == 2 else 4):
                            if p == 2:
                                pe.wait_ge(xn_ready, 2 * b + 4)
                            project(A(f"k{p}"), wk, (1 - p // 2), p % 2)
                        if kt == 6:
                            project_v(A(f"v{p}"), (1 - p // 2), p % 2)
                    if kt == 5 and post:
                        transpose_z(Bn("zT" + tag), ph)
                    if kt == 6 + 0 and p == 3:
                        out_proj(Bn("o0"), 0, 0, 4 * b + 3)
                    if kt == 7 and p == 3:
                        out_proj(Bn("o1"), 0, 1, 4 * b + 3)
                    if kt == 6 and prev and not first:
                        out_proj(Bn("o2'"), 1, 0, 4 * b)
                    if kt == 7 and prev and not first:
                        out_proj(Bn("o3'"), 1, 1, 4 * b)

            body(0, True, False)
            with pe.Fori(1, B - 1) as b:
                body(b, False, False)
            body(B - 1, False, True)
            Bn = lambda name: b_order(name, B - 1, False, "after")
            transpose_n(Bn("nT3'"), 4 * B - 1)
            transpose_d(a_order("dT3'", B - 1, False, "after"), 4 * B - 1)
            transpose_z(Bn("zT3'"), 4 * B - 1)
            out_proj(Bn("o2'"), 1, 0, 4 * B)
            out_proj(Bn("o3'"), 1, 1, 4 * B)

        @block.vector
        def _(dve):
            dve.wait_ge(consts, 16 * NCONST)
            dve.wait_ge(made, 2)

            def q_rotate_in(n, a, g, c):
                if not isinstance(n, int) or n > 0:
                    dve.wait_ge(lo_ready, n)
                dve.wait_ge(a_ready, a + 1)
                nc.vector.tensor_tensor(t1[:].rearrange("p (a b) -> p a b", b=32), pA[:].rearrange("p (a b) -> p a b", b=32),
                                        rsc[:, g, CROWS * c:CROWS * c + CROWS].unsqueeze(2).to_broadcast([128, CROWS, 32]),
                                        ALU.mult).then_inc(t1_ready, 1)

            def rotate(n, c):
                dve.wait_ge(t1_ready, n + 1)
                dve.sem_inc(waited, 1)
                nc.vector.stream_shuffle(t2[:], t1[:], [i ^ 1 for i in range(32)]).then_inc(shuffled, 1)
                dve.wait_ge(shuffled, n + 1)
                nc.vector.tensor_tensor(t1[:], t1[:], cos_sb[:, QC * c:QC * c + QC], ALU.mult).then_inc(rot_ready, 1)
                nc.vector.tensor_tensor(t2[:], t2[:], sin_sb[:, QC * c:QC * c + QC], ALU.mult).then_inc(rot_ready, 1)

            def products(b, i, first):
                p, kt = i // KT, i % KT
                g, c = p // 2, p % 2
                w0 = 32 * (CROWS * c - 4 * kt + ROWS - 4)
                for j in range(2):
                    n = 2 * i + j
                    dve.wait_ge(scores_ready, 2 * STEPS * b + n + 1)
                    if not (first and i < 2):
                        dve.wait_ge(av_done, STEPS * b + i - 1)
                        dve.wait_ge(abs_ready, 2 * STEPS * b + n - 3)
                    nc.vector.tensor_tensor(prod[n % 4][:], sc[j][:], win[:, 4 * g + 2 * j:4 * g + 2 * j + 2, w0:w0 + QC],
                                            ALU.mult).then_inc(prod_ready, 1)

            def take_den(phase):
                dve.wait_ge(den_done, KT * (phase + 1))
                nc.vector.tensor_scalar(tB[:].rearrange("p t c -> p (t c)"), den[:], 1.0, 50000.0, ALU.max,
                                        ALU.min).then_inc(d_taken, 1)

            def centre(n, phase):
                dve.wait_ge(b_ready, n + 1)
                nT = pB[:].rearrange("p (m d) -> p m d", d=32)
                nc.vector.tensor_reduce(nsum[:], nT, AX.X, ALU.add).then_inc(nsum_ready, 1)
                dve.wait_ge(nsum_ready, phase + 1)
                nc.vector.tensor_scalar(nmean[:], nsum[:], -1.0 / HD, None, ALU.mult).then_inc(nmean_ready, 1)
                dve.wait_ge(nmean_ready, phase + 1)
                nc.vector.tensor_tensor(tA[:].rearrange("p t (h d) -> p (t h) d", d=32), nT,
                                        nmean[:].unsqueeze(2).to_broadcast([128, 16, 32]), ALU.add).then_inc(centred, 1)
                dve.wait_ge(centred, phase + 1)
                dve.sem_inc(b_free, 1)

            def take_rden(a, phase):
                dve.wait_ge(a_ready, a + 1)
                nc.vector.reciprocal(rden[:], pA[:, 0:16]).then_inc(rden_ready, 1)
                dve.wait_ge(rden_ready, phase + 1)
                dve.sem_inc(a_free, 1)

            def variance(phase):
                dve.wait_ge(sq_ready, phase + 1)
                nc.vector.tensor_reduce(sqs[:], tB[:].rearrange("p t (h d) -> p (t h) d", d=32), AX.X,
                                        ALU.add).then_inc(u_step, 1)
                nc.vector.tensor_tensor(var[:], rden[:], rden[:], ALU.mult).then_inc(u_step, 1)
                dve.wait_ge(u_step, 3 * phase + 2)
                nc.vector.tensor_tensor(var[:], var[:], sqs[:], ALU.mult).then_inc(u_step, 1)
                dve.wait_ge(u_step, 3 * phase + 3)
                nc.vector.tensor_scalar(var[:], var[:], 1.0 / HD, LN_EPS, ALU.mult, ALU.add).then_inc(u_ready, 1)

            def statistics(b):
                dve.wait_ge(x_in, 16 * (b + 1))
                for k in range(2):
                    for s in range(2):
                        nc.vector.bn_stats(stats[:, k, s, :], raw[:, k, 512 * s:512 * s + 512]).then_inc(stats_done, 1)

            def aggregate(b):
                dve.wait_ge(stats_done, 4 * (b + 1))
                dve.sem_inc(waited, 1)
                for k in range(2):
                    ins = nc.vector.bn_aggr(mv[:, k, :], stats[:, k, :, :].rearrange("p s f -> p (s f)"))
                ins.then_inc(agg_done, 1)

            def group_mean(b, a):
                dve.wait_ge(a_ready, a + 1)
                nc.vector.tensor_copy(gmean[:], pA[:, 0:2]).then_inc(gmean_ready, 1)
                dve.wait_ge(gmean_ready, 3 * b + 1)
                dve.sem_inc(a_free, 1)
                nc.vector.tensor_tensor(dmean[:], mv[:, :, 0], gmean[:], ALU.subtract).then_inc(gmean_ready, 1)
                dve.wait_ge(gmean_ready, 3 * b + 2)
                nc.vector.tensor_tensor(dmean[:], dmean[:], dmean[:], ALU.mult).then_inc(gmean_ready, 1)
                dve.wait_ge(gmean_ready, 3 * b + 3)
                nc.vector.tensor_tensor(gvar[:], mv[:, :, 1], dmean[:], ALU.add).then_inc(gvar_ready, 1)

            def group_var(b, a):
                dve.wait_ge(a_ready, a + 1)
                nc.vector.tensor_scalar(dmean[:], pA[:, 0:2], GN_EPS, None, ALU.add).then_inc(geps_ready, 1)
                dve.wait_ge(geps_ready, b + 1)
                dve.sem_inc(a_free, 1)

            def normalise(b):
                dve.wait_ge(grstd_ready, b + 1)
                for k in range(2):
                    nc.vector.tensor_scalar(xn[:, k, :], raw[:, k, :], gmean[:, k:k + 1], grstd[:, k:k + 1],
                                            ALU.subtract, ALU.mult).then_inc(xn_ready, 1)

            def add_residual(bn, n, k, count):
                dve.wait_ge(b_ready, bn + 1)
                dve.wait_ge(xo_in[n], count)
                nc.vector.tensor_tensor(xo[n][:].rearrange("p t e -> p (t e)"), pB[:], xo[n][:].rearrange("p t e -> p (t e)"),
                                        ALU.add).then_inc(o_added, 1)
                dve.wait_ge(o_added, k)
                dve.sem_inc(b_free, 1)

            def q_take(n, a, g, c):
                q_rotate_in(n, a, g, c)
                dve.wait_ge(t1_ready, n + 1)
                dve.sem_inc(a_free, 1)

            statistics(0)
            aggregate(0)
            group_mean(0, 0)
            group_var(0, 1)
            normalise(0)
            rotate(0, 0)
            rotate(1, 1)
            q_take(2, 6, 0, 0)
            rotate(2, 0)

            def body(b, first, last):
                A = lambda name: a_order(name, b, first, last)
                Bn = lambda name: b_order(name, b, first, last)
                for i in range(STEPS):
                    p, kt = i // KT, i % KT
                    products(b, i, first)
                    prev = p == 0
                    post = not (prev and first)
                    tag = "3'" if prev else str(p - 1)
                    ph = nphase(b, p - 1, prev)
                    if kt == 0 and post:
                        take_den(ph)
                    if kt == 0 and p == 1 and not first:
                        add_residual(Bn("o3'"), 1, 4 * b, 16 * 2 * b)
                    if kt == 0 and p == 0 and not first:
                        add_residual(Bn("nT3'") - 1, 1, 4 * b - 2, 16 * (2 * b - 1))
                    if kt == 1:
                        if p < 3 or not last:
                            g, c = ((p + 1) // 2 % 2, (p + 1) % 2)
                            q_take(prep_order(f"q{p}", b), A(f"q{p}"), g, c)
                        if post:
                            centre(Bn("nT" + tag), ph)
                    if kt == 2:
                        if post:
                            take_rden(A("dT" + tag), ph)
                        if p < 3 or not last:
                            rotate(prep_order(f"q{p}", b), (p + 1) % 2)
                    if kt == 3 and post:
                        variance(ph)
                    if not last:
                        if p == 1 and kt == 4:
                            statistics(b + 1)
                        if p == 1 and kt == 5:
                            aggregate(b + 1)
                        if p == 2 and kt == 3:
                            group_mean(b + 1, A("gn1"))
                        if p == 2 and kt == 4:
                            group_var(b + 1, A("gn2"))
                        if p == 2 and kt == 5:
                            normalise(b + 1)
                    if (p < 2 or not last) and kt == (7 if p == 2 else 6):
                        rotate(prep_order(f"k{p}", b), p % 2)
                    if kt == 7 and p == 3:
                        add_residual(Bn("o0"), 0, 4 * b + 1, 16 * (2 * b + 1))
                    if kt == 7 and prev and not first:
                        add_residual(Bn("o2'"), 0, 4 * b - 1, 32 * b)

            body(0, True, False)
            with dve.Fori(1, B - 1) as b:
                body(b, False, False)
            body(B - 1, False, True)
            Bn = lambda name: b_order(name, B - 1, False, "after")
            take_den(4 * B - 1)
            add_residual(Bn("nT3'") - 1, 1, 4 * B - 2, 16 * (2 * B - 1))
            centre(Bn("nT3'"), 4 * B - 1)
            take_rden(a_order("dT3'", B - 1, False, "after"), 4 * B - 1)
            variance(4 * B - 1)
            add_residual(Bn("o2'"), 0, 4 * B - 1, 32 * B)
            add_residual(Bn("o3'"), 1, 4 * B, 32 * B)

        @block.scalar
        def _(act):
            act.wait_ge(consts, 16 * NCONST)

            def k_take(n, a):
                if not isinstance(n, int) or n > 0:
                    act.wait_ge(lo_ready, n)
                act.wait_ge(a_ready, a + 1)
                nc.scalar.activation(t1[:], pA[:], ACT.Copy, scale=SCALING).then_inc(t1_ready, 1)
                act.wait_ge(t1_ready, n + 1)
                act.sem_inc(a_free, 1)

            def high(n, before, count):
                if before is not None:
                    act.wait_ge(before, count)
                act.wait_ge(sum_ready, n + 1)
                nc.scalar.activation(hi[:], t1[:], ACT.Copy).then_inc(hi_ready, 1)

            def v_take(a, g, half, n):
                act.wait_ge(a_ready, a + 1)
                nc.scalar.activation(vsb[g][:, 4 * half:4 * half + 4, :].rearrange("p t c -> p (t c)"), pA[:],
                                     ACT.Copy).then_inc(v_ready, 1)
                act.wait_ge(v_ready, n)
                act.sem_inc(a_free, 1)

            def absolutes(b, i, first):
                for j in range(2):
                    n = 2 * i + j
                    act.wait_ge(prod_ready, 2 * STEPS * b + n + 1)
                    if not (first and i < 2):
                        act.wait_ge(den_done, STEPS * b + i - 1)
                    nc.scalar.activation(absp[n % 4][:], prod[n % 4][:], ACT.Abs).then_inc(abs_ready, 1)

            def take_num(phase):
                act.wait_ge(av_done, KT * (phase + 1))
                nc.scalar.activation(tA[:].rearrange("p t c -> p (t c)"), num[:], ACT.Copy).then_inc(n_taken, 1)

            def squares(a, phase):
                act.wait_ge(a_ready, a + 1)
                act.wait_ge(centred, phase + 1)
                nc.scalar.activation(tB[:], tA[:], ACT.Square).then_inc(sq_ready, 1)

            def gelu(n, phase, g, c):
                act.wait_ge(b_ready, n + 1)
                nc.scalar.activation(z[:, g, QC * c:QC * c + QC], pB[:], ACT.Gelu, bias=lngb[:, 1:2],
                                     scale=lngb[:, 0:1]).then_inc(z_ready, 1)
                act.wait_ge(z_ready, phase + 1)
                act.sem_inc(b_free, 1)

            def before(name, b):
                if name[0] == "q":
                    p = int(name[1])
                    return k_stacked[(p + 1) % 2], STACK * (2 * b + [1, 2, 2, 3][p])
                return q_stacked, STACK * (4 * b + int(name[1]) + 2)

            k_take(0, 2)
            high(0, None, 0)
            k_take(1, 3)
            high(1, k_stacked[0], STACK)
            v_take(4, 0, 0, 1)
            v_take(5, 0, 1, 2)
            high(2, k_stacked[1], STACK)

            def body(b, first, last):
                A = lambda name: a_order(name, b, first, last)
                Bn = lambda name: b_order(name, b, first, last)
                for i in range(STEPS):
                    p, kt = i // KT, i % KT
                    absolutes(b, i, first)
                    prev = p == 0
                    post = not (prev and first)
                    tag = "3'" if prev else str(p - 1)
                    ph = nphase(b, p - 1, prev)
                    if kt == 0 and post:
                        take_num(ph)
                    if kt == 2 and post:
                        squares(A("dT" + tag), ph)
                    if kt == 3 and (p < 3 or not last):
                        high(prep_order(f"q{p}", b), *before(f"q{p}", b))
                    if (p < 2 or not last):
                        if kt == (6 if p == 2 else 5):
                            k_take(prep_order(f"k{p}", b), A(f"k{p}"))
                        if kt == 7:
                            if p != 2:
                                high(prep_order(f"k{p}", b), *before(f"k{p}", b))
                            v_take(A(f"v{p}"), 1 - p // 2, p % 2, 4 * b + 3 + p)
                    if p == 3 and kt == 0 and not last:
                        high(prep_order("k2", b), *before("k2", b))
                    if kt == 6 and post:
                        g, c = (1, 1) if prev else ((p - 1) // 2, (p - 1) % 2)
                        gelu(Bn("zT" + tag), ph, g, c)

            body(0, True, False)
            with act.Fori(1, B - 1) as b:
                body(b, False, False)
            body(B - 1, False, True)
            take_num(4 * B - 1)
            squares(a_order("dT3'", B - 1, False, "after"), 4 * B - 1)
            gelu(b_order("zT3'", B - 1, False, "after"), 4 * B - 1, 1, 1)

        @block.gpsimd
        def _(pool):
            nc.gpsimd.memset(ones[:], 1.0).then_inc(made, 1)
            nc.gpsimd.memset(mhalf[:], -0.5).then_inc(made, 1)
            pool.wait_ge(made, 2)

            def split(n, before, count):
                pool.wait_ge(rot_ready, 2 * n + 2)
                nc.gpsimd.tensor_tensor(t1[:], t1[:], t2[:], ALU.add).then_inc(sum_ready, 1)

            def low(n, before, count):
                if before is not None:
                    pool.wait_ge(before, count)
                pool.wait_ge(hi_ready, n + 1)
                nc.gpsimd.tensor_tensor(lo[:], t1[:], hi[:].bitcast(F32), ALU.subtract).then_inc(lo_ready, 1)

            def before(name, b):
                if name[0] == "q":
                    p = int(name[1])
                    return k_stacked[(p + 1) % 2], STACK * (2 * b + [1, 2, 2, 3][p])
                return q_stacked, STACK * (4 * b + int(name[1]) + 2)

            def group_rstd(b):
                pool.wait_ge(geps_ready, b + 1)
                nc.gpsimd.tensor_tensor(grstd[:], dmean[:], mhalf[:, 0:2], ALU.pow).then_inc(grstd_ready, 1)

            def scale_heads(phase):
                pool.wait_ge(u_ready, phase + 1)
                nc.gpsimd.tensor_tensor(rstd[:], var[:], mhalf[:], ALU.pow).then_inc(rstd_ready, 1)
                pool.wait_ge(rstd_ready, phase + 1)
                nc.gpsimd.tensor_tensor(fac[:], rstd[:], rden[:], ALU.mult).then_inc(fac_ready, 1)
                pool.wait_ge(fac_ready, phase + 1)
                tv = tA[:].rearrange("p t (h d) -> p (t h) d", d=32)
                nc.gpsimd.tensor_tensor(tv, tv, fac[:].unsqueeze(2).to_broadcast([128, 16, 32]),
                                        ALU.mult).then_inc(on_ready, 1)

            group_rstd(0)
            split(0, None, 0)
            low(0, None, 0)
            split(1, None, 0)
            low(1, k_stacked[0], STACK)
            split(2, None, 0)
            low(2, k_stacked[1], STACK)

            def body(b, first, last):
                for p in range(PHASES):
                    ph = nphase(b, p - 1, p == 0)
                    if p == 3 and not last:
                        low(prep_order("k2", b), *before("k2", b))
                    if p < 3 or not last:
                        split(prep_order(f"q{p}", b), None, 0)
                        low(prep_order(f"q{p}", b), *before(f"q{p}", b))
                    if not (first and p == 0):
                        scale_heads(ph)
                    if p == 2 and not last:
                        group_rstd(b + 1)
                    if p < 2 or not last:
                        split(prep_order(f"k{p}", b), None, 0)
                        if p != 2:
                            low(prep_order(f"k{p}", b), *before(f"k{p}", b))

            body(0, True, False)
            with pool.Fori(1, B - 1) as b:
                body(b, False, False)
            body(B - 1, False, True)
            scale_heads(4 * B - 1)


def layer1_attention(nc, x1, wqT, wkT, wv, ident, causal, t2, xn2T, featD):
    B, L, E = x1.shape
    NT = L // 128
    LN_EPS = 1e-5
    SCALE = float(E) ** -0.5

    T_TASKS = [f"T{k}{h}" for k in range(2) for h in range(2)]
    Q_TASKS = [f"Q{k}{h}" for k in range(2) for h in range(2)]
    V_TASKS = [f"V{n}" for n in range(4)]
    X_TASKS = [f"X{k}{h}" for k in range(2) for h in range(2)]
    P_TASKS = [f"P{t}{h}" for t in range(NT) for h in range(t // 4 + 1)]
    M_MID = T_TASKS + Q_TASKS + V_TASKS + X_TASKS + P_TASKS
    M_FIRST = [t for t in M_MID if t[0] != "X"]

    def number(name, b, first):
        if name == "end":
            return 2 + len(M_FIRST) + len(M_MID) * (B - 1)
        if first:
            return 2 + M_FIRST.index(name)
        return 2 + len(M_FIRST) + len(M_MID) * (b - 1) + M_MID.index(name)

    def place(name, first):
        return (M_FIRST if first else M_MID).index(name) % 2

    def earlier(name, b, first):
        if name == "end":
            return 1 + len(M_FIRST) // 2 + len(M_MID) // 2 * (B - 1)
        if first:
            return 1 + M_FIRST.index(name) // 2
        return 1 + len(M_FIRST) // 2 + len(M_MID) // 2 * (b - 1) + M_MID.index(name) // 2

    with ExitStack() as ctx:
        def sb(name, shape, dt=F32):
            return ctx.enter_context(nc.sbuf_tensor("l1_" + name, shape, dt))

        def sem(name):
            return ctx.enter_context(nc.semaphore("l1_" + name))

        idn, mask = sb("ident", [128, 128]), sb("causal", [128, 128])
        wq_in, wk_in, wv_in = (sb(n, [128, 2, E]) for n in ("wq_in", "wk_in", "wv_in"))
        ahi, alo, vhw, vlw = (sb(n, [128, 2, E], F32R) for n in ("ahi", "alo", "wvhi", "wvlo"))
        xa, xr = sb("xa", [128, NT, E]), sb("xr", [128, NT, E])
        xn, xn2 = sb("xn", [128, NT, E]), sb("xn2", [128, NT, E])
        feat = sb("feat", [128, NT, E])
        t2s = sb("t2s", [128, NT, E])
        xt2 = sb("xt2", [128, 2, L])
        xhi, xlo, qhi, qlo = (sb(n, [128, 2, L], F32R) for n in ("xhi", "xlo", "qhi", "qlo"))
        vhi, vlo = (sb(n, [128, NT, E], F32R) for n in ("vhi", "vlo"))
        prob = [sb(f"prob{n}", [128, L]) for n in range(2)]
        phi = [sb(f"phi{n}", [128, NT, 128], F32R) for n in range(2)]
        plo = [sb(f"plo{n}", [128, NT, 128], F32R) for n in range(2)]
        st1, st2 = sb("st1", [128, NT, 6]), sb("st2", [128, NT, 6])
        mv1, mv2 = sb("mv1", [128, NT, 2]), sb("mv2", [128, NT, 2])
        eps1, eps2, rstd1, rstd2, mhalf = (sb(n, [128, NT]) for n in ("eps1", "eps2", "rstd1", "rstd2", "mhalf"))
        nmax, rsum, rinv = sb("nmax", [128, NT]), sb("rsum", [128, NT]), sb("rinv", [128, NT])

        def bank(name, shape):
            return ctx.enter_context(nc.psum_tensor("l1_" + name, shape, F32))

        sc = [bank(f"scores{n}", [128, L]) for n in range(2)]
        av = [bank(f"av{n}", [128, 512]) for n in range(2)]
        ring = [bank(f"ring{n}", [128, 512]) for n in range(2)]

        consts, xa_in, xr_in, made = sem("consts"), sem("xa_in"), sem("xr_in"), sem("made")
        waited = sem("waited")
        ring_ready, hi_ready = sem("ring_ready"), sem("hi_ready")
        ring_read = [sem(f"ring_read{n}") for n in range(2)]
        wv_hi, wv_split = sem("wv_hi"), sem("wv_split")
        stats1, agg1, eps1_ready, rstd1_ready, xn_ready = (sem(n) for n in ("stats1", "agg1", "eps1_ready", "rstd1_ready",
                                                                            "xn_ready"))
        stats2, agg2, eps2_ready, rstd2_ready, xn2_ready = (sem(n) for n in ("stats2", "agg2", "eps2_ready", "rstd2_ready",
                                                                             "xn2_ready"))
        feat_added, feat_zero, feat_out = sem("feat_added"), sem("feat_zero"), sem("feat_out")
        scores_ready, masked, max_ready, prob_ready = (sem(n) for n in ("scores_ready", "masked", "max_ready", "prob_ready"))
        av_ready, rinv_ready, out_ready = sem("av_ready"), sem("rinv_ready"), sem("out_ready")
        xt2_ready, xt2_out, t2_out = sem("xt2_ready"), sem("xt2_out"), sem("t2_out")
        NCONST = 5

        block = ctx.enter_context(nc.Block())

        @block.sync
        def _(sp):
            tiles = lambda a: a.rearrange("(t p) e -> p t e", p=128)
            sp.dma_start(xa[:], tiles(x1[0])).then_inc(xa_in, 16)
            for dst, src in ((wq_in[:], wqT.rearrange("(k p) n -> p k n", p=128)),
                             (wk_in[:], wkT.rearrange("(k p) n -> p k n", p=128)),
                             (wv_in[:], wv.rearrange("(k p) n -> p k n", p=128)),
                             (idn[:], ident), (mask[:], causal)):
                sp.dma_start(dst, src).then_inc(consts, 16)

            def body(b, first, last):
                if not first:
                    sp.wait_ge(out_ready, NT * b)
                    sp.dma_start(tiles(t2[b - 1]), t2s[:]).then_inc(t2_out, 16)
                sp.dma_start(xr[:], tiles(x1[b])).then_inc(xr_in, 16)
                if not last:
                    sp.wait_ge(xn_ready, b + 1)
                    sp.dma_start(xa[:], tiles(x1[b + 1])).then_inc(xa_in, 16)
                if not first:
                    sp.wait_ge(xt2_ready, 4 * b)
                    sp.dma_start(xn2T[b - 1].rearrange("(k p) t -> p k t", p=128), xt2[:]).then_inc(xt2_out, 16)

            body(0, True, False)
            with sp.Fori(1, B - 1) as b:
                body(b, False, False)
            body(B - 1, False, True)
            sp.wait_ge(out_ready, NT * B)
            sp.dma_start(tiles(t2[B - 1]), t2s[:]).then_inc(t2_out, 16)
            sp.wait_ge(xt2_ready, 4 * B)
            sp.dma_start(xn2T[B - 1].rearrange("(k p) t -> p k t", p=128), xt2[:]).then_inc(xt2_out, 16)
            sp.wait_ge(feat_added, B)
            sp.dma_start(featD, feat[:]).then_inc(feat_out, 16)
            sp.wait_ge(feat_out, 16)
            sp.wait_ge(t2_out, 16 * B)
            sp.wait_ge(xt2_out, 16 * B)

        @block.tensor
        def _(pe):
            def three(out, a, b, start, stop):
                nc.tensor.matmul(out, a[0], b[0], start=start, stop=False)
                nc.tensor.matmul(out, a[0], b[1], start=False, stop=False)
                return nc.tensor.matmul(out, a[1], b[0], start=False, stop=stop)

            def whole(names, b, first):
                for name in names[-2:]:
                    pe.wait_ge(ring_read[place(name, first)], earlier(name, b, first) + 1)

            def begin(name, b, first):
                n = place(name, first)
                pe.wait_ge(ring_read[n], earlier(name, b, first))
                return ring[n]

            pe.wait_ge(consts, 16 * NCONST)
            for i in range(2):
                for k in range(2):
                    mm = nc.tensor.matmul(ring[i][:, 0:E], wq_in[:, k, 128 * i:128 * i + 128], wk_in[:, k, :],
                                          start=(k == 0), stop=(k == 1))
                mm.then_inc(ring_ready, 1)

            def xn2_transposes(b, count, banks):
                pe.wait_ge(xn2_ready, count)
                for n, (bk, before) in enumerate(banks):
                    pe.wait_ge(ring_read[bk], before)
                    for t in range(4):
                        mm = nc.tensor.transpose(ring[bk][:, 128 * t:128 * t + 128],
                                                 xn2[:, 4 * (n % 2) + t, 128 * (n // 2):128 * (n // 2) + 128], idn[:])
                    mm.then_inc(ring_ready, 1)

            def body(b, first, last):
                pe.wait_ge(xn_ready, b + 1)
                for k in range(2):
                    for h in range(2):
                        bk = begin(f"T{k}{h}", b, first)
                        for t in range(4):
                            mm = nc.tensor.transpose(bk[:, 128 * t:128 * t + 128], xn[:, 4 * h + t, 128 * k:128 * k + 128],
                                                     idn[:])
                        mm.then_inc(ring_ready, 1)
                whole(T_TASKS, b, first)
                if first:
                    pe.wait_ge(wv_split, 2)
                for j in range(2):
                    for h in range(2):
                        bk = begin(f"Q{j}{h}", b, first)
                        tok = slice(512 * h, 512 * h + 512)
                        for k in range(2):
                            mm = three(bk[:], (ahi[:, k, 128 * j:128 * j + 128], alo[:, k, 128 * j:128 * j + 128]),
                                       (xhi[:, k, tok], xlo[:, k, tok]), k == 0, k == 1)
                        mm.then_inc(ring_ready, 1)
                for n in range(4):
                    bk = begin(f"V{n}", b, first)
                    for t in range(2):
                        tok = slice(256 * n + 128 * t, 256 * n + 128 * t + 128)
                        for k in range(2):
                            mm = three(bk[:, E * t:E * t + E], (xhi[:, k, tok], xlo[:, k, tok]),
                                       (vhw[:, k, :], vlw[:, k, :]), k == 0, k == 1)
                    mm.then_inc(ring_ready, 1)
                if not first:
                    xn2_transposes(b, b, [(place(n, first), earlier(n, b, first)) for n in X_TASKS])
                whole(V_TASKS, b, first)
                for t in range(NT + 2):
                    if t < NT:
                        if t >= 2:
                            pe.wait_ge(prob_ready, NT * b + t - 1)
                        for c0 in range(0, 128 * (t + 1), 512):
                            c1 = min(c0 + 512, 128 * (t + 1))
                            for k in range(2):
                                tok = slice(128 * t, 128 * t + 128)
                                mm = three(sc[t % 2][:, c0:c1], (qhi[:, k, tok], qlo[:, k, tok]),
                                           (xhi[:, k, c0:c1], xlo[:, k, c0:c1]), k == 0, k == 1)
                        mm.then_inc(scores_ready, 1)
                    if 1 <= t <= NT:
                        q = t - 1
                        pe.wait_ge(prob_ready, NT * b + q + 1)
                        for h in range(q // 4 + 1):
                            bk = begin(f"P{q}{h}", b, first)
                            for kb in range(4 * h, min(4 * h + 4, q + 1)):
                                mm = nc.tensor.transpose(bk[:, 128 * (kb % 4):128 * (kb % 4) + 128],
                                                         prob[q % 2][:, 128 * kb:128 * kb + 128], idn[:])
                            mm.then_inc(ring_ready, 1)
                    if t >= 2:
                        q = t - 2
                        whole([f"P{q}{h}" for h in range(q // 4 + 1)], b, first)
                        if q >= 2 or not first:
                            pe.wait_ge(out_ready, NT * b + q - 1)
                        for kb in range(q + 1):
                            mm = three(av[q % 2][:, 0:E], (phi[q % 2][:, kb, :], plo[q % 2][:, kb, :]),
                                       (vhi[:, kb, :], vlo[:, kb, :]), kb == 0, kb == q)
                        mm.then_inc(av_ready, 1)

            body(0, True, False)
            with pe.Fori(1, B - 1) as b:
                body(b, False, False)
            body(B - 1, False, True)
            e = earlier("end", 0, False)
            xn2_transposes(B, B, [(n % 2, e + n // 2) for n in range(4)])

        def parts(name):
            if name[0] in "TQ":
                k, h = int(name[1]), int(name[2])
                hi, lo = (xhi, xlo) if name[0] == "T" else (qhi, qlo)
                return hi[:, k, 512 * h:512 * h + 512], lo[:, k, 512 * h:512 * h + 512], 512
            if name[0] == "V":
                n = int(name[1])
                flat = lambda a: a[:, 2 * n:2 * n + 2, :].rearrange("p t e -> p (t e)")
                return flat(vhi), flat(vlo), 512
            q, h = int(name[1]), int(name[2])
            kb = min(4 * h + 4, q + 1)
            flat = lambda a: a[:, 4 * h:kb, :].rearrange("p t e -> p (t e)")
            return flat(phi[q % 2]), flat(plo[q % 2]), 128 * (kb - 4 * h)

        SPLITS_FIRST = [t for t in M_FIRST if t[0] != "X"]

        def split_number(name, b):
            return len(SPLITS_FIRST) * b + SPLITS_FIRST.index(name)

        @block.scalar
        def _(act):
            act.wait_ge(consts, 16 * NCONST)
            for i in range(2):
                act.wait_ge(ring_ready, i + 1)
                nc.scalar.activation(ahi[:, i, :], ring[i][:, 0:E], ACT.Copy, scale=SCALE).then_inc(hi_ready, 1)
            nc.scalar.activation(vhw[:], wv_in[:], ACT.Copy).then_inc(wv_hi, 1)

            def high(name, b, first):
                hi, lo, w = parts(name)
                if name[0] == "P" and int(name[1]) >= 2:
                    act.wait_ge(av_ready, NT * b + int(name[1]) - 1)
                act.wait_ge(ring_ready, number(name, b, first) + 1)
                nc.scalar.activation(hi, ring[place(name, first)][:, 0:w], ACT.Copy).then_inc(hi_ready, 1)

            def take_x(n, bk, num, b, count):
                k, h = n // 2, n % 2
                if n == 0 and count is not None:
                    act.wait_ge(xt2_out, count)
                act.wait_ge(ring_ready, num + 1)
                nc.scalar.activation(xt2[:, k, 512 * h:512 * h + 512], ring[bk][:], ACT.Copy).then_inc(xt2_ready, 1)
                act.wait_ge(xt2_ready, 4 * (b - 1) + n + 1)
                act.sem_inc(ring_read[bk], 1)

            def body(b, first, last):
                for name in T_TASKS + Q_TASKS + V_TASKS:
                    high(name, b, first)
                if not first:
                    for n in range(4):
                        take_x(n, place(X_TASKS[n], first), number(X_TASKS[n], b, first), b, 16 * (b - 1) if n == 0 else None)
                for t in range(NT + 1):
                    if t < NT:
                        act.wait_ge(max_ready, NT * b + t + 1)
                        nc.scalar.activation(prob[t % 2][:, 0:128 * (t + 1)], sc[t % 2][:, 0:128 * (t + 1)], ACT.Exp,
                                             bias=nmax[:, t:t + 1], accum_out=rsum[:, t:t + 1]).then_inc(prob_ready, 1)
                    if t >= 1:
                        for h in range((t - 1) // 4 + 1):
                            high(f"P{t - 1}{h}", b, first)

            body(0, True, False)
            with act.Fori(1, B - 1) as b:
                body(b, False, False)
            body(B - 1, False, True)
            for n in range(4):
                take_x(n, n % 2, number("end", 0, False) + n, B, 16 * (B - 1) if n == 0 else None)

        @block.vector
        def _(dve):
            dve.wait_ge(consts, 16 * NCONST)
            dve.wait_ge(made, 1)

            def ln1_stats(b, t):
                if t == 0:
                    dve.wait_ge(xa_in, 16 * (b + 1))
                nc.vector.bn_stats(st1[:, t, :], xa[:, t, :]).then_inc(stats1, 1)

            def ln1_eps(b):
                dve.wait_ge(stats1, NT * (b + 1))
                dve.sem_inc(waited, 1)
                for t in range(NT):
                    nc.vector.bn_aggr(mv1[:, t, :], st1[:, t, :]).then_inc(agg1, 1)
                dve.wait_ge(agg1, NT * (b + 1))
                nc.vector.tensor_scalar(eps1[:], mv1[:, :, 1], LN_EPS, None, ALU.add).then_inc(eps1_ready, 1)

            def ln1_apply(b):
                dve.wait_ge(rstd1_ready, b + 1)
                for t in range(NT):
                    ins = nc.vector.tensor_scalar(xn[:, t, :], xa[:, t, :], mv1[:, t, 0:1], rstd1[:, t:t + 1],
                                                  ALU.subtract, ALU.mult)
                ins.then_inc(xn_ready, 1)

            def ln2_eps(b):
                dve.wait_ge(stats2, NT * b)
                dve.sem_inc(waited, 1)
                for t in range(NT):
                    nc.vector.bn_aggr(mv2[:, t, :], st2[:, t, :]).then_inc(agg2, 1)
                dve.wait_ge(agg2, NT * b)
                nc.vector.tensor_scalar(eps2[:], mv2[:, :, 1], LN_EPS, None, ALU.add).then_inc(eps2_ready, 1)

            def ln2_apply(b, first_use):
                dve.wait_ge(rstd2_ready, b)
                if not first_use:
                    dve.wait_ge(feat_added, b - 1)
                for t in range(NT):
                    ins = nc.vector.tensor_scalar(xn2[:, t, :], t2s[:, t, :], mv2[:, t, 0:1], rstd2[:, t:t + 1],
                                                  ALU.subtract, ALU.mult)
                ins.then_inc(xn2_ready, 1)

            def low(name, b, first):
                hi, lo, w = parts(name)
                bk = place(name, first)
                dve.wait_ge(hi_ready, 2 + split_number(name, b) + 1)
                nc.vector.tensor_tensor(lo, ring[bk][:, 0:w], hi.bitcast(F32), ALU.subtract).then_inc(ring_read[bk], 1)

            for t in range(NT):
                ln1_stats(0, t)
            ln1_eps(0)
            ln1_apply(0)
            for i in range(2):
                dve.wait_ge(hi_ready, i + 1)
                nc.vector.scalar_tensor_tensor(out=alo[:, i, :], in0=ring[i][:, 0:E], scalar=SCALE,
                                               in1=ahi[:, i, :].bitcast(F32), op0=ALU.mult,
                                               op1=ALU.subtract).then_inc(ring_read[i], 1)
            dve.wait_ge(wv_hi, 1)
            nc.vector.tensor_tensor(vlw[:], wv_in[:], vhw[:].bitcast(F32), ALU.subtract).then_inc(wv_split, 2)

            def body(b, first, last):
                if not first:
                    ln2_eps(b)
                for name in T_TASKS:
                    low(name, b, first)
                if not first:
                    ln2_apply(b, False if not isinstance(b, int) else b == 1)
                for name in Q_TASKS + V_TASKS:
                    low(name, b, first)
                for t in range(NT + 2):
                    if t < NT:
                        w = 128 * (t + 1)
                        dve.wait_ge(scores_ready, NT * b + t + 1)
                        nc.vector.tensor_tensor(sc[t % 2][:, w - 128:w], sc[t % 2][:, w - 128:w], mask[:],
                                                ALU.add).then_inc(masked, 1)
                        dve.wait_ge(masked, NT * b + t + 1)
                        nc.vector.tensor_reduce(nmax[:, t:t + 1], sc[t % 2][:, 0:w], AX.X, ALU.max,
                                                negate=True).then_inc(max_ready, 1)
                    if 1 <= t <= NT:
                        for h in range((t - 1) // 4 + 1):
                            if t >= 3 and h == 0:
                                dve.wait_ge(av_ready, NT * b + t - 2)
                            low(f"P{t - 1}{h}", b, first)
                    if t >= 2:
                        q = t - 2
                        if q == 0:
                            dve.wait_ge(xr_in, 16 * (b + 1))
                            if not first:
                                dve.wait_ge(t2_out, 16 * b)
                        nc.vector.reciprocal(rinv[:, q:q + 1], rsum[:, q:q + 1]).then_inc(rinv_ready, 1)
                        dve.wait_ge(rinv_ready, NT * b + q + 1)
                        dve.wait_ge(av_ready, NT * b + q + 1)
                        nc.vector.scalar_tensor_tensor(out=t2s[:, q, :], in0=av[q % 2][:, 0:E], scalar=rinv[:, q:q + 1],
                                                       in1=xr[:, q, :], op0=ALU.mult, op1=ALU.add).then_inc(out_ready, 1)
                        if not last and q < 4:
                            ln1_stats(b + 1, 2 * q)
                            ln1_stats(b + 1, 2 * q + 1)
                        if not last and q == 4:
                            ln1_eps(b + 1)
                        if not last and q == 6:
                            ln1_apply(b + 1)
                        dve.wait_ge(out_ready, NT * b + q + 1)
                        nc.vector.bn_stats(st2[:, q, :], t2s[:, q, :]).then_inc(stats2, 1)

            body(0, True, False)
            with dve.Fori(1, B - 1) as b:
                body(b, False, False)
            body(B - 1, False, True)
            ln2_eps(B)
            ln2_apply(B, False)

        @block.gpsimd
        def _(pool):
            nc.gpsimd.memset(mhalf[:], -0.5).then_inc(made, 1)
            nc.gpsimd.memset(feat[:], 0.0).then_inc(feat_zero, 1)
            pool.wait_ge(made, 1)

            def rstd(ready, eps, out, done, count):
                pool.wait_ge(ready, count)
                nc.gpsimd.tensor_tensor(out[:], eps[:], mhalf[:], ALU.pow).then_inc(done, 1)

            rstd(eps1_ready, eps1, rstd1, rstd1_ready, 1)

            def add_feat(b):
                pool.wait_ge(xn2_ready, b)
                pool.wait_ge(feat_zero, 1)
                if not isinstance(b, int) or b > 1:
                    pool.wait_ge(feat_added, b - 1)
                nc.gpsimd.tensor_tensor(feat[:], feat[:], xn2[:], ALU.add).then_inc(feat_added, 1)

            def body(b, first, last):
                if not first:
                    rstd(eps2_ready, eps2, rstd2, rstd2_ready, b)
                    add_feat(b)
                if not last:
                    rstd(eps1_ready, eps1, rstd1, rstd1_ready, b + 2)

            body(0, True, False)
            with pool.Fori(1, B - 1) as b:
                body(b, False, False)
            body(B - 1, False, True)
            rstd(eps2_ready, eps2, rstd2, rstd2_ready, B)
            add_feat(B)


def layer1_experts(nc, t2, xn2T, featD, wr, br, w1, bn1, w2, bn2, wo, bo, ident, selE, out):
    B, L, D = t2.shape
    NE = w1.shape[0]
    NT = L // 128
    CH = 512
    U = 2 * NE
    BN_EPS = 1e-3
    NS = 2

    with ExitStack() as ctx:
        def sb(name, shape, dt=F32):
            return ctx.enter_context(nc.sbuf_tensor("e_" + name, shape, dt))

        def sem(name):
            return ctx.enter_context(nc.semaphore("e_" + name))

        whi, wlo = sb("whi", [128, NE, 3, 2, D], F32R), sb("wlo", [128, NE, 3, 2, D], F32R)
        stage = [sb(f"stage{n}", [128, 2, D]) for n in range(NS)]
        wbc = sb("wbc", [128, NE, L])
        feat = wbc[:, 0:2, :].rearrange("p a b -> p (a b)").rearrange("p (t e) -> p t e", e=D)
        featT = wbc[:, 2:4, :]
        xraw = sb("xraw", [128, 2, CH])
        xhi = [sb(f"xhi{c}", [128, 2, CH], F32R) for c in range(2)]
        xlo = [sb(f"xlo{c}", [128, 2, CH], F32R) for c in range(2)]
        r1 = [sb(f"r1{m}", [128, CH]) for m in range(2)]
        r2 = [sb(f"r2{m}", [128, CH]) for m in range(2)]
        h1hi, h1lo, h2hi, h2lo = ([sb(f"{n}{c}", [128, 2, CH], F32R) for c in range(2)]
                                  for n in ("h1hi", "h1lo", "h2hi", "h2lo"))
        res = [sb(f"res{c}", [128, 4, D]) for c in range(2)]
        idn = sb("ident", [128, 128])
        sel = res[1][0:NE, :, :].rearrange("p t e -> p (t e)").rearrange("p (n m) -> p n m", m=128)
        wr_sb, br_sb, bo_sb, ones = sb("wr", [128, 2, NE]), sb("br", [1, NE]), sb("bo", [NE, D]), sb("ones", [1, 128])
        bn = [[sb(f"bn{n}{q}", [128, 2, NE]) for q in range(5)] for n in range(2)]
        mhalf, rs = sb("mhalf", [128, 2, NE]), [sb(f"rs{n}", [128, 2, NE]) for n in range(2)]
        nm, sm, rsm = sb("nm", [128, NT]), sb("sm", [128, NT]), sb("rsm", [128, NT])
        lg, wt = sb("lg", [128, NT, NE]), sb("wt", [128, NT, NE])
        wT = sb("wT", [NE, L])

        def bank(name, shape):
            return ctx.enter_context(nc.psum_tensor("e_" + name, shape, F32))

        p1 = [bank(f"h1_{m}", [128, CH]) for m in range(2)]
        p2 = [bank(f"h2_{m}", [128, CH]) for m in range(2)]
        py = [bank(f"y_{c}", [128, 4, D]) for c in range(2)]
        four = [p1[0], p1[1], p2[0], p2[1]]

        consts, feat_in, x_in, made = sem("consts"), sem("feat_in"), sem("x_in"), sem("made")
        waited = sem("waited")
        stage_in = [sem(f"stage_in{n}") for n in range(NS)]
        wsplit_hi, wsplit = sem("wsplit_hi"), sem("wsplit")
        x_split_hi, x_split = sem("x_split_hi"), sem("x_split")
        bn_step, bn_eps, bn_rs, bn_ready = sem("bn_step"), sem("bn_eps"), sem("bn_rs"), sem("bn_ready")
        setup_pe, featT_ready, soft = sem("setup_pe"), sem("featT_ready"), sem("soft")
        exp_ready, wT_ready, wbc_ready = sem("exp_ready"), sem("wT_ready"), sem("wbc_ready")
        h1_ready, r1_ready, hi1_ready, lo1_ready = sem("h1_ready"), sem("r1_ready"), sem("hi1_ready"), sem("lo1_ready")
        h2_ready, r2_ready, w2_ready = sem("h2_ready"), sem("r2_ready"), sem("w2_ready")
        hi2_ready, lo2_ready, y_ready, y_read = sem("hi2_ready"), sem("lo2_ready"), sem("y_ready"), sem("y_read")
        res_in = [sem(f"res_in{c}") for c in range(2)]
        res_out = [sem(f"res_out{c}") for c in range(2)]
        NCONST = 16

        block = ctx.enter_context(nc.Block())

        @block.sync
        def _(sp):
            sp.dma_start(feat, featD).then_inc(feat_in, 16)
            cols = lambda a: a.rearrange("(k p) n -> p k n", p=128)
            for n, w in ((0, w1), (1, w2)):
                sp.dma_start(stage[n][:], cols(w[0])).then_inc(stage_in[n], 16)
            sp.dma_start(xraw[:], cols(xn2T[0])[:, :, 0:CH]).then_inc(x_in, 16)
            for dst, src in [(idn[:], ident), (sel, selE), (wr_sb[:], cols(wr)), (br_sb[:], br), (bo_sb[:], bo)]:
                sp.dma_start(dst, src).then_inc(consts, 16)
            for n, arrays in enumerate((bn1, bn2)):
                for q in range(5):
                    sp.dma_start(bn[n][q][:], cols(arrays[q])).then_inc(consts, 16)
            sp.wait_ge(consts, 16 * 15)
            for i in range(NS, 3 * NE):
                sp.wait_ge(wsplit, i - NS + 1)
                sp.dma_start(stage[i % NS][:], cols((w1, w2, wo)[i % 3][i // 3])).then_inc(stage_in[i % NS], 16)
                if i == 6:
                    sp.wait_ge(x_split, 1)
                    sp.dma_start(xraw[:], cols(xn2T[0])[:, :, CH:L]).then_inc(x_in, 16)

            def rows(a, b, c):
                return a[b, CH * c:CH * c + CH, :].rearrange("(t p) e -> p t e", p=128)

            def body(b, first, last):
                for c in range(2):
                    if not (first and c == 0):
                        nb, ncx = (b, 1) if c == 0 else (b + 1, 0)
                        if not (last and c == 1):
                            sp.wait_ge(x_split, 2 * b + c + 1)
                            sp.dma_start(xraw[:], cols(xn2T[nb])[:, :, CH * ncx:CH * ncx + CH]).then_inc(x_in, 16)
                    if not first:
                        sp.wait_ge(res_out[c], 16 * b)
                        sp.sem_inc(waited, 1)
                    if first and c == 1:
                        sp.wait_ge(wbc_ready, 2 * NE)
                    sp.dma_start(res[c][:], rows(t2, b, c)).then_inc(res_in[c], 16)
                    if not (first and c == 0):
                        pb = b if c == 1 else b - 1
                        sp.wait_ge(y_read, 2 * b + c)
                        sp.dma_start(rows(out, pb, 1 - c), res[1 - c][:]).then_inc(res_out[1 - c], 16)

            body(0, True, False)
            with sp.Fori(1, B - 1) as b:
                body(b, False, False)
            body(B - 1, False, True)
            sp.wait_ge(y_read, 2 * B)
            sp.dma_start(rows(out, B - 1, 1), res[1][:]).then_inc(res_out[1], 16)
            for c in range(2):
                sp.wait_ge(res_out[c], 16 * B)

        @block.tensor
        def _(pe):
            def three(o, a, b, start, stop):
                nc.tensor.matmul(o, a[0], b[0], start=start, stop=False, skip_group_check=True)
                nc.tensor.matmul(o, a[0], b[1], start=False, stop=False, skip_group_check=True)
                return nc.tensor.matmul(o, a[1], b[0], start=False, stop=stop, skip_group_check=True)

            pe.wait_ge(consts, 16 * 15)
            pe.wait_ge(feat_in, 16)
            pe.wait_ge(made, 2)
            for k in range(2):
                for h in range(2):
                    for t in range(4):
                        mm = nc.tensor.transpose(four[2 * k + h][:, 128 * t:128 * t + 128],
                                                 feat[:, 4 * h + t, 128 * k:128 * k + 128], idn[:])
                    mm.then_inc(setup_pe, 1)
            pe.wait_ge(featT_ready, 4)
            for t in range(NT):
                o = py[0][:, 0, NE * t:NE * t + NE]
                for k in range(2):
                    nc.tensor.matmul(o, featT[:, k, 128 * t:128 * t + 128], wr_sb[:, k, :], start=(k == 0), stop=False)
                mm = nc.tensor.matmul(o, ones[:], br_sb[:], start=False, stop=True)
            mm.then_inc(setup_pe, 1)
            pe.wait_ge(soft, 5)
            for t in range(NT):
                mm = nc.tensor.transpose(py[1][0:NE, t // 2, 128 * (t % 2):128 * (t % 2) + 128], wt[:, t, :], idn[:])
            mm.then_inc(setup_pe, 1)
            pe.wait_ge(wT_ready, 1)
            for n in range(2 * NE):
                if n >= 4:
                    pe.wait_ge(wbc_ready, n - 3)
                nc.tensor.matmul(four[n % 4][:], sel[:, n // 2, :], wT[:, CH * (n % 2):CH * (n % 2) + CH],
                                 start=True, stop=True).then_inc(setup_pe, 1)
            pe.wait_ge(wbc_ready, 2 * NE)

            def hidden1(b, u, first):
                c, e = u // NE, u % NE
                if e == 0:
                    pe.wait_ge(x_split, 2 * b + c + 1)
                if first:
                    if c == 0:
                        pe.wait_ge(wsplit, 3 * e + 3)
                for m in range(2):
                    if u > 0 or not first:
                        pe.wait_ge(r1_ready, 2 * (U * b + u) + m - 1)
                    for k in range(2):
                        cut = slice(128 * m, 128 * m + 128)
                        mm = three(p1[m][:], (whi[:, e, 0, k, cut], wlo[:, e, 0, k, cut]),
                                   (xhi[c][:, k, :], xlo[c][:, k, :]), k == 0, k == 1)
                    mm.then_inc(h1_ready, 1)

            def hidden2(b, u, first):
                e = u % NE
                pe.wait_ge(lo1_ready, 2 * (U * b + u) + 2)
                for m in range(2):
                    if u > 0 or not first:
                        pe.wait_ge(r2_ready, 2 * (U * b + u) + m - 1)
                    for k in range(2):
                        cut = slice(128 * m, 128 * m + 128)
                        mm = three(p2[m][:], (whi[:, e, 1, k, cut], wlo[:, e, 1, k, cut]),
                                   (h1hi[u % 2][:, k, :], h1lo[u % 2][:, k, :]), k == 0, k == 1)
                    mm.then_inc(h2_ready, 1)

            def output(b, u, first):
                c, e = u // NE, u % NE
                if e == 0:
                    if not first:
                        pe.wait_ge(y_read, 2 * b + c - 1)
                    for t in range(4):
                        nc.tensor.matmul(py[c][:, t, :], wT[:, CH * c + 128 * t:CH * c + 128 * t + 128], bo_sb[:],
                                         start=(t % 2 == 0), stop=False, skip_group_check=True)
                pe.wait_ge(lo2_ready, 2 * (U * b + u) + 2)
                for t in range(4):
                    cut = slice(128 * t, 128 * t + 128)
                    for k in range(2):
                        mm = three(py[c][:, t, :], (h2hi[u % 2][:, k, cut], h2lo[u % 2][:, k, cut]),
                                   (whi[:, e, 2, k, :], wlo[:, e, 2, k, :]), False, e == NE - 1 and k == 1)
                mm.then_inc(y_ready, 1)

            hidden1(0, 0, True)

            def body(b, first, last):
                for s in range(U):
                    if s + 1 < U:
                        hidden1(b, s + 1, first)
                    elif not last:
                        hidden1(b + 1, 0, False)
                    hidden2(b, s, first)
                    if s > 0:
                        output(b, s - 1, first)
                    elif not first:
                        output(b - 1, U - 1, False)

            body(0, True, False)
            with pe.Fori(1, B - 1) as b:
                body(b, False, False)
            body(B - 1, False, True)
            output(B - 1, U - 1, False)

        def flat(a):
            return a.rearrange("p k n -> p (k n)")

        @block.scalar
        def _(act):
            def weights_high(e):
                for j in range(3):
                    i = 3 * e + j
                    act.wait_ge(stage_in[i % NS], 16 * (i // NS + 1))
                    nc.scalar.activation(flat(whi[:, e, j]), flat(stage[i % NS][:]), ACT.Copy).then_inc(wsplit_hi, 1)

            for n in range(4):
                act.wait_ge(setup_pe, n + 1)
                nc.scalar.activation(featT[:, n // 2, 512 * (n % 2):512 * (n % 2) + 512], four[n][:], ACT.Copy,
                                     scale=1.0 / B).then_inc(featT_ready, 1)
            act.wait_ge(soft, 2)
            nc.scalar.activation(flat(wt[:]), flat(lg[:]), ACT.Exp).then_inc(exp_ready, 1)
            weights_high(0)
            weights_high(1)
            for n in range(0, 2 * NE, 2):
                act.wait_ge(setup_pe, 7 + n)
                nc.scalar.activation(wbc[:, n // 2, 0:CH], four[n % 4][:], ACT.Copy).then_inc(exp_ready, 1)
                act.wait_ge(exp_ready, n // 2 + 2)
                if n:
                    act.wait_ge(wbc_ready, n)
                act.sem_inc(wbc_ready, 1)
            act.wait_ge(bn_ready, 2)

            def relu(b, u, layer, first):
                e = u % NE
                ready, done, lo_done, p, r = ((h1_ready, r1_ready, lo1_ready, p1, r1),
                                              (h2_ready, r2_ready, lo2_ready, p2, r2))[layer]
                for m in range(2):
                    n = 2 * (U * b + u) + m
                    act.wait_ge(ready, n + 1)
                    if u > 0 or not first:
                        act.wait_ge(lo_done, n - 1)
                    nc.scalar.activation(r[m][:], p[m][:], ACT.Relu, bias=bn[layer][1][:, m, e:e + 1],
                                         scale=rs[layer][:, m, e:e + 1]).then_inc(done, 1)

            def high2(b, u, first):
                for m in range(2):
                    n = 2 * (U * b + u) + m
                    if m == 0 and (u >= 2 or not first):
                        act.wait_ge(y_ready, U * b + u - 1)
                    act.wait_ge(w2_ready, n + 1)
                    nc.scalar.activation(h2hi[u % 2][:, m, :], r2[m][:], ACT.Copy).then_inc(hi2_ready, 1)

            relu(0, 0, 0, True)

            def body(b, first, last):
                for s in range(U):
                    if s > 0:
                        high2(b, s - 1, first)
                    elif not first:
                        high2(b - 1, U - 1, False)
                    if s + 1 < U:
                        relu(b, s + 1, 0, first)
                    elif not last:
                        relu(b + 1, 0, 0, False)
                    relu(b, s, 1, first)
                    if first and s + 2 < NE:
                        weights_high(s + 2)

            body(0, True, False)
            with act.Fori(1, B - 1) as b:
                body(b, False, False)
            body(B - 1, False, True)
            high2(B - 1, U - 1, False)

        @block.vector
        def _(dve):
            def weights_low(e):
                for j in range(3):
                    i = 3 * e + j
                    dve.wait_ge(wsplit_hi, i + 1)
                    nc.vector.tensor_tensor(flat(wlo[:, e, j]), flat(stage[i % NS][:]), flat(whi[:, e, j]).bitcast(F32),
                                            ALU.subtract).then_inc(wsplit, 1)

            def split_x(b, c, first):
                dve.wait_ge(x_in, 16 * (2 * b + c + 1))
                if not first:
                    dve.wait_ge(h1_ready, 2 * (U * b + NE * c - NE))
                nc.vector.tensor_copy(flat(xhi[c][:]), flat(xraw[:])).then_inc(x_split_hi, 1)
                dve.wait_ge(x_split_hi, 2 * b + c + 1)
                nc.vector.tensor_tensor(flat(xlo[c][:]), flat(xraw[:]), flat(xhi[c][:]).bitcast(F32),
                                        ALU.subtract).then_inc(x_split, 1)

            dve.wait_ge(consts, 16 * 15)
            for n in range(2):
                g, bb, be, m, v = (flat(a[:]) for a in bn[n])
                nc.vector.tensor_scalar(v, v, BN_EPS, None, ALU.add).then_inc(bn_eps, 1)
                nc.vector.tensor_tensor(bb, bb, m, ALU.subtract).then_inc(bn_step, 1)
            split_x(0, 0, True)
            for n in range(2):
                g, bb, be, m, v = (flat(a[:]) for a in bn[n])
                dve.wait_ge(bn_rs, n + 1)
                nc.vector.tensor_tensor(flat(rs[n][:]), flat(rs[n][:]), g, ALU.mult).then_inc(bn_step, 1)
                dve.wait_ge(bn_step, 3 + 2 * n)
                nc.vector.tensor_tensor(bb, bb, flat(rs[n][:]), ALU.mult).then_inc(bn_step, 1)
                dve.wait_ge(bn_step, 4 + 2 * n)
                nc.vector.tensor_tensor(bb, bb, be, ALU.add).then_inc(bn_ready, 1)
            dve.wait_ge(setup_pe, 5)
            logits = py[0][:, 0, 0:NT * NE].rearrange("p (t e) -> p t e", e=NE)
            nc.vector.tensor_reduce(nm[:], logits, AX.X, ALU.max, negate=True).then_inc(soft, 1)
            dve.wait_ge(soft, 1)
            nc.vector.tensor_tensor(lg[:], logits, nm[:].unsqueeze(2).to_broadcast([128, NT, NE]), ALU.add).then_inc(soft, 1)
            dve.wait_ge(exp_ready, 1)
            nc.vector.tensor_reduce(sm[:], wt[:], AX.X, ALU.add).then_inc(soft, 1)
            dve.wait_ge(soft, 3)
            nc.vector.reciprocal(rsm[:], sm[:]).then_inc(soft, 1)
            dve.wait_ge(soft, 4)
            nc.vector.tensor_tensor(wt[:], wt[:], rsm[:].unsqueeze(2).to_broadcast([128, NT, NE]), ALU.mult).then_inc(soft, 1)
            dve.wait_ge(setup_pe, 6)
            nc.vector.tensor_copy(wT[:], py[1][0:NE, :, :].rearrange("p a b -> p (a b)")).then_inc(wT_ready, 1)
            weights_low(0)
            weights_low(1)
            for n in range(1, 2 * NE, 2):
                dve.wait_ge(setup_pe, 7 + n)
                dve.wait_ge(wbc_ready, n)
                nc.vector.tensor_copy(wbc[:, n // 2, CH:L], four[n % 4][:]).then_inc(wbc_ready, 1)

            def split1(b, u, first):
                for m in range(2):
                    n = 2 * (U * b + u) + m
                    dve.wait_ge(r1_ready, n + 1)
                    if m == 0 and (u >= 2 or not first):
                        dve.wait_ge(h2_ready, 2 * (U * b + u) - 2)
                    nc.vector.tensor_copy(h1hi[u % 2][:, m, :], r1[m][:]).then_inc(hi1_ready, 1)
                    dve.wait_ge(hi1_ready, n + 1)
                    nc.vector.tensor_tensor(h1lo[u % 2][:, m, :], r1[m][:], h1hi[u % 2][:, m, :].bitcast(F32),
                                            ALU.subtract).then_inc(lo1_ready, 1)

            def weigh(b, u):
                c, e = u // NE, u % NE
                for m in range(2):
                    dve.wait_ge(r2_ready, 2 * (U * b + u) + m + 1)
                    nc.vector.tensor_tensor(r2[m][:], r2[m][:], wbc[:, e, CH * c:CH * c + CH], ALU.mult).then_inc(w2_ready, 1)

            def low2(b, u):
                for m in range(2):
                    dve.wait_ge(hi2_ready, 2 * (U * b + u) + m + 1)
                    nc.vector.tensor_tensor(h2lo[u % 2][:, m, :], r2[m][:], h2hi[u % 2][:, m, :].bitcast(F32),
                                            ALU.subtract).then_inc(lo2_ready, 1)

            def finish(b, c):
                dve.wait_ge(y_ready, U * b + NE * c + NE)
                dve.wait_ge(res_in[c], 16 * (b + 1))
                nc.vector.tensor_tensor(flat(res[c][:]), flat(py[c][:]), flat(res[c][:]), ALU.add).then_inc(y_read, 1)

            split1(0, 0, True)

            def body(b, first, last):
                for s in range(U):
                    if s > 0:
                        low2(b, s - 1)
                    elif not first:
                        low2(b - 1, U - 1)
                    if s + 1 < U:
                        split1(b, s + 1, first)
                    elif not last:
                        split1(b + 1, 0, False)
                    weigh(b, s)
                    if first and s + 2 < NE:
                        weights_low(s + 2)
                    if s == 1 and not first:
                        finish(b - 1, 1)
                    if s == NE + 1:
                        finish(b, 0)
                    if s == 4:
                        split_x(b, 1, first)
                    if s == NE + 4 and not last:
                        split_x(b + 1, 0, False)

            body(0, True, False)
            with dve.Fori(1, B - 1) as b:
                body(b, False, False)
            body(B - 1, False, True)
            low2(B - 1, U - 1)
            finish(B - 1, 1)

        @block.gpsimd
        def _(pool):
            nc.gpsimd.memset(ones[:], 1.0).then_inc(made, 1)
            nc.gpsimd.memset(mhalf[:], -0.5).then_inc(made, 1)
            pool.wait_ge(made, 2)
            for n in range(2):
                pool.wait_ge(bn_eps, n + 1)
                nc.gpsimd.tensor_tensor(flat(rs[n][:]), flat(bn[n][4][:]), flat(mhalf[:]), ALU.pow).then_inc(bn_rs, 1)


def program(nc, I, out):
    B, L, E = I["x"].shape
    x1 = nc.dram_tensor("x1_scratch", (B, L, E), F32, kind="Internal").ap()
    t2 = nc.dram_tensor("t2_scratch", (B, L, E), F32, kind="Internal").ap()
    xn2T = nc.dram_tensor("xn2T_scratch", (B, E, L), F32, kind="Internal").ap()
    feat = nc.dram_tensor("feat_scratch", (128, L // 128, E), F32, kind="Internal").ap()
    layer0(nc, I["x"], I["xT"], I["wqT0"], I["wkT0"], I["wvT0"], I["woT0"], I["ln_g"], I["ln_b"], I["window"],
           I["rowscale"], I["cosT"], I["sinT"], I["avg8"], I["ident"], I["headpick"], x1)
    layer1_attention(nc, x1, I["wqT1"], I["wkT1"], I["wv1"], I["ident"], I["causal"], t2, xn2T, feat)
    layer1_experts(nc, t2, xn2T, feat, I["wr"], I["br"], I["w1"], [I[n + "1"] for n in ("g", "b", "be", "m", "v")],
                   I["w2"], [I[n + "2"] for n in ("g", "b", "be", "m", "v")], I["wo"], I["bo"], I["ident"],
                   I["selectors"], out)


def shape_constants(H=8, R=32):
    gamma = 1.0 - 2.0 ** (-2.0 - 5.0 * np.arange(H) / H)
    i = np.arange(R)
    factor = 1 / np.sqrt((gamma[:, None, None] ** np.abs(i[:, None] - i[None, :])).sum(-1))
    r, j2, u = np.arange(128) // R, np.arange(128) % R, np.arange(4 - R, R)
    dist = np.abs(u[None, None, :, None] - r[:, None, None, None]) + np.abs(i[None, None, None, :] - j2[:, None, None, None])
    window = gamma[None, :, None, None] ** dist * factor[None, :, None, :]
    rowscale = np.stack([factor[4 * g + np.arange(128) // 32] for g in range(2)], 1)
    angle = np.repeat(1.0 / 10000.0 ** np.linspace(0.0, 1.0, 16), 2)
    turn = (i[:, None] + i[None, :]).reshape(-1)[None, :] * angle[:, None]
    sine = np.sin(turn)
    sine[0::2] *= -1
    pick = np.zeros((128, 4))
    pick[32 * np.arange(4), np.arange(4)] = 1
    selectors = np.zeros((8, 8, 128))
    selectors[np.arange(8), np.arange(8)] = 1
    tri = np.arange(128)
    out = {
        "window": window.reshape(128, H, -1), "rowscale": rowscale, "cosT": np.tile(np.cos(turn), (4, 1)),
        "sinT": np.tile(sine, (4, 1)), "avg8": np.kron(np.eye(16), np.full((8, 8), 1 / 8)), "ident": np.eye(128),
        "headpick": pick, "selectors": selectors, "causal": np.where(tri[None, :] > tri[:, None], -3e38, 0.0),
    }
    return {k: np.ascontiguousarray(v, dtype=np.float32) for k, v in out.items()}


def kernel(**inputs):
    import concourse.bacc as bacc
    from concourse.bass_utils import run_bass_kernel_spmd

    a = {k: np.asarray(v) for k, v in inputs.items()}
    B, N1, N2, E = a["x"].shape
    x = a["x"].reshape(B, N1 * N2, E)
    arrays = {"x": x, "xT": x.transpose(0, 2, 1)}
    for n, k in (("wqT0", "Wq"), ("wkT0", "Wk"), ("wvT0", "Wv"), ("woT0", "Wo")):
        arrays[n] = a["L0_conv_" + k].T
    for n in ("g", "b"):
        arrays["ln_" + n] = np.tile(a["L0_conv_ln_" + n], 4)[:, None]
    arrays |= {"wqT1": a["L1_attn_Wq"].T, "wkT1": a["L1_attn_Wk"].T, "wv1": a["L1_attn_Wv"]}
    for n in ("Wr", "W1", "W2", "Wo", "bo"):
        arrays[n.lower()] = a["L1_ffn_" + n]
    arrays["br"] = a["L1_ffn_br"][None]
    for n in ("g", "b", "be", "m", "v"):
        for layer in "12":
            arrays[n + layer] = a["L1_ffn_" + n + layer].T
    arrays |= shape_constants()
    arrays = {"in_" + k: np.ascontiguousarray(v) for k, v in arrays.items()}

    nc = bacc.Bacc("TRN2", target_bir_lowering=False, num_devices=1)
    I = {k[3:]: nc.dram_tensor(k, v.shape, mybir.dt.from_np(v.dtype), kind="ExternalInput").ap() for k, v in arrays.items()}
    out = nc.dram_tensor("out", (B, N1 * N2, E), F32, kind="ExternalOutput").ap()
    program(nc, I, out)
    r = run_bass_kernel_spmd(nc, [arrays], core_ids=[0])
    return r.results[0]["out"].reshape(B, N1, N2, E)
```

```python
from contextlib import ExitStack

import numpy as np

import concourse.bass as bass
from concourse import mybir

ALU = mybir.AluOpType
ACT = mybir.ActivationFunctionType
AX = mybir.AxisListType
F32 = mybir.dt.float32
F32R = mybir.dt.float32r


def layer0(nc, x, xT, wqT, wkT, wvT, woT, lng, lnb, window, rowscale, cosT, sinT, avg8, ident, x1):
    B, L, E = x.shape
    H, HD = 8, E // 8
    QC = 512
    KT = L // 128
    STEPS, PHASES = 4 * KT, 4
    ROWS = L // 32
    CROWS = QC // 32
    LN_EPS, GN_EPS = 1e-5, 1e-5
    SCALING = float(HD) ** -0.5
    STACK = 16 * 16

    A_HEAD = ["gn1", "gn2", "k", "v", "q", "v'", "k'"]
    A_MID = ["q0", "dT3'", "k0", "v0", "q1", "dT0", "k1", "v1", "q2", "dT1", "gn1", "gn2", "k2", "v2",
             "q3", "dT2", "k3", "v3"]
    A_FIRST = [t for t in A_MID if t != "dT3'"]
    A_LAST = [t for t in A_MID if t not in ("gn1", "gn2", "k2", "v2", "q3", "k3", "v3")] + ["dT3'"]
    B_MID = ["nT3'", "zT3'", "o2'", "o3'", "nT0", "zT0", "nT1", "zT1", "nT2", "zT2", "o0", "o1"]
    B_FIRST = B_MID[4:]
    B_LAST = B_MID + B_MID[:4]

    def order(name, b, first, last, lists, head):
        one, mid, end = lists
        if first:
            return head + one.index(name)
        if last:
            n = len(end) - 1 - end[::-1].index(name) if last == "after" else end.index(name)
            return head + len(one) + len(mid) * (B - 2) + n
        return head + len(one) + len(mid) * (b - 1) + mid.index(name)

    def a_order(name, b, first, last):
        return order(name, b, first, last, (A_FIRST, A_MID, A_LAST), len(A_HEAD))

    def b_order(name, b, first, last):
        return order(name, b, first, last, (B_FIRST, B_MID, B_LAST), 0)

    def prep_order(name, b):
        return 3 + 8 * b + ["q0", "k0", "q1", "k1", "q2", "k2", "q3", "k3"].index(name)

    with ExitStack() as ctx:
        def sb(name, shape, dt=F32):
            return ctx.enter_context(nc.sbuf_tensor("l0_" + name, shape, dt))

        def sem(name):
            return ctx.enter_context(nc.semaphore("l0_" + name))

        win = sb("window", [128, H, (2 * ROWS - 4) * 32])
        rsc = sb("rowscale", [128, 2, ROWS])
        cos_sb, sin_sb = sb("cos", [128, L]), sb("sin", [128, L])
        wq, wk, wv, wo = (sb(n, [128, 2, E]) for n in ("wq", "wk", "wv", "wo"))
        avg, idn = sb("avg8", [128, 128]), sb("ident", [128, 128])
        ones = sb("ones", [128, HD])
        lngb = sb("lngb", [128, 2])
        raw, xn = sb("raw", [128, 2, L]), sb("xn", [128, 2, L])
        t1, t2 = sb("t1", [128, QC]), sb("t2", [128, QC])
        hi, lo = sb("hi", [128, QC], F32R), sb("lo", [128, QC], F32R)
        kst = [sb(f"kst{g}", [128, 4, L], F32R) for g in range(2)]
        qst = [sb(f"qst{c}", [128, 4, QC], F32R) for c in range(2)]
        vsb = [sb(f"v{g}", [128, KT, 128]) for g in range(2)]
        prod = [sb(f"prod{n}", [128, 2, QC]) for n in range(4)]
        absp = [sb(f"absp{n}", [128, 2, QC]) for n in range(4)]
        tA, tB = sb("tA", [128, 4, 128]), sb("tB", [128, 4, 128])
        z = sb("z", [128, 2, L])
        xo = [sb(f"xo{n}", [128, 2, E]) for n in range(2)]
        stats, mv = sb("stats", [128, 2, 2, 6]), sb("mv", [128, 2, 2])
        gmean, dmean, gvar, grstd = (sb(n, [128, 2]) for n in ("gmean", "dmean", "gvar", "grstd"))
        mhalf = sb("mhalf", [128, 16])
        nsum, dent, var, fac, epst = (sb(n, [128, 16]) for n in ("nsum", "den_t", "var", "fac", "eps"))

        def bank(name, shape):
            return ctx.enter_context(nc.psum_tensor("l0_" + name, shape, F32))

        sc = [bank(f"scores{j}", [128, 2, QC]) for j in range(2)]
        num, den = bank("num", [128, QC]), bank("den", [128, QC])
        pA, pB = bank("bankA", [128, QC]), bank("bankB", [128, QC])

        def sems(names):
            return (sem(n) for n in names.split())

        weights_in, tables_in, consts, made, x_in, waited, window_in = sems("weights_in tables_in consts made x_in waited window_in")
        stats_done, agg_done, gmean_ready, gvar_ready = sems("stats_done agg_done gmean_ready gvar_ready")
        geps_ready, grstd_ready, xn_ready = sems("geps_ready grstd_ready xn_ready")
        scores_ready, prod_ready, abs_ready, av_done, den_done = sems("scores_ready prod_ready abs_ready av_done den_done")
        a_ready, b_ready = sems("a_ready b_ready")
        t1_ready, shuffled, rot_ready, sum_ready = sems("t1_ready shuffled rot_ready sum_ready")
        cos_ready = sem("cos_ready")
        hi_ready, lo_ready, q_stacked, v_ready = sems("hi_ready lo_ready q_stacked v_ready")
        n_taken, d_taken, nsum_ready, centred = sems("n_taken d_taken nsum_ready centred")
        sq_ready, den_ready, var_ready, fac_step = sems("sq_ready den_ready var_ready fac_step")
        on_ready, z_ready, o_added = sems("on_ready z_ready o_added")
        k_stacked = [sem(f"k_stacked{c}") for c in range(2)]
        xo_in = [sem(f"xo_in{n}") for n in range(2)]
        xo_out = [sem(f"xo_out{n}") for n in range(2)]

        NWEIGHTS, NTABLES, NCONST = 4, 3, 5
        NMADE = 3

        def nphase(b, p, prev):
            return 4 * b - 1 if prev else 4 * b + p

        block = ctx.enter_context(nc.Block())

        @block.sync
        def _(sp):
            sp.dma_start(raw[:], xT[0].rearrange("(k p) t -> p k t", p=128)).then_inc(x_in, 16)
            for dst, src in ((avg[:], avg8), (wk[:], wkT.rearrange("(k p) n -> p k n", p=128)),
                             (wv[:], wvT.rearrange("(k p) n -> p k n", p=128)),
                             (wq[:], wqT.rearrange("(k p) n -> p k n", p=128))):
                sp.dma_start(dst, src).then_inc(weights_in, 16)
            for dst, src in ((sin_sb[:], sinT), (cos_sb[:], cosT), (rsc[:], rowscale)):
                sp.dma_start(dst, src).then_inc(tables_in, 16)
            for dst, src in ((win[:, 0:H // 2], window[:, 0:H // 2]), (idn[:], ident),
                             (lngb[:, 0:1], lng), (lngb[:, 1:2], lnb),
                             (wo[:], woT.rearrange("(k p) n -> p k n", p=128))):
                sp.dma_start(dst, src).then_inc(consts, 16)

            def stack(n, dst, quads, done):
                sp.wait_ge(hi_ready, n + 1)
                for part, tile, ready in (("hi", hi, None), ("lo", lo, lo_ready)):
                    if ready is not None:
                        sp.wait_ge(ready, n + 1)
                    for quad in range(4):
                        if quads[quad] == part:
                            for h in range(4):
                                sp.dma_start(dst[32 * quad:32 * quad + 32, h, :].bitcast(F32),
                                             tile[32 * h:32 * h + 32, :].bitcast(F32)).then_inc(done, 16)

            QUADS = {"q": ("hi", "hi", "lo", "lo"), "k": ("hi", "lo", "hi", "lo")}
            stack(0, kst[0][:, :, 0:QC], QUADS["k"], k_stacked[0])
            stack(1, qst[0][:, :, :], QUADS["q"], q_stacked)
            sp.dma_start(win[:, H // 2:H], window[:, H // 2:H]).then_inc(window_in, 16)
            stack(2, kst[0][:, :, QC:L], QUADS["k"], k_stacked[1])

            def load_x(n, bb, t0, count):
                if count is not None:
                    sp.wait_ge(xo_out[n], count)
                sp.dma_start(xo[n][:], x[bb, t0:t0 + 256, :].rearrange("(t p) e -> p t e", p=128)).then_inc(xo_in[n], 16)

            def store_x(n, bb, t0, added):
                sp.wait_ge(o_added, added)
                sp.dma_start(x1[bb, t0:t0 + 256, :].rearrange("(t p) e -> p t e", p=128), xo[n][:]).then_inc(xo_out[n], 16)

            def body(b, first, last):
                if not last:
                    sp.wait_ge(xn_ready, 2 * b + 2)
                    sp.dma_start(raw[:], xT[b + 1].rearrange("(k p) t -> p k t", p=128)).then_inc(x_in, 16)
                if not first:
                    for n in range(2):
                        load_x(n, b - 1, QC + 256 * n, 16 * (2 * b - 1))
                stack(prep_order("q0", b), qst[1][:, :, :], QUADS["q"], q_stacked)
                stack(prep_order("k0", b), kst[1][:, :, 0:QC], QUADS["k"], k_stacked[0])
                if not first:
                    store_x(0, b - 1, QC, 4 * b - 1)
                    store_x(1, b - 1, QC + 256, 4 * b)
                stack(prep_order("q1", b), qst[0][:, :, :], QUADS["q"], q_stacked)
                stack(prep_order("k1", b), kst[1][:, :, QC:L], QUADS["k"], k_stacked[1])
                stack(prep_order("q2", b), qst[1][:, :, :], QUADS["q"], q_stacked)
                if not last:
                    stack(prep_order("k2", b), kst[0][:, :, 0:QC], QUADS["k"], k_stacked[0])
                for n in range(2):
                    load_x(n, b, 256 * n, None if first else 32 * b)
                if not last:
                    stack(prep_order("q3", b), qst[0][:, :, :], QUADS["q"], q_stacked)
                    stack(prep_order("k3", b), kst[0][:, :, QC:L], QUADS["k"], k_stacked[1])
                store_x(0, b, 0, 4 * b + 1)
                store_x(1, b, 256, 4 * b + 2)

            body(0, True, False)
            with sp.Fori(1, B - 1) as b:
                body(b, False, False)
            body(B - 1, False, True)
            for n in range(2):
                load_x(n, B - 1, QC + 256 * n, 16 * (2 * B - 1))
            for n in range(2):
                store_x(n, B - 1, QC + 256 * n, 4 * B - 1 + n)
            for n in range(2):
                sp.wait_ge(xo_out[n], 32 * B)

        @block.tensor
        def _(pe):
            pe.wait_ge(weights_in, 16 * NWEIGHTS)
            pe.wait_ge(made, NMADE)

            def a_free(name, b, first, last):
                tasks = A_FIRST if first else (A_LAST if last else A_MID)
                k = len(tasks) - 1 if last == "after" else tasks.index(name)
                before = tasks[k - 1] if k > 0 else "v3'"
                if first and k == 0:
                    pe.wait_ge(t1_ready, 3)
                elif before[0] in "qk":
                    pe.wait_ge(t1_ready, prep_order(before, b) + 1)
                elif before == "v3'":
                    pe.wait_ge(v_ready, 4 * b + 2)
                elif before[0] == "v":
                    pe.wait_ge(v_ready, 4 * b + 3 + int(before[1]))
                elif before == "gn1":
                    pe.wait_ge(gmean_ready, 3 * b + 4)
                elif before == "gn2":
                    pe.wait_ge(geps_ready, b + 2)
                else:
                    pe.wait_ge(den_ready, 4 * b if before == "dT3'" else 4 * b + int(before[2]) + 1)

            def b_free(name, b, first, last):
                tasks = B_FIRST if first else (B_LAST if last else B_MID)
                k = len(tasks) - 1 - tasks[::-1].index(name) if last == "after" else tasks.index(name)
                if first and k == 0:
                    return
                before = tasks[k - 1] if k > 0 else "o1'"
                if k > len(B_MID):
                    b = b + 1
                if before[0] == "o":
                    pe.wait_ge(o_added, {"o1'": 4 * b - 2, "o2'": 4 * b - 1, "o3'": 4 * b, "o0": 4 * b + 1,
                                         "o1": 4 * b + 2}[before])
                else:
                    taken = centred if before[0] == "n" else z_ready
                    pe.wait_ge(taken, 4 * b if before[2:] == "3'" else 4 * b + int(before[2]) + 1)

            def project(w, g, c, part=None):
                for k in range(2) if part is None else (part,):
                    mm = nc.tensor.matmul(pA[:], w[:, k, 128 * g:128 * g + 128], xn[:, k, QC * c:QC * c + QC],
                                          start=(k == 0), stop=(k == 1))
                if part != 0:
                    mm.then_inc(a_ready, 1)

            def project_v(g, half, part=None):
                for t in range(4) if part is None else range(2 * part, 2 * part + 2):
                    tok = QC * half + 128 * t
                    for k in range(2):
                        mm = nc.tensor.matmul(pA[:, 128 * t:128 * t + 128], xn[:, k, tok:tok + 128],
                                              wv[:, k, 128 * g:128 * g + 128], start=(k == 0), stop=(k == 1))
                if part != 0:
                    mm.then_inc(a_ready, 1)

            def group_sums(rhs, sem_, count):
                pe.wait_ge(sem_, count)
                nc.tensor.matmul(pA[:, 0:2], avg[:], rhs, start=True, stop=True).then_inc(a_ready, 1)

            def transpose_n(phase):
                pe.wait_ge(n_taken, phase + 1)
                for t in range(4):
                    mm = nc.tensor.transpose(pB[:, 128 * t:128 * t + 128], tA[:, t, :], idn[:])
                mm.then_inc(b_ready, 1)

            def transpose_d(phase):
                pe.wait_ge(d_taken, phase + 1)
                for t in range(4):
                    mm = nc.tensor.transpose(pA[:, 128 * t:128 * t + 128], tB[:, t, :], idn[:])
                mm.then_inc(a_ready, 1)

            def transpose_z(phase):
                pe.wait_ge(on_ready, phase + 1)
                for t in range(4):
                    mm = nc.tensor.transpose(pB[:, 128 * t:128 * t + 128], tA[:, t, :], idn[:])
                mm.then_inc(b_ready, 1)

            def out_proj(c, half, phases):
                pe.wait_ge(z_ready, phases)
                for t in range(2):
                    tok = QC * c + 256 * half + 128 * t
                    for g in range(2):
                        mm = nc.tensor.matmul(pB[:, 256 * t:256 * t + 256], z[:, g, tok:tok + 128], wo[:, g, :],
                                              start=(g == 0), stop=(g == 1))
                mm.then_inc(b_ready, 1)

            def scores(b, i, j):
                p, kt = i // KT, i % KT
                g, c = p // 2, p % 2
                if kt == 0 and j == 0:
                    pe.wait_ge(q_stacked, STACK * (4 * b + p + 1))
                if c == 0 and kt % 4 == 0 and j == 0:
                    pe.wait_ge(k_stacked[kt // 4], STACK * (2 * b + g + 1))
                n = 2 * i + j
                if n >= 2 or not isinstance(b, int) or b > 0:
                    pe.wait_ge(prod_ready, 2 * STEPS * b + n - 1)
                for s in range(2):
                    h = 2 * j + s
                    mm = nc.tensor.matmul(sc[j][:, s, :], kst[g][:, h, 128 * kt:128 * kt + 128], qst[c][:, h, :],
                                          start=True, stop=True)
                mm.then_inc(scores_ready, 1)

            def weighted(b, i, first):
                p, kt = i // KT, i % KT
                g = p // 2
                if p % 2 == 0 and kt % 4 == 0:
                    pe.wait_ge(v_ready, 4 * b + 2 * g + kt // 4 + 1)
                if kt == 0 and not (first and p == 0):
                    pe.wait_ge(n_taken, 4 * b + p)
                pe.wait_ge(prod_ready, 2 * STEPS * b + 2 * i + 2)
                for h in range(4):
                    mm = nc.tensor.matmul(num[32 * h:32 * h + 32, :], vsb[g][:, kt, 32 * h:32 * h + 32],
                                          prod[2 * (i % 2) + h // 2][:, h % 2, :], start=(kt == 0), stop=(kt == KT - 1))
                mm.then_inc(av_done, 1)

            def sums(b, i, first):
                p, kt = i // KT, i % KT
                if kt == 0 and not (first and p == 0):
                    pe.wait_ge(d_taken, 4 * b + p)
                pe.wait_ge(abs_ready, 2 * STEPS * b + 2 * i + 2)
                for h in range(4):
                    mm = nc.tensor.matmul(den[32 * h:32 * h + 32, :], ones[:],
                                          absp[2 * (i % 2) + h // 2][:, h % 2, :], start=(kt == 0), stop=(kt == KT - 1))
                mm.then_inc(den_done, 1)

            group_sums(mv[:, :, 0], agg_done, 1)
            group_sums(gvar[:], gvar_ready, 1)
            pe.wait_ge(xn_ready, 2)
            project(wk, 0, 0)
            pe.wait_ge(t1_ready, 1)
            project_v(0, 0)
            pe.wait_ge(v_ready, 1)
            project(wq, 0, 0)
            pe.wait_ge(t1_ready, 2)
            project_v(0, 1)
            pe.wait_ge(v_ready, 2)
            project(wk, 0, 1)
            scores(0, 0, 0)
            scores(0, 0, 1)
            pe.wait_ge(consts, 16 * NCONST)

            def body(b, first, last):
                def A(name, task, *args):
                    if task not in (project, project_v) or args[-1] != 1:
                        a_free(name, b, first, last)
                    task(*args)

                def Bk(name, task, *args):
                    b_free(name, b, first, last)
                    task(*args)

                for i in range(STEPS):
                    p, kt = i // KT, i % KT
                    prev = p == 0
                    post = not (prev and first)
                    tag = "3'" if prev else str(p - 1)
                    ph = nphase(b, p - 1, prev)
                    g, c = ((p + 1) // 2 % 2, (p + 1) % 2)
                    prep_q, prep_kv = p < 3 or not last, p < 2 or not last
                    nb, ni = (b, i + 1) if i + 1 < STEPS else (b + 1, 0)
                    more = i + 1 < STEPS or not last
                    if more:
                        scores(nb, ni, 0)
                    if i > 0:
                        sums(b, i - 1, first)
                    elif not first:
                        sums(b - 1, STEPS - 1, False)
                    if kt == 0 and prep_q:
                        A(f"q{p}", project, wq, g, c, 0)
                    if p != 2 and kt == 4 and prep_kv:
                        A(f"k{p}", project, wk, (1 - p // 2), p % 2, 0)
                    if p == 2 and kt == 6 and prep_kv:
                        pe.wait_ge(xn_ready, 2 * b + 4)
                        A(f"k{p}", project, wk, (1 - p // 2), p % 2, 1)
                    if kt == 6 and post:
                        Bk("zT" + tag, transpose_z, ph)
                    if kt == 7 and p == 3:
                        Bk("o0", out_proj, 0, 0, 4 * b + 3)
                    if kt == 7 and prev and not first:
                        Bk("o2'", out_proj, 1, 0, 4 * b)
                    if kt == (7 if p == 2 else 6) and prep_kv:
                        A(f"v{p}", project_v, (1 - p // 2), p % 2, 0)
                    if more:
                        scores(nb, ni, 1)
                    weighted(b, i, first)
                    if kt == 0 and prep_q:
                        A(f"q{p}", project, wq, g, c, 1)
                    if kt == 0 and post:
                        Bk("nT" + tag, transpose_n, ph)
                    if kt == 1 and post:
                        A("dT" + tag, transpose_d, ph)
                    if p == 2 and kt == 2 and not last:
                        A("gn1", group_sums, mv[:, :, 0], agg_done, b + 2)
                    if p == 2 and kt == 3 and not last:
                        A("gn2", group_sums, gvar[:], gvar_ready, b + 2)
                    if p != 2 and kt == 4 and prep_kv:
                        A(f"k{p}", project, wk, (1 - p // 2), p % 2, 1)
                    if p == 2 and kt == 5 and prep_kv:
                        pe.wait_ge(xn_ready, 2 * b + 3)
                        A(f"k{p}", project, wk, (1 - p // 2), p % 2, 0)
                    if kt == (7 if p == 2 else 6) and prep_kv:
                        A(f"v{p}", project_v, (1 - p // 2), p % 2, 1)
                    if kt == 7 and p == 3:
                        Bk("o1", out_proj, 0, 1, 4 * b + 3)
                    if kt == 7 and prev and not first:
                        Bk("o3'", out_proj, 1, 1, 4 * b)

            body(0, True, False)
            with pe.Fori(1, B - 1) as b:
                body(b, False, False)
            body(B - 1, False, True)
            sums(B - 1, STEPS - 1, False)
            b_free("nT3'", B - 1, False, "after")
            transpose_n(4 * B - 1)
            a_free("dT3'", B - 1, False, "after")
            transpose_d(4 * B - 1)
            b_free("zT3'", B - 1, False, "after")
            transpose_z(4 * B - 1)
            b_free("o2'", B - 1, False, "after")
            out_proj(1, 0, 4 * B)
            b_free("o3'", B - 1, False, "after")
            out_proj(1, 1, 4 * B)

        @block.vector
        def _(dve):

            def q_rotate_in(n, a, g, c):
                if not isinstance(n, int) or n > 0:
                    dve.wait_ge(lo_ready, n)
                dve.wait_ge(a_ready, a + 1)
                nc.vector.tensor_tensor(t1[:].rearrange("p (a b) -> p a b", b=32), pA[:].rearrange("p (a b) -> p a b", b=32),
                                        rsc[:, g, CROWS * c:CROWS * c + CROWS].unsqueeze(2).to_broadcast([128, CROWS, 32]),
                                        ALU.mult).then_inc(t1_ready, 1)

            def shuffle(n):
                dve.wait_ge(t1_ready, n + 1)
                dve.sem_inc(waited, 1)
                nc.vector.stream_shuffle(t2[:], t1[:], [i ^ 1 for i in range(32)]).then_inc(shuffled, 1)

            def rotate_sin(n, c):
                dve.wait_ge(shuffled, n + 1)
                nc.vector.tensor_tensor(t2[:], t2[:], sin_sb[:, QC * c:QC * c + QC], ALU.mult).then_inc(rot_ready, 1)

            def products(b, i, j, first):
                p, kt = i // KT, i % KT
                g, c = p // 2, p % 2
                w0 = 32 * (CROWS * c - 4 * kt + ROWS - 4)
                n = 2 * i + j
                dve.wait_ge(scores_ready, 2 * STEPS * b + n + 1)
                if not (first and i < 2):
                    dve.wait_ge(av_done, STEPS * b + i - 1)
                    dve.wait_ge(abs_ready, 2 * STEPS * b + n - 3)
                nc.vector.tensor_tensor(prod[n % 4][:], sc[j][:], win[:, 4 * g + 2 * j:4 * g + 2 * j + 2, w0:w0 + QC],
                                        ALU.mult).then_inc(prod_ready, 1)

            nT = pB[:].rearrange("p (m d) -> p m d", d=32)

            def head_sums(n):
                dve.wait_ge(b_ready, n + 1)
                nc.vector.tensor_reduce(nsum[:], nT, AX.X, ALU.add).then_inc(nsum_ready, 1)

            def centre(phase):
                dve.wait_ge(nsum_ready, phase + 1)
                nc.vector.scalar_tensor_tensor(tA[:].rearrange("p t (h d) -> p (t h) d", d=32),
                                               nsum[:].unsqueeze(2).to_broadcast([128, 16, 32]), -1.0 / HD, nT,
                                               ALU.mult, ALU.add).then_inc(centred, 1)

            nT_A = pA[:].rearrange("p (m d) -> p m d", d=32)

            def take_den(a):
                dve.wait_ge(a_ready, a + 1)
                nc.vector.tensor_scalar(dent[:], nT_A[:, :, 0], 1.0, 50000.0, ALU.max, ALU.min).then_inc(den_ready, 1)

            def variance(phase):
                dve.wait_ge(sq_ready, phase + 1)
                nc.vector.tensor_reduce(var[:], tB[:].rearrange("p t (h d) -> p (t h) d", d=32), AX.X,
                                        ALU.add).then_inc(var_ready, 1)

            def statistics(b, quarters):
                if 0 in quarters:
                    dve.wait_ge(x_in, 16 * (b + 1))
                for n in quarters:
                    k, s = n // 2, n % 2
                    nc.vector.bn_stats(stats[:, k, s, :], raw[:, k, 512 * s:512 * s + 512]).then_inc(stats_done, 1)

            def aggregate(b):
                dve.wait_ge(stats_done, 4 * (b + 1))
                dve.sem_inc(waited, 1)
                for k in range(2):
                    ins = nc.vector.bn_aggr(mv[:, k, :], stats[:, k, :, :].rearrange("p s f -> p (s f)"))
                ins.then_inc(agg_done, 1)

            def group_mean(b, a):
                dve.wait_ge(a_ready, a + 1)
                nc.vector.tensor_copy(gmean[:], pA[:, 0:2]).then_inc(gmean_ready, 1)
                dve.wait_ge(gmean_ready, 3 * b + 1)
                nc.vector.tensor_tensor(dmean[:], mv[:, :, 0], gmean[:], ALU.subtract).then_inc(gmean_ready, 1)
                dve.wait_ge(gmean_ready, 3 * b + 2)
                nc.vector.tensor_tensor(dmean[:], dmean[:], dmean[:], ALU.mult).then_inc(gmean_ready, 1)
                dve.wait_ge(gmean_ready, 3 * b + 3)
                nc.vector.tensor_tensor(gvar[:], mv[:, :, 1], dmean[:], ALU.add).then_inc(gvar_ready, 1)

            def group_var(b, a):
                dve.wait_ge(a_ready, a + 1)
                nc.vector.tensor_scalar(dmean[:], pA[:, 0:2], GN_EPS, None, ALU.add).then_inc(geps_ready, 1)

            def normalise(b, parts):
                if 0 in parts:
                    dve.wait_ge(grstd_ready, b + 1)
                for k in parts:
                    nc.vector.tensor_scalar(xn[:, k, :], raw[:, k, :], gmean[:, k:k + 1], grstd[:, k:k + 1],
                                            ALU.subtract, ALU.mult).then_inc(xn_ready, 1)

            def add_residual(bn, n, k, count):
                dve.wait_ge(b_ready, bn + 1)
                dve.wait_ge(xo_in[n], count)
                nc.vector.tensor_tensor(xo[n][:].rearrange("p t e -> p (t e)"), pB[:], xo[n][:].rearrange("p t e -> p (t e)"),
                                        ALU.add).then_inc(o_added, 1)


            statistics(0, range(4))
            aggregate(0)
            group_mean(0, 0)
            group_var(0, 1)
            normalise(0, (0, 1))
            dve.wait_ge(tables_in, 16 * NTABLES)
            for n in range(3):
                if n == 1:
                    q_rotate_in(1, 4, 0, 0)
                shuffle(n)
                rotate_sin(n, n // 2)
            dve.wait_ge(consts, 16 * NCONST)

            def body(b, first, last):
                A = lambda name: a_order(name, b, first, last)
                Bn = lambda name: b_order(name, b, first, last)
                for i in range(STEPS):
                    p, kt = i // KT, i % KT
                    prev = p == 0
                    post = not (prev and first)
                    tag = "3'" if prev else str(p - 1)
                    ph = nphase(b, p - 1, prev)
                    g, c = ((p + 1) // 2 % 2, (p + 1) % 2)
                    prep_q, prep_k = p < 3 or not last, p < 2 or not last
                    nq, nk = prep_order(f"q{p}", b), prep_order(f"k{p}", b)
                    if first and i == 2 * KT:
                        dve.wait_ge(window_in, 16)
                    products(b, i, 0, first)
                    if kt == 1 and prep_q:
                        q_rotate_in(nq, A(f"q{p}"), g, c)
                    if kt == 2 and prep_q:
                        rotate_sin(nq, (p + 1) % 2)
                    if kt == 3 and post:
                        centre(ph)
                    if kt == (7 if p == 2 else 6) and prep_k:
                        shuffle(nk)
                    if not last:
                        if p == 1 and kt == 5:
                            statistics(b + 1, (1,))
                        if p == 1 and kt == 7:
                            statistics(b + 1, (3,))
                        if p == 2 and kt == 4:
                            group_var(b + 1, A("gn2"))
                        if p == 2 and kt == 5:
                            normalise(b + 1, (0,))
                    products(b, i, 1, first)
                    if kt == 0 and p == 1 and not first:
                        add_residual(Bn("o3'"), 1, 4 * b, 16 * 2 * b)
                    if kt == 0 and p == 0 and not first:
                        add_residual(Bn("nT3'") - 1, 1, 4 * b - 2, 16 * (2 * b - 1))
                    if kt == 1 and prep_q:
                        shuffle(nq)
                    if kt == 4 and post:
                        variance(ph)
                    if kt == 2 and post:
                        take_den(A("dT" + tag))
                        head_sums(Bn("nT" + tag))
                    if kt == (7 if p == 2 else 6) and prep_k:
                        rotate_sin(nk, p % 2)
                    if not last:
                        if p == 1 and kt == 4:
                            statistics(b + 1, (0,))
                        if p == 1 and kt == 5:
                            statistics(b + 1, (2,))
                        if p == 1 and kt == 7:
                            aggregate(b + 1)
                        if p == 2 and kt == 3:
                            group_mean(b + 1, A("gn1"))
                        if p == 2 and kt == 5:
                            normalise(b + 1, (1,))
                    if kt == 7 and p == 3:
                        add_residual(Bn("o0"), 0, 4 * b + 1, 16 * (2 * b + 1))
                    if kt == 7 and prev and not first:
                        add_residual(Bn("o2'"), 0, 4 * b - 1, 32 * b)

            body(0, True, False)
            with dve.Fori(1, B - 1) as b:
                body(b, False, False)
            body(B - 1, False, True)
            Bn = lambda name: b_order(name, B - 1, False, "after")
            add_residual(Bn("nT3'") - 1, 1, 4 * B - 2, 16 * (2 * B - 1))
            head_sums(Bn("nT3'"))
            centre(4 * B - 1)
            take_den(a_order("dT3'", B - 1, False, "after"))
            variance(4 * B - 1)
            add_residual(Bn("o2'"), 0, 4 * B - 1, 32 * B)
            add_residual(Bn("o3'"), 1, 4 * B, 32 * B)

        @block.scalar
        def _(act):

            def k_take(n, a):
                if not isinstance(n, int) or n > 0:
                    act.wait_ge(lo_ready, n)
                act.wait_ge(a_ready, a + 1)
                nc.scalar.activation(t1[:], pA[:], ACT.Copy, scale=SCALING).then_inc(t1_ready, 1)

            def high(n, before, count):
                if before is not None:
                    act.wait_ge(before, count)
                act.wait_ge(sum_ready, n + 1)
                nc.scalar.activation(hi[:], t1[:], ACT.Copy).then_inc(hi_ready, 1)

            def v_take(a, g, half, n):
                act.wait_ge(a_ready, a + 1)
                nc.scalar.activation(vsb[g][:, 4 * half:4 * half + 4, :].rearrange("p t c -> p (t c)"), pA[:],
                                     ACT.Copy).then_inc(v_ready, 1)

            def absolutes(b, i, first):
                for j in range(2):
                    n = 2 * i + j
                    act.wait_ge(prod_ready, 2 * STEPS * b + n + 1)
                    if not (first and i < 2):
                        act.wait_ge(den_done, STEPS * b + i - 1)
                    nc.scalar.activation(absp[n % 4][:], prod[n % 4][:], ACT.Abs).then_inc(abs_ready, 1)

            def take_num(phase):
                act.wait_ge(av_done, KT * (phase + 1))
                nc.scalar.activation(tA[:].rearrange("p t c -> p (t c)"), num[:], ACT.Copy).then_inc(n_taken, 1)

            def take_den(phase):
                act.wait_ge(den_done, KT * (phase + 1))
                nc.scalar.activation(tB[:].rearrange("p t c -> p (t c)"), den[:], ACT.Copy).then_inc(d_taken, 1)

            def squares(a, phase):
                act.wait_ge(a_ready, a + 1)
                act.wait_ge(centred, phase + 1)
                nc.scalar.activation(tB[:], tA[:], ACT.Square, scale=HD ** -0.5).then_inc(sq_ready, 1)

            def gelu(n, phase, g, c):
                act.wait_ge(b_ready, n + 1)
                nc.scalar.activation(z[:, g, QC * c:QC * c + QC], pB[:], ACT.Gelu, bias=lngb[:, 1:2],
                                     scale=lngb[:, 0:1]).then_inc(z_ready, 1)

            def before(name, b):
                if name[0] == "q":
                    p = int(name[1])
                    return k_stacked[(p + 1) % 2], STACK * (2 * b + [1, 2, 2, 3][p])
                return q_stacked, STACK * (4 * b + int(name[1]) + 2)

            k_take(0, 2)
            v_take(3, 0, 0, 1)
            high(0, None, 0)
            v_take(5, 0, 1, 2)
            high(1, k_stacked[0], STACK)
            k_take(2, 6)
            high(2, q_stacked, STACK)
            act.wait_ge(consts, 16 * NCONST)

            def body(b, first, last):
                A = lambda name: a_order(name, b, first, last)
                Bn = lambda name: b_order(name, b, first, last)
                for i in range(STEPS):
                    p, kt = i // KT, i % KT
                    prev = p == 0
                    post = not (prev and first)
                    tag = "3'" if prev else str(p - 1)
                    ph = nphase(b, p - 1, prev)
                    if kt == 0 and post:
                        take_num(ph)
                    absolutes(b, i, first)
                    if kt == 0 and post:
                        take_den(ph)
                    if kt == 3 and post:
                        squares(A("dT" + tag), ph)
                    if kt == 3 and (p < 3 or not last):
                        high(prep_order(f"q{p}", b), *before(f"q{p}", b))
                    if (p < 2 or not last):
                        if kt == (6 if p == 2 else 5):
                            k_take(prep_order(f"k{p}", b), A(f"k{p}"))
                        if kt == 7:
                            if p != 2:
                                high(prep_order(f"k{p}", b), *before(f"k{p}", b))
                            v_take(A(f"v{p}"), 1 - p // 2, p % 2, 4 * b + 3 + p)
                    if p == 3 and kt == 0 and not last:
                        high(prep_order("k2", b), *before("k2", b))
                    if kt == 6 and post:
                        g, c = (1, 1) if prev else ((p - 1) // 2, (p - 1) % 2)
                        gelu(Bn("zT" + tag), ph, g, c)

            body(0, True, False)
            with act.Fori(1, B - 1) as b:
                body(b, False, False)
            body(B - 1, False, True)
            take_num(4 * B - 1)
            take_den(4 * B - 1)
            squares(a_order("dT3'", B - 1, False, "after"), 4 * B - 1)
            gelu(b_order("zT3'", B - 1, False, "after"), 4 * B - 1, 1, 1)

        @block.gpsimd
        def _(pool):
            nc.gpsimd.memset(ones[:], 1.0).then_inc(made, 1)
            nc.gpsimd.memset(mhalf[:], -0.5).then_inc(made, 1)
            nc.gpsimd.memset(epst[:], LN_EPS).then_inc(made, 1)
            pool.wait_ge(made, NMADE)

            def rotate_cos(n, c):
                pool.wait_ge(shuffled, n + 1)
                nc.gpsimd.tensor_tensor(t1[:], t1[:], cos_sb[:, QC * c:QC * c + QC], ALU.mult).then_inc(cos_ready, 1)

            def split(n):
                pool.wait_ge(cos_ready, n + 1)
                pool.wait_ge(rot_ready, n + 1)
                nc.gpsimd.tensor_tensor(t1[:], t1[:], t2[:], ALU.add).then_inc(sum_ready, 1)

            def low(n, before, count):
                if before is not None:
                    pool.wait_ge(before, count)
                pool.wait_ge(hi_ready, n + 1)
                nc.gpsimd.tensor_tensor(lo[:], t1[:], hi[:].bitcast(F32), ALU.subtract).then_inc(lo_ready, 1)

            def before(name, b):
                if name[0] == "q":
                    p = int(name[1])
                    return k_stacked[(p + 1) % 2], STACK * (2 * b + [1, 2, 2, 3][p])
                return q_stacked, STACK * (4 * b + int(name[1]) + 2)

            def group_rstd(b):
                pool.wait_ge(geps_ready, b + 1)
                nc.gpsimd.tensor_tensor(grstd[:], dmean[:], mhalf[:, 0:2], ALU.pow).then_inc(grstd_ready, 1)

            def scale_heads(phase):
                pool.wait_ge(den_ready, phase + 1)
                nc.gpsimd.tensor_tensor(fac[:], dent[:], dent[:], ALU.mult).then_inc(fac_step, 1)
                pool.wait_ge(fac_step, 4 * phase + 1)
                nc.gpsimd.tensor_tensor(fac[:], fac[:], epst[:], ALU.mult).then_inc(fac_step, 1)
                pool.wait_ge(fac_step, 4 * phase + 2)
                pool.wait_ge(var_ready, phase + 1)
                nc.gpsimd.tensor_tensor(fac[:], fac[:], var[:], ALU.add).then_inc(fac_step, 1)
                pool.wait_ge(fac_step, 4 * phase + 3)
                nc.gpsimd.tensor_tensor(fac[:], fac[:], mhalf[:], ALU.pow).then_inc(fac_step, 1)
                pool.wait_ge(fac_step, 4 * phase + 4)
                tv = tA[:].rearrange("p t (h d) -> p (t h) d", d=32)
                nc.gpsimd.tensor_tensor(tv, tv, fac[:].unsqueeze(2).to_broadcast([128, 16, 32]),
                                        ALU.mult).then_inc(on_ready, 1)

            group_rstd(0)
            pool.wait_ge(tables_in, 16 * NTABLES)
            rotate_cos(0, 0)
            split(0)
            low(0, None, 0)
            rotate_cos(1, 0)
            split(1)
            low(1, k_stacked[0], STACK)
            rotate_cos(2, 1)
            split(2)
            low(2, q_stacked, STACK)

            def body(b, first, last):
                for p in range(PHASES):
                    ph = nphase(b, p - 1, p == 0)
                    if p == 3 and not last:
                        low(prep_order("k2", b), *before("k2", b))
                    if p < 3 or not last:
                        rotate_cos(prep_order(f"q{p}", b), (p + 1) % 2)
                        split(prep_order(f"q{p}", b))
                        low(prep_order(f"q{p}", b), *before(f"q{p}", b))
                    if p == 2 and not last:
                        group_rstd(b + 1)
                    if not (first and p == 0):
                        scale_heads(ph)
                    if p < 2 or not last:
                        rotate_cos(prep_order(f"k{p}", b), p % 2)
                        split(prep_order(f"k{p}", b))
                        if p != 2:
                            low(prep_order(f"k{p}", b), *before(f"k{p}", b))

            body(0, True, False)
            with pool.Fori(1, B - 1) as b:
                body(b, False, False)
            body(B - 1, False, True)
            scale_heads(4 * B - 1)


def layer1_attention(nc, x1, wqT, wkT, wv, ident, causal, t2, xn2T, featD):
    B, L, E = x1.shape
    NT = L // 128
    LN_EPS = 1e-5
    SCALE = float(E) ** -0.5

    ORDER = [3, 4, 5, 6, 7, 2, 1, 0]
    assert sorted(ORDER) == list(range(NT))

    T_TASKS = ["T00", "T10", "T01", "T11"]
    QV_TASKS = ["Q00", "Q10", "V0", "V1", "Q01", "Q11", "V2", "V3"]
    X_TASKS = [f"X{k}{h}" for k in range(2) for h in range(2)]
    P_TASKS = [f"P{i}{h}" for i in range(NT) for h in range(ORDER[i] // 4 + 1)]
    LISTS = {"first": QV_TASKS + P_TASKS + T_TASKS, "mid": QV_TASKS + X_TASKS + P_TASKS + T_TASKS,
             "last": QV_TASKS + X_TASKS + P_TASKS}
    HEAD = ["A0", "A1"] + T_TASKS

    def place(name):
        if name[0] == "A":
            return 4 + int(name[1])
        if name[0] == "T":
            return T_TASKS.index(name)
        if name in QV_TASKS:
            return [4, 5, 0, 1, 2, 3, 4, 5][QV_TASKS.index(name)]
        return 4 + (X_TASKS if name[0] == "X" else P_TASKS).index(name) % 2

    def before(name, b, first, last, counts):
        of = lambda names: sum(1 for t in names if counts(t))
        one, mid = of(LISTS["first"]), of(LISTS["mid"])
        if name == "end":
            return of(HEAD) + one + mid * (B - 2) + of(LISTS["last"])
        if name in HEAD and isinstance(b, str):
            return of(HEAD[:HEAD.index(name)])
        tasks = LISTS["first" if first else "mid"]
        here = of(tasks[:tasks.index(name)])
        return of(HEAD) + here if first else of(HEAD) + one + mid * (b - 1) + here

    def number(name, b, first):
        return before(name, b, first, False, lambda t: True)

    def earlier(name, b, first):
        return before(name, b, first, False, lambda t: place(t) == place(name))

    def split_number(name, b, first):
        return before(name, b, first, False, lambda t: t[0] != "X")

    with ExitStack() as ctx:
        def sb(name, shape, dt=F32):
            return ctx.enter_context(nc.sbuf_tensor("l1_" + name, shape, dt))

        def sem(name):
            return ctx.enter_context(nc.semaphore("l1_" + name))

        idn, mask = sb("ident", [128, 128]), sb("causal", [128, 128])
        wq_in, wk_in, wv_in = (sb(n, [128, 2, E]) for n in ("wq_in", "wk_in", "wv_in"))
        ahi, alo, vhw, vlw = (sb(n, [128, 2, E], F32R) for n in ("ahi", "alo", "wvhi", "wvlo"))
        xa, xr = sb("xa", [128, NT, E]), sb("xr", [128, NT, E])
        xn, xn2 = sb("xn", [128, NT, E]), sb("xn2", [128, NT, E])
        feat = sb("feat", [128, NT, E])
        t2s = sb("t2s", [128, NT, E])
        xt2 = sb("xt2", [128, 2, L])
        xhi, xlo, qhi, qlo = (sb(n, [128, 2, L], F32R) for n in ("xhi", "xlo", "qhi", "qlo"))
        vhi, vlo = (sb(n, [128, NT, E], F32R) for n in ("vhi", "vlo"))
        prob = [sb(f"prob{n}", [128, L]) for n in range(2)]
        phi = [sb(f"phi{n}", [128, NT, 128], F32R) for n in range(2)]
        plo = [sb(f"plo{n}", [128, NT, 128], F32R) for n in range(2)]
        st1, st2 = sb("st1", [128, NT, 6]), sb("st2", [128, NT, 6])
        mv1, mv2 = sb("mv1", [128, NT, 2]), sb("mv2", [128, NT, 2])
        eps1, eps2, rstd1, rstd2, mhalf = (sb(n, [128, NT]) for n in ("eps1", "eps2", "rstd1", "rstd2", "mhalf"))
        shift1, shift2, minus = (sb(n, [128, NT]) for n in ("shift1", "shift2", "minus"))
        nmax, rsum, rinv = sb("nmax", [128, NT]), sb("rsum", [128, NT]), sb("rinv", [128, NT])

        def bank(name, shape):
            return ctx.enter_context(nc.psum_tensor("l1_" + name, shape, F32))

        sc = [bank(f"scores{n}", [128, L]) for n in range(2)]
        av = [bank(f"av{n}", [128, 512]) for n in range(2)]
        ring = [sc[n // 2][:, 512 * (n % 2):512 * (n % 2) + 512] for n in range(4)] + [bank(f"ring{n}", [128, 512])[:]
                                                                                     for n in range(2)]

        consts, xa_in, xr_in, made = sem("consts"), sem("xa_in"), sem("xr_in"), sem("made")
        waited = sem("waited")
        ring_ready, hi_ready = sem("ring_ready"), sem("hi_ready")
        ring_read = [sem(f"ring_read{n}") for n in range(6)]
        wv_hi, wv_split = sem("wv_hi"), sem("wv_split")
        stats1, agg1, eps1_ready, rstd1_ready, xn_ready = (sem(n) for n in ("stats1", "agg1", "eps1_ready", "rstd1_ready",
                                                                            "xn_ready"))
        stats2, agg2, eps2_ready, rstd2_ready, xn2_ready = (sem(n) for n in ("stats2", "agg2", "eps2_ready", "rstd2_ready",
                                                                             "xn2_ready"))
        feat_added, feat_out = sem("feat_added"), sem("feat_out")
        scores_ready, masked, max_ready, prob_ready = (sem(n) for n in ("scores_ready", "masked", "max_ready", "prob_ready"))
        av_ready, rinv_ready, out_ready = sem("av_ready"), sem("rinv_ready"), sem("out_ready")
        xt2_out, t2_out = sem("xt2_out"), sem("t2_out")
        NCONST = 5

        block = ctx.enter_context(nc.Block())

        @block.sync
        def _(sp):
            tiles = lambda a: a.rearrange("(t p) e -> p t e", p=128)
            sp.sem_inc(xt2_out, 16)
            sp.dma_start(xa[:], tiles(x1[0])).then_inc(xa_in, 16)
            for dst, src in ((wq_in[:], wqT.rearrange("(k p) n -> p k n", p=128)),
                             (wk_in[:], wkT.rearrange("(k p) n -> p k n", p=128)),
                             (wv_in[:], wv.rearrange("(k p) n -> p k n", p=128)),
                             (idn[:], ident), (mask[:], causal)):
                sp.dma_start(dst, src).then_inc(consts, 16)

            def body(b, first, last):
                if not first:
                    sp.wait_ge(out_ready, NT * b)
                    sp.dma_start(tiles(t2[b - 1]), t2s[:]).then_inc(t2_out, 16)
                sp.dma_start(xr[:], tiles(x1[b])).then_inc(xr_in, 16)
                if not last:
                    sp.wait_ge(xn_ready, b + 1)
                    sp.dma_start(xa[:], tiles(x1[b + 1])).then_inc(xa_in, 16)
                if not first:
                    for name in X_TASKS[2:]:
                        sp.wait_ge(ring_read[place(name)], earlier(name, b, first) + 1)
                    sp.dma_start(xn2T[b - 1].rearrange("(k p) t -> p k t", p=128), xt2[:]).then_inc(xt2_out, 16)

            body(0, True, False)
            with sp.Fori(1, B - 1) as b:
                body(b, False, False)
            body(B - 1, False, True)
            sp.wait_ge(out_ready, NT * B)
            sp.dma_start(tiles(t2[B - 1]), t2s[:]).then_inc(t2_out, 16)
            for n in (4, 5):
                sp.wait_ge(ring_read[n], before("end", 0, False, False, lambda t: place(t) == n) + 2)
            sp.dma_start(xn2T[B - 1].rearrange("(k p) t -> p k t", p=128), xt2[:]).then_inc(xt2_out, 16)
            sp.wait_ge(feat_added, B + 1)
            sp.dma_start(featD, feat[:]).then_inc(feat_out, 16)
            sp.wait_ge(feat_out, 16)
            sp.wait_ge(t2_out, 16 * B)
            sp.wait_ge(xt2_out, 16 * (B + 1))

        @block.tensor
        def _(pe):
            def three(out, a, b, start, stop):
                nc.tensor.matmul(out, a[0], b[0], start=start, stop=False)
                nc.tensor.matmul(out, a[0], b[1], start=False, stop=False)
                return nc.tensor.matmul(out, a[1], b[0], start=False, stop=stop)

            def whole(names, b, first):
                latest = {place(name): name for name in names}
                for n, name in latest.items():
                    pe.wait_ge(ring_read[n], earlier(name, b, first) + 1)

            def begin(name, b, first):
                n = place(name)
                if not (isinstance(b, str) and n < 4):
                    pe.wait_ge(ring_read[n], earlier(name, b, first))
                return ring[n]

            pe.wait_ge(consts, 16 * NCONST)
            for i in range(2):
                for k in range(2):
                    mm = nc.tensor.matmul(ring[4 + i][:, 0:E], wq_in[:, k, 128 * i:128 * i + 128], wk_in[:, k, :],
                                          start=(k == 0), stop=(k == 1))
                mm.then_inc(ring_ready, 1)

            def xn_transposes(b, first, count):
                pe.wait_ge(xn_ready, count)
                for name in T_TASKS:
                    bk, k, h = begin(name, b, first), int(name[1]), int(name[2])
                    for t in range(4):
                        mm = nc.tensor.transpose(bk[:, 128 * t:128 * t + 128], xn[:, 4 * h + t, 128 * k:128 * k + 128],
                                                 idn[:])
                    mm.then_inc(ring_ready, 1)

            def xn2_transposes(count, befores):
                for n, before_ in befores:
                    if n == 0:
                        pe.wait_ge(xn2_ready, count)
                    bk = 4 + n % 2
                    pe.wait_ge(ring_read[bk], before_)
                    for t in range(4):
                        mm = nc.tensor.transpose(ring[bk][:, 128 * t:128 * t + 128],
                                                 xn2[:, 4 * (n % 2) + t, 128 * (n // 2):128 * (n // 2) + 128], idn[:])
                    mm.then_inc(ring_ready, 1)

            def xn_whole(b, first, h):
                for k in range(2):
                    name = f"T{k}{h}"
                    after = {"T00": "V0", "T10": "V1", "T01": "Q01", "T11": "Q11"}[name]
                    assert place(after) == place(name)
                    pe.wait_ge(ring_read[place(name)], earlier(after, b, first))

            def body(b, first, last):
                if first:
                    pe.wait_ge(ring_read[4], 1)
                    pe.wait_ge(ring_read[5], 1)
                for name in QV_TASKS:
                    if name in ("Q00", "Q01"):
                        xn_whole(b, first, int(name[2]))
                    if first and name == "V0":
                        pe.wait_ge(wv_split, 2)
                    bk = begin(name, b, first)
                    if name[0] == "Q":
                        j, h = int(name[1]), int(name[2])
                        tok = slice(512 * h, 512 * h + 512)
                        for k in range(2):
                            mm = three(bk, (ahi[:, k, 128 * j:128 * j + 128], alo[:, k, 128 * j:128 * j + 128]),
                                       (xhi[:, k, tok], xlo[:, k, tok]), k == 0, k == 1)
                    else:
                        n = int(name[1])
                        for t in range(2):
                            tok = slice(256 * n + 128 * t, 256 * n + 128 * t + 128)
                            for k in range(2):
                                mm = three(bk[:, E * t:E * t + E], (xhi[:, k, tok], xlo[:, k, tok]),
                                           (vhw[:, k, :], vlw[:, k, :]), k == 0, k == 1)
                    mm.then_inc(ring_ready, 1)
                whole(QV_TASKS[2:6], b, first)
                for i in range(NT + 2):
                    if i < NT:
                        t = ORDER[i]
                        if i >= 2:
                            pe.wait_ge(prob_ready, NT * b + i - 1)
                        for c0 in range(0, 128 * (t + 1), 512):
                            c1 = min(c0 + 512, 128 * (t + 1))
                            for k in range(2):
                                tok = slice(128 * t, 128 * t + 128)
                                mm = three(sc[i % 2][:, c0:c1], (qhi[:, k, tok], qlo[:, k, tok]),
                                           (xhi[:, k, c0:c1], xlo[:, k, c0:c1]), k == 0, k == 1)
                        mm.then_inc(scores_ready, 1)
                    if i < 2 and not first:
                        xn2_transposes(b, [(n, earlier(X_TASKS[n], b, first)) for n in (2 * i, 2 * i + 1)])
                    if 1 <= i <= NT:
                        q = ORDER[i - 1]
                        pe.wait_ge(prob_ready, NT * b + i)
                        for h in range(q // 4 + 1):
                            bk = begin(f"P{i - 1}{h}", b, first)
                            for kb in range(4 * h, min(4 * h + 4, q + 1)):
                                mm = nc.tensor.transpose(bk[:, 128 * (kb % 4):128 * (kb % 4) + 128],
                                                         prob[(i - 1) % 2][:, 128 * kb:128 * kb + 128], idn[:])
                            mm.then_inc(ring_ready, 1)
                    if i == NT and not last:
                        xn_transposes(b, first, b + 2)
                    if i >= 2:
                        q, n = ORDER[i - 2], i % 2
                        whole([f"P{i - 2}{h}" for h in range(q // 4 + 1)], b, first)
                        if i >= 4 or not first:
                            pe.wait_ge(out_ready, NT * b + i - 3)
                        for kb in range(q + 1):
                            mm = three(av[n][:, 0:E], (phi[n][:, kb, :], plo[n][:, kb, :]),
                                       (vhi[:, kb, :], vlo[:, kb, :]), kb == 0, kb == q)
                        mm.then_inc(av_ready, 1)

            xn_transposes("head", False, 1)
            body(0, True, False)
            with pe.Fori(1, B - 1) as b:
                body(b, False, False)
            body(B - 1, False, True)
            e = [before("end", 0, False, False, lambda t: place(t) == 4 + n) for n in range(2)]
            xn2_transposes(B, [(n, e[n % 2] + n // 2) for n in range(4)])

        def parts(name):
            if name[0] in "TQ":
                k, h = int(name[1]), int(name[2])
                hi, lo = (xhi, xlo) if name[0] == "T" else (qhi, qlo)
                return hi[:, k, 512 * h:512 * h + 512], lo[:, k, 512 * h:512 * h + 512], 512
            if name[0] == "V":
                n = int(name[1])
                flat = lambda a: a[:, 2 * n:2 * n + 2, :].rearrange("p t e -> p (t e)")
                return flat(vhi), flat(vlo), 512
            i, h = int(name[1]), int(name[2])
            kb = min(4 * h + 4, ORDER[i] + 1)
            flat = lambda a: a[:, 4 * h:kb, :].rearrange("p t e -> p (t e)")
            return flat(phi[i % 2]), flat(plo[i % 2]), 128 * (kb - 4 * h)

        @block.scalar
        def _(act):
            act.wait_ge(consts, 16 * NCONST)
            def ln1_apply(b, tiles):
                if 0 in tiles:
                    act.wait_ge(rstd1_ready, 3 * (b + 1))
                for t in tiles:
                    ins = nc.scalar.activation(xn[:, t, :], xa[:, t, :], ACT.Identity, bias=shift1[:, t:t + 1],
                                               scale=rstd1[:, t:t + 1])
                if NT - 1 in tiles:
                    ins.then_inc(xn_ready, 1)

            def ln2_apply(b, tiles):
                if 0 in tiles:
                    act.wait_ge(rstd2_ready, 3 * b)
                    act.wait_ge(feat_added, b)
                for t in tiles:
                    ins = nc.scalar.activation(xn2[:, t, :], t2s[:, t, :], ACT.Identity, bias=shift2[:, t:t + 1],
                                               scale=rstd2[:, t:t + 1])
                if NT - 1 in tiles:
                    ins.then_inc(xn2_ready, 1)

            ln1_apply(0, range(NT))
            for i in range(2):
                act.wait_ge(ring_ready, i + 1)
                nc.scalar.activation(ahi[:, i, :], ring[4 + i][:, 0:E], ACT.Copy, scale=SCALE).then_inc(hi_ready, 1)
            nc.scalar.activation(vhw[:], wv_in[:], ACT.Copy).then_inc(wv_hi, 1)

            def high(name, b, first):
                hi, lo, w = parts(name)
                if name[0] == "P" and (int(name[1]) >= 2 or not first):
                    act.wait_ge(av_ready, NT * b + int(name[1]) - 1)
                act.wait_ge(ring_ready, number(name, b, first) + 1)
                nc.scalar.activation(hi, ring[place(name)][:, 0:w], ACT.Copy).then_inc(hi_ready, 1)

            def take_x(n, num, b, count):
                k, h = n // 2, n % 2
                bk = 4 + n % 2
                if n == 0:
                    act.wait_ge(xt2_out, count)
                act.wait_ge(ring_ready, num + 1)
                nc.scalar.activation(xt2[:, k, 512 * h:512 * h + 512], ring[bk], ACT.Copy).then_inc(ring_read[bk], 1)

            def body(b, first, last):
                for n, name in enumerate(QV_TASKS):
                    high(name, b, first)
                    if not first and 3 <= n <= 6:
                        ln2_apply(b, (2 * n - 6, 2 * n - 5))
                for i in range(NT + 1):
                    if i < 2 and not first:
                        for n in (2 * i, 2 * i + 1):
                            take_x(n, number(X_TASKS[n], b, first), b, 16 * b)
                    if i < NT:
                        t = ORDER[i]
                        act.wait_ge(max_ready, NT * b + i + 1)
                        nc.scalar.activation(prob[i % 2][:, 0:128 * (t + 1)], sc[i % 2][:, 0:128 * (t + 1)], ACT.Exp,
                                             bias=nmax[:, t:t + 1], accum_out=rsum[:, t:t + 1]).then_inc(prob_ready, 1)
                    if i >= 1:
                        for h in range(ORDER[i - 1] // 4 + 1):
                            high(f"P{i - 1}{h}", b, first)
                    if not last and 5 <= i <= 7:
                        ln1_apply(b + 1, {5: range(0, 3), 6: range(3, 6), 7: range(6, NT)}[i])
                if not last:
                    for name in T_TASKS:
                        high(name, b, first)

            for name in T_TASKS:
                high(name, "head", False)
            body(0, True, False)
            with act.Fori(1, B - 1) as b:
                body(b, False, False)
            body(B - 1, False, True)
            ln2_apply(B, range(NT))
            for n in range(4):
                take_x(n, number("end", 0, False) + n, B, 16 * B)

        @block.vector
        def _(dve):
            dve.wait_ge(consts, 16 * NCONST)
            dve.wait_ge(made, 2)

            def ln1_stats(b, t):
                if t == 0:
                    dve.wait_ge(xa_in, 16 * (b + 1))
                nc.vector.bn_stats(st1[:, t, :], xa[:, t, :]).then_inc(stats1, 1)

            def ln1_eps(b):
                dve.wait_ge(stats1, NT * (b + 1))
                dve.sem_inc(waited, 1)
                for t in range(NT):
                    nc.vector.bn_aggr(mv1[:, t, :], st1[:, t, :]).then_inc(agg1, 1)
                dve.wait_ge(agg1, NT * (b + 1))
                nc.vector.tensor_scalar(eps1[:], mv1[:, :, 1], LN_EPS, None, ALU.add).then_inc(eps1_ready, 1)

            def ln2_eps(b):
                dve.wait_ge(stats2, NT * b)
                dve.sem_inc(waited, 1)
                for t in range(NT):
                    nc.vector.bn_aggr(mv2[:, t, :], st2[:, t, :]).then_inc(agg2, 1)
                dve.wait_ge(agg2, NT * b)
                nc.vector.tensor_scalar(eps2[:], mv2[:, :, 1], LN_EPS, None, ALU.add).then_inc(eps2_ready, 1)

            def low(name, b, first):
                hi, lo, w = parts(name)
                bk = place(name)
                dve.wait_ge(hi_ready, split_number(name, b, first) + 1)
                nc.vector.tensor_tensor(lo, ring[bk][:, 0:w], hi.bitcast(F32), ALU.subtract).then_inc(ring_read[bk], 1)

            for t in range(NT):
                ln1_stats(0, t)
            ln1_eps(0)
            for i in range(2):
                dve.wait_ge(hi_ready, i + 1)
                nc.vector.scalar_tensor_tensor(out=alo[:, i, :], in0=ring[4 + i][:, 0:E], scalar=SCALE,
                                               in1=ahi[:, i, :].bitcast(F32), op0=ALU.mult,
                                               op1=ALU.subtract).then_inc(ring_read[4 + i], 1)
            dve.wait_ge(wv_hi, 1)
            nc.vector.tensor_tensor(vlw[:], wv_in[:], vhw[:].bitcast(F32), ALU.subtract).then_inc(wv_split, 2)
            for name in T_TASKS:
                low(name, "head", False)

            def output(b, i, last):
                q = ORDER[i]
                if i == 0:
                    dve.wait_ge(xr_in, 16 * (b + 1))
                    if not isinstance(b, int) or b > 0:
                        dve.wait_ge(t2_out, 16 * b)
                nc.vector.reciprocal(rinv[:, q:q + 1], rsum[:, q:q + 1]).then_inc(rinv_ready, 1)
                dve.wait_ge(rinv_ready, NT * b + i + 1)
                dve.wait_ge(av_ready, NT * b + i + 1)
                nc.vector.scalar_tensor_tensor(out=t2s[:, q, :], in0=av[i % 2][:, 0:E], scalar=rinv[:, q:q + 1],
                                               in1=xr[:, q, :], op0=ALU.mult, op1=ALU.add).then_inc(out_ready, 1)

            def body(b, first, last):
                for name in QV_TASKS:
                    if name == "V0" and not first:
                        ln2_eps(b)
                    low(name, b, first)
                for i in range(NT + 2):
                    if i < NT:
                        t = ORDER[i]
                        w = 128 * (t + 1)
                        dve.wait_ge(scores_ready, NT * b + i + 1)
                        nc.vector.tensor_tensor(sc[i % 2][:, w - 128:w], sc[i % 2][:, w - 128:w], mask[:],
                                                ALU.add).then_inc(masked, 1)
                        dve.wait_ge(masked, NT * b + i + 1)
                        nc.vector.tensor_reduce(nmax[:, t:t + 1], sc[i % 2][:, 0:w], AX.X, ALU.max,
                                                negate=True).then_inc(max_ready, 1)
                    if 1 <= i <= NT:
                        for h in range(ORDER[i - 1] // 4 + 1):
                            if (i >= 3 or not first) and h == 0:
                                dve.wait_ge(av_ready, NT * b + i - 2)
                            low(f"P{i - 1}{h}", b, first)
                    if i == NT and not last:
                        for name in T_TASKS:
                            low(name, b, first)
                    if i >= 2:
                        output(b, i - 2, last)
                    if not last and i < 4:
                        ln1_stats(b + 1, 2 * i)
                        ln1_stats(b + 1, 2 * i + 1)
                    if not last and i == 4:
                        ln1_eps(b + 1)
                    if i >= 2:
                        q = ORDER[i - 2]
                        dve.wait_ge(out_ready, NT * b + i - 1)
                        nc.vector.bn_stats(st2[:, q, :], t2s[:, q, :]).then_inc(stats2, 1)

            body(0, True, False)
            with dve.Fori(1, B - 1) as b:
                body(b, False, False)
            body(B - 1, False, True)
            ln2_eps(B)

        @block.gpsimd
        def _(pool):
            nc.gpsimd.memset(mhalf[:], -0.5).then_inc(made, 1)
            nc.gpsimd.memset(minus[:], -1.0).then_inc(made, 1)
            nc.gpsimd.memset(feat[:], 0.0).then_inc(feat_added, 1)
            pool.wait_ge(made, 2)

            def rstd(ready, eps, out, done, count, mv, shift):
                pool.wait_ge(ready, count)
                nc.gpsimd.tensor_tensor(out[:], eps[:], mhalf[:], ALU.pow).then_inc(done, 1)
                pool.wait_ge(done, 3 * count - 2)
                nc.gpsimd.tensor_tensor(shift[:], mv[:, :, 0], out[:], ALU.mult).then_inc(done, 1)
                pool.wait_ge(done, 3 * count - 1)
                nc.gpsimd.tensor_tensor(shift[:], shift[:], minus[:], ALU.mult).then_inc(done, 1)

            def ln1(b):
                rstd(eps1_ready, eps1, rstd1, rstd1_ready, b + 1, mv1, shift1)

            def ln2(b):
                rstd(eps2_ready, eps2, rstd2, rstd2_ready, b, mv2, shift2)
                pool.wait_ge(xn2_ready, b)
                pool.wait_ge(feat_added, b)
                nc.gpsimd.tensor_tensor(feat[:], feat[:], xn2[:], ALU.add).then_inc(feat_added, 1)

            def body(b, first, last):
                if not first:
                    ln2(b)
                if not last:
                    ln1(b + 1)

            ln1(0)
            body(0, True, False)
            with pool.Fori(1, B - 1) as b:
                body(b, False, False)
            body(B - 1, False, True)
            ln2(B)


def layer1_experts(nc, t2, xn2T, featD, wr, br, w1, bn1, w2, bn2, wo, bo, ident, selE, out):
    B, L, D = t2.shape
    NE = w1.shape[0]
    NT = L // 128
    CH = 512
    U = 2 * NE
    BN_EPS = 1e-3
    NS = 2

    with ExitStack() as ctx:
        def sb(name, shape, dt=F32):
            return ctx.enter_context(nc.sbuf_tensor("e_" + name, shape, dt))

        def sem(name):
            return ctx.enter_context(nc.semaphore("e_" + name))

        whi, wlo = sb("whi", [128, NE, 3, 2, D], F32R), sb("wlo", [128, NE, 3, 2, D], F32R)
        stage = [sb(f"stage{n}", [128, 2, D]) for n in range(NS)]
        wbc = sb("wbc", [128, NE, L])
        feat = wbc[:, 0:2, :].rearrange("p a b -> p (a b)").rearrange("p (t e) -> p t e", e=D)
        featT = wbc[:, 2:4, :]
        xraw = sb("xraw", [128, 2, CH])
        xhi = [sb(f"xhi{c}", [128, 2, CH], F32R) for c in range(2)]
        xlo = [sb(f"xlo{c}", [128, 2, CH], F32R) for c in range(2)]
        r1 = [sb(f"r1{m}", [128, CH]) for m in range(2)]
        r2 = [sb(f"r2{m}", [128, CH]) for m in range(2)]
        h1hi, h1lo, h2hi, h2lo = ([sb(f"{n}{c}", [128, 2, CH], F32R) for c in range(2)]
                                  for n in ("h1hi", "h1lo", "h2hi", "h2lo"))
        res = [sb(f"res{c}", [128, 4, D]) for c in range(2)]
        idn = sb("ident", [128, 128])
        sel = res[1][0:NE, :, :].rearrange("p t e -> p (t e)").rearrange("p (n m) -> p n m", m=128)
        wr_sb, br_sb, bo_sb, ones = sb("wr", [128, 2, NE]), sb("br", [1, NE]), sb("bo", [NE, D]), sb("ones", [1, 128])
        bn = [[sb(f"bn{n}{q}", [128, 2, NE]) for q in range(5)] for n in range(2)]
        mhalf, rs = sb("mhalf", [128, 2, NE]), [sb(f"rs{n}", [128, 2, NE]) for n in range(2)]
        nm, sm, rsm = sb("nm", [128, NT]), sb("sm", [128, NT]), sb("rsm", [128, NT])
        lg, wt = sb("lg", [128, NT, NE]), sb("wt", [128, NT, NE])
        wT = sb("wT", [NE, L])

        def bank(name, shape):
            return ctx.enter_context(nc.psum_tensor("e_" + name, shape, F32))

        p1 = [bank(f"h1_{m}", [128, CH]) for m in range(2)]
        p2 = [bank(f"h2_{m}", [128, CH]) for m in range(2)]
        py = [bank(f"y_{c}", [128, 4, D]) for c in range(2)]
        four = [p1[0], p1[1], p2[0], p2[1]]

        consts, feat_in, x_in, made = sem("consts"), sem("feat_in"), sem("x_in"), sem("made")
        waited = sem("waited")
        stage_in = [sem(f"stage_in{n}") for n in range(NS)]
        wsplit_hi, wsplit = sem("wsplit_hi"), sem("wsplit")
        x_split_hi, x_split = sem("x_split_hi"), sem("x_split")
        bn_step, bn_eps, bn_rs, bn_ready = sem("bn_step"), sem("bn_eps"), sem("bn_rs"), sem("bn_ready")
        setup_pe, featT_ready, soft = sem("setup_pe"), sem("featT_ready"), sem("soft")
        exp_ready, wT_ready, wbc_ready = sem("exp_ready"), sem("wT_ready"), sem("wbc_ready")
        h1_ready, r1_ready, hi1_ready, lo1_ready = sem("h1_ready"), sem("r1_ready"), sem("hi1_ready"), sem("lo1_ready")
        h2_ready, r2_ready, w2_ready = sem("h2_ready"), sem("r2_ready"), sem("w2_ready")
        hi2_ready, lo2_ready, y_ready, y_read = sem("hi2_ready"), sem("lo2_ready"), sem("y_ready"), sem("y_read")
        res_in = [sem(f"res_in{c}") for c in range(2)]
        res_out = [sem(f"res_out{c}") for c in range(2)]
        NCONST = 16

        block = ctx.enter_context(nc.Block())

        @block.sync
        def _(sp):
            sp.dma_start(feat, featD).then_inc(feat_in, 16)
            cols = lambda a: a.rearrange("(k p) n -> p k n", p=128)
            for n, w in ((0, w1), (1, w2)):
                sp.dma_start(stage[n][:], cols(w[0])).then_inc(stage_in[n], 16)
            sp.dma_start(xraw[:], cols(xn2T[0])[:, :, 0:CH]).then_inc(x_in, 16)
            for dst, src in [(idn[:], ident), (sel, selE), (wr_sb[:], cols(wr)), (br_sb[:], br), (bo_sb[:], bo)]:
                sp.dma_start(dst, src).then_inc(consts, 16)
            for n, arrays in enumerate((bn1, bn2)):
                for q in range(5):
                    sp.dma_start(bn[n][q][:], cols(arrays[q])).then_inc(consts, 16)
            sp.wait_ge(consts, 16 * 15)
            for i in range(NS, 3 * NE):
                sp.wait_ge(wsplit, i - NS + 1)
                sp.dma_start(stage[i % NS][:], cols((w1, w2, wo)[i % 3][i // 3])).then_inc(stage_in[i % NS], 16)
                if i == 6:
                    sp.wait_ge(x_split, 1)
                    sp.dma_start(xraw[:], cols(xn2T[0])[:, :, CH:L]).then_inc(x_in, 16)

            def rows(a, b, c):
                return a[b, CH * c:CH * c + CH, :].rearrange("(t p) e -> p t e", p=128)

            def body(b, first, last):
                for c in range(2):
                    if not (first and c == 0):
                        nb, ncx = (b, 1) if c == 0 else (b + 1, 0)
                        if not (last and c == 1):
                            sp.wait_ge(x_split, 2 * b + c + 1)
                            sp.dma_start(xraw[:], cols(xn2T[nb])[:, :, CH * ncx:CH * ncx + CH]).then_inc(x_in, 16)
                    if not first:
                        sp.wait_ge(res_out[c], 16 * b)
                        sp.sem_inc(waited, 1)
                    if first and c == 1:
                        sp.wait_ge(wbc_ready, 2 * NE)
                    sp.dma_start(res[c][:], rows(t2, b, c)).then_inc(res_in[c], 16)
                    if not (first and c == 0):
                        pb = b if c == 1 else b - 1
                        sp.wait_ge(y_read, 2 * b + c)
                        sp.dma_start(rows(out, pb, 1 - c), res[1 - c][:]).then_inc(res_out[1 - c], 16)

            body(0, True, False)
            with sp.Fori(1, B - 1) as b:
                body(b, False, False)
            body(B - 1, False, True)
            sp.wait_ge(y_read, 2 * B)
            sp.dma_start(rows(out, B - 1, 1), res[1][:]).then_inc(res_out[1], 16)
            for c in range(2):
                sp.wait_ge(res_out[c], 16 * B)

        @block.tensor
        def _(pe):
            def three(o, a, b, start, stop):
                nc.tensor.matmul(o, a[0], b[0], start=start, stop=False, skip_group_check=True)
                nc.tensor.matmul(o, a[0], b[1], start=False, stop=False, skip_group_check=True)
                return nc.tensor.matmul(o, a[1], b[0], start=False, stop=stop, skip_group_check=True)

            pe.wait_ge(consts, 16 * 15)
            pe.wait_ge(feat_in, 16)
            pe.wait_ge(made, 2)
            for k in range(2):
                for h in range(2):
                    for t in range(4):
                        mm = nc.tensor.transpose(four[2 * k + h][:, 128 * t:128 * t + 128],
                                                 feat[:, 4 * h + t, 128 * k:128 * k + 128], idn[:])
                    mm.then_inc(setup_pe, 1)
            pe.wait_ge(featT_ready, 4)
            for t in range(NT):
                o = py[0][:, 0, NE * t:NE * t + NE]
                for k in range(2):
                    nc.tensor.matmul(o, featT[:, k, 128 * t:128 * t + 128], wr_sb[:, k, :], start=(k == 0), stop=False)
                mm = nc.tensor.matmul(o, ones[:], br_sb[:], start=False, stop=True)
            mm.then_inc(setup_pe, 1)
            pe.wait_ge(soft, 5)
            for t in range(NT):
                mm = nc.tensor.transpose(py[1][0:NE, t // 2, 128 * (t % 2):128 * (t % 2) + 128], wt[:, t, :], idn[:])
            mm.then_inc(setup_pe, 1)
            pe.wait_ge(wT_ready, 1)
            for n in range(2 * NE):
                if n >= 4:
                    pe.wait_ge(wbc_ready, n - 3)
                nc.tensor.matmul(four[n % 4][:], sel[:, n // 2, :], wT[:, CH * (n % 2):CH * (n % 2) + CH],
                                 start=True, stop=True).then_inc(setup_pe, 1)
            pe.wait_ge(wbc_ready, 2 * NE)

            def hidden1(b, u, first):
                c, e = u // NE, u % NE
                if e == 0:
                    pe.wait_ge(x_split, 2 * b + c + 1)
                if first:
                    if c == 0:
                        pe.wait_ge(wsplit, 3 * e + 3)
                for m in range(2):
                    if u > 0 or not first:
                        pe.wait_ge(r1_ready, 2 * (U * b + u) + m - 1)
                    for k in range(2):
                        cut = slice(128 * m, 128 * m + 128)
                        mm = three(p1[m][:], (whi[:, e, 0, k, cut], wlo[:, e, 0, k, cut]),
                                   (xhi[c][:, k, :], xlo[c][:, k, :]), k == 0, k == 1)
                    mm.then_inc(h1_ready, 1)

            def hidden2(b, u, first):
                e = u % NE
                pe.wait_ge(lo1_ready, 2 * (U * b + u) + 2)
                for m in range(2):
                    if u > 0 or not first:
                        pe.wait_ge(r2_ready, 2 * (U * b + u) + m - 1)
                    for k in range(2):
                        cut = slice(128 * m, 128 * m + 128)
                        mm = three(p2[m][:], (whi[:, e, 1, k, cut], wlo[:, e, 1, k, cut]),
                                   (h1hi[u % 2][:, k, :], h1lo[u % 2][:, k, :]), k == 0, k == 1)
                    mm.then_inc(h2_ready, 1)

            def output(b, u, first):
                c, e = u // NE, u % NE
                if e == 0:
                    if not first:
                        pe.wait_ge(y_read, 2 * b + c - 1)
                    for t in range(4):
                        nc.tensor.matmul(py[c][:, t, :], wT[:, CH * c + 128 * t:CH * c + 128 * t + 128], bo_sb[:],
                                         start=(t % 2 == 0), stop=False, skip_group_check=True)
                pe.wait_ge(lo2_ready, 2 * (U * b + u) + 2)
                for t in range(4):
                    cut = slice(128 * t, 128 * t + 128)
                    for k in range(2):
                        mm = three(py[c][:, t, :], (h2hi[u % 2][:, k, cut], h2lo[u % 2][:, k, cut]),
                                   (whi[:, e, 2, k, :], wlo[:, e, 2, k, :]), False, e == NE - 1 and k == 1)
                mm.then_inc(y_ready, 1)

            hidden1(0, 0, True)

            def body(b, first, last):
                for s in range(U):
                    if s + 1 < U:
                        hidden1(b, s + 1, first)
                    elif not last:
                        hidden1(b + 1, 0, False)
                    hidden2(b, s, first)
                    if s > 0:
                        output(b, s - 1, first)
                    elif not first:
                        output(b - 1, U - 1, False)

            body(0, True, False)
            with pe.Fori(1, B - 1) as b:
                body(b, False, False)
            body(B - 1, False, True)
            output(B - 1, U - 1, False)

        def flat(a):
            return a.rearrange("p k n -> p (k n)")

        @block.scalar
        def _(act):
            def weights_high(e):
                for j in range(3):
                    i = 3 * e + j
                    act.wait_ge(stage_in[i % NS], 16 * (i // NS + 1))
                    nc.scalar.activation(flat(whi[:, e, j]), flat(stage[i % NS][:]), ACT.Copy).then_inc(wsplit_hi, 1)

            for n in range(4):
                act.wait_ge(setup_pe, n + 1)
                nc.scalar.activation(featT[:, n // 2, 512 * (n % 2):512 * (n % 2) + 512], four[n][:], ACT.Copy,
                                     scale=1.0 / B).then_inc(featT_ready, 1)
            act.wait_ge(soft, 2)
            nc.scalar.activation(flat(wt[:]), flat(lg[:]), ACT.Exp).then_inc(exp_ready, 1)
            weights_high(0)
            weights_high(1)
            for n in range(0, 2 * NE, 2):
                act.wait_ge(setup_pe, 7 + n)
                nc.scalar.activation(wbc[:, n // 2, 0:CH], four[n % 4][:], ACT.Copy).then_inc(exp_ready, 1)
                act.wait_ge(exp_ready, n // 2 + 2)
                if n:
                    act.wait_ge(wbc_ready, n)
                act.sem_inc(wbc_ready, 1)
            act.wait_ge(bn_ready, 2)

            def relu(b, u, layer, first):
                e = u % NE
                ready, done, lo_done, p, r = ((h1_ready, r1_ready, lo1_ready, p1, r1),
                                              (h2_ready, r2_ready, lo2_ready, p2, r2))[layer]
                for m in range(2):
                    n = 2 * (U * b + u) + m
                    act.wait_ge(ready, n + 1)
                    if u > 0 or not first:
                        act.wait_ge(lo_done, n - 1)
                    nc.scalar.activation(r[m][:], p[m][:], ACT.Relu, bias=bn[layer][1][:, m, e:e + 1],
                                         scale=rs[layer][:, m, e:e + 1]).then_inc(done, 1)

            def high2(b, u, first):
                for m in range(2):
                    n = 2 * (U * b + u) + m
                    if m == 0 and (u >= 2 or not first):
                        act.wait_ge(y_ready, U * b + u - 1)
                    act.wait_ge(w2_ready, n + 1)
                    nc.scalar.activation(h2hi[u % 2][:, m, :], r2[m][:], ACT.Copy).then_inc(hi2_ready, 1)

            relu(0, 0, 0, True)

            def body(b, first, last):
                for s in range(U):
                    if s > 0:
                        high2(b, s - 1, first)
                    elif not first:
                        high2(b - 1, U - 1, False)
                    if s + 1 < U:
                        relu(b, s + 1, 0, first)
                    elif not last:
                        relu(b + 1, 0, 0, False)
                    relu(b, s, 1, first)
                    if first and s + 2 < NE:
                        weights_high(s + 2)

            body(0, True, False)
            with act.Fori(1, B - 1) as b:
                body(b, False, False)
            body(B - 1, False, True)
            high2(B - 1, U - 1, False)

        @block.vector
        def _(dve):
            def weights_low(e):
                for j in range(3):
                    i = 3 * e + j
                    dve.wait_ge(wsplit_hi, i + 1)
                    nc.vector.tensor_tensor(flat(wlo[:, e, j]), flat(stage[i % NS][:]), flat(whi[:, e, j]).bitcast(F32),
                                            ALU.subtract).then_inc(wsplit, 1)

            def split_x(b, c, first):
                dve.wait_ge(x_in, 16 * (2 * b + c + 1))
                if not first:
                    dve.wait_ge(h1_ready, 2 * (U * b + NE * c - NE))
                nc.vector.tensor_copy(flat(xhi[c][:]), flat(xraw[:])).then_inc(x_split_hi, 1)
                dve.wait_ge(x_split_hi, 2 * b + c + 1)
                nc.vector.tensor_tensor(flat(xlo[c][:]), flat(xraw[:]), flat(xhi[c][:]).bitcast(F32),
                                        ALU.subtract).then_inc(x_split, 1)

            dve.wait_ge(consts, 16 * 15)
            for n in range(2):
                g, bb, be, m, v = (flat(a[:]) for a in bn[n])
                nc.vector.tensor_scalar(v, v, BN_EPS, None, ALU.add).then_inc(bn_eps, 1)
                nc.vector.tensor_tensor(bb, bb, m, ALU.subtract).then_inc(bn_step, 1)
            split_x(0, 0, True)
            for n in range(2):
                g, bb, be, m, v = (flat(a[:]) for a in bn[n])
                dve.wait_ge(bn_rs, n + 1)
                nc.vector.tensor_tensor(flat(rs[n][:]), flat(rs[n][:]), g, ALU.mult).then_inc(bn_step, 1)
                dve.wait_ge(bn_step, 3 + 2 * n)
                nc.vector.tensor_tensor(bb, bb, flat(rs[n][:]), ALU.mult).then_inc(bn_step, 1)
                dve.wait_ge(bn_step, 4 + 2 * n)
                nc.vector.tensor_tensor(bb, bb, be, ALU.add).then_inc(bn_ready, 1)
            dve.wait_ge(setup_pe, 5)
            logits = py[0][:, 0, 0:NT * NE].rearrange("p (t e) -> p t e", e=NE)
            nc.vector.tensor_reduce(nm[:], logits, AX.X, ALU.max, negate=True).then_inc(soft, 1)
            dve.wait_ge(soft, 1)
            nc.vector.tensor_tensor(lg[:], logits, nm[:].unsqueeze(2).to_broadcast([128, NT, NE]), ALU.add).then_inc(soft, 1)
            dve.wait_ge(exp_ready, 1)
            nc.vector.tensor_reduce(sm[:], wt[:], AX.X, ALU.add).then_inc(soft, 1)
            dve.wait_ge(soft, 3)
            nc.vector.reciprocal(rsm[:], sm[:]).then_inc(soft, 1)
            dve.wait_ge(soft, 4)
            nc.vector.tensor_tensor(wt[:], wt[:], rsm[:].unsqueeze(2).to_broadcast([128, NT, NE]), ALU.mult).then_inc(soft, 1)
            dve.wait_ge(setup_pe, 6)
            nc.vector.tensor_copy(wT[:], py[1][0:NE, :, :].rearrange("p a b -> p (a b)")).then_inc(wT_ready, 1)
            weights_low(0)
            weights_low(1)
            for n in range(1, 2 * NE, 2):
                dve.wait_ge(setup_pe, 7 + n)
                dve.wait_ge(wbc_ready, n)
                nc.vector.tensor_copy(wbc[:, n // 2, CH:L], four[n % 4][:]).then_inc(wbc_ready, 1)

            def split1(b, u, first):
                for m in range(2):
                    n = 2 * (U * b + u) + m
                    dve.wait_ge(r1_ready, n + 1)
                    if m == 0 and (u >= 2 or not first):
                        dve.wait_ge(h2_ready, 2 * (U * b + u) - 2)
                    nc.vector.tensor_copy(h1hi[u % 2][:, m, :], r1[m][:]).then_inc(hi1_ready, 1)
                    dve.wait_ge(hi1_ready, n + 1)
                    nc.vector.tensor_tensor(h1lo[u % 2][:, m, :], r1[m][:], h1hi[u % 2][:, m, :].bitcast(F32),
                                            ALU.subtract).then_inc(lo1_ready, 1)

            def weigh(b, u):
                c, e = u // NE, u % NE
                for m in range(2):
                    dve.wait_ge(r2_ready, 2 * (U * b + u) + m + 1)
                    nc.vector.tensor_tensor(r2[m][:], r2[m][:], wbc[:, e, CH * c:CH * c + CH], ALU.mult).then_inc(w2_ready, 1)

            def low2(b, u):
                for m in range(2):
                    dve.wait_ge(hi2_ready, 2 * (U * b + u) + m + 1)
                    nc.vector.tensor_tensor(h2lo[u % 2][:, m, :], r2[m][:], h2hi[u % 2][:, m, :].bitcast(F32),
                                            ALU.subtract).then_inc(lo2_ready, 1)

            def finish(b, c):
                dve.wait_ge(y_ready, U * b + NE * c + NE)
                dve.wait_ge(res_in[c], 16 * (b + 1))
                nc.vector.tensor_tensor(flat(res[c][:]), flat(py[c][:]), flat(res[c][:]), ALU.add).then_inc(y_read, 1)

            split1(0, 0, True)

            def body(b, first, last):
                for s in range(U):
                    if s > 0:
                        low2(b, s - 1)
                    elif not first:
                        low2(b - 1, U - 1)
                    if s + 1 < U:
                        split1(b, s + 1, first)
                    elif not last:
                        split1(b + 1, 0, False)
                    weigh(b, s)
                    if first and s + 2 < NE:
                        weights_low(s + 2)
                    if s == 1 and not first:
                        finish(b - 1, 1)
                    if s == NE + 1:
                        finish(b, 0)
                    if s == 4:
                        split_x(b, 1, first)
                    if s == NE + 4 and not last:
                        split_x(b + 1, 0, False)

            body(0, True, False)
            with dve.Fori(1, B - 1) as b:
                body(b, False, False)
            body(B - 1, False, True)
            low2(B - 1, U - 1)
            finish(B - 1, 1)

        @block.gpsimd
        def _(pool):
            nc.gpsimd.memset(ones[:], 1.0).then_inc(made, 1)
            nc.gpsimd.memset(mhalf[:], -0.5).then_inc(made, 1)
            pool.wait_ge(made, 2)
            for n in range(2):
                pool.wait_ge(bn_eps, n + 1)
                nc.gpsimd.tensor_tensor(flat(rs[n][:]), flat(bn[n][4][:]), flat(mhalf[:]), ALU.pow).then_inc(bn_rs, 1)


def program(nc, I, out):
    B, L, E = I["x"].shape
    x1 = nc.dram_tensor("x1_scratch", (B, L, E), F32, kind="Internal").ap()
    t2 = nc.dram_tensor("t2_scratch", (B, L, E), F32, kind="Internal").ap()
    xn2T = nc.dram_tensor("xn2T_scratch", (B, E, L), F32, kind="Internal").ap()
    feat = nc.dram_tensor("feat_scratch", (128, L // 128, E), F32, kind="Internal").ap()
    layer0(nc, I["x"], I["xT"], I["wqT0"], I["wkT0"], I["wvT0"], I["woT0"], I["ln_g"], I["ln_b"], I["window"],
           I["rowscale"], I["cosT"], I["sinT"], I["avg8"], I["ident"], x1)
    layer1_attention(nc, x1, I["wqT1"], I["wkT1"], I["wv1"], I["ident"], I["causal"], t2, xn2T, feat)
    layer1_experts(nc, t2, xn2T, feat, I["wr"], I["br"], I["w1"], [I[n + "1"] for n in ("g", "b", "be", "m", "v")],
                   I["w2"], [I[n + "2"] for n in ("g", "b", "be", "m", "v")], I["wo"], I["bo"], I["ident"],
                   I["selectors"], out)


def shape_constants(H=8, R=32):
    gamma = 1.0 - 2.0 ** (-2.0 - 5.0 * np.arange(H) / H)
    i = np.arange(R)
    factor = 1 / np.sqrt((gamma[:, None, None] ** np.abs(i[:, None] - i[None, :])).sum(-1))
    r, j2, u = np.arange(128) // R, np.arange(128) % R, np.arange(4 - R, R)
    dist = np.abs(u[None, None, :, None] - r[:, None, None, None]) + np.abs(i[None, None, None, :] - j2[:, None, None, None])
    window = gamma[None, :, None, None] ** dist * factor[None, :, None, :]
    rowscale = np.stack([factor[4 * g + np.arange(128) // 32] for g in range(2)], 1)
    angle = np.repeat(1.0 / 10000.0 ** np.linspace(0.0, 1.0, 16), 2)
    turn = (i[:, None] + i[None, :]).reshape(-1)[None, :] * angle[:, None]
    sine = np.sin(turn)
    sine[0::2] *= -1
    selectors = np.zeros((8, 8, 128))
    selectors[np.arange(8), np.arange(8)] = 1
    tri = np.arange(128)
    out = {
        "window": window.reshape(128, H, -1), "rowscale": rowscale, "cosT": np.tile(np.cos(turn), (4, 1)),
        "sinT": np.tile(sine, (4, 1)), "avg8": np.kron(np.eye(16), np.full((8, 8), 1 / 8)), "ident": np.eye(128),
        "selectors": selectors, "causal": np.where(tri[None, :] > tri[:, None], -3e38, 0.0),
    }
    return {k: np.ascontiguousarray(v, dtype=np.float32) for k, v in out.items()}


def kernel(**inputs):
    import concourse.bacc as bacc
    from concourse.bass_utils import run_bass_kernel_spmd

    a = {k: np.asarray(v) for k, v in inputs.items()}
    B, N1, N2, E = a["x"].shape
    x = a["x"].reshape(B, N1 * N2, E)
    arrays = {"x": x, "xT": x.transpose(0, 2, 1)}
    for n, k in (("wqT0", "Wq"), ("wkT0", "Wk"), ("wvT0", "Wv"), ("woT0", "Wo")):
        arrays[n] = a["L0_conv_" + k].T
    for n in ("g", "b"):
        arrays["ln_" + n] = np.tile(a["L0_conv_ln_" + n], 4)[:, None]
    arrays |= {"wqT1": a["L1_attn_Wq"].T, "wkT1": a["L1_attn_Wk"].T, "wv1": a["L1_attn_Wv"]}
    for n in ("Wr", "W1", "W2", "Wo", "bo"):
        arrays[n.lower()] = a["L1_ffn_" + n]
    arrays["br"] = a["L1_ffn_br"][None]
    for n in ("g", "b", "be", "m", "v"):
        for layer in "12":
            arrays[n + layer] = a["L1_ffn_" + n + layer].T
    arrays |= shape_constants()
    arrays = {"in_" + k: np.ascontiguousarray(v) for k, v in arrays.items()}

    nc = bacc.Bacc("TRN2", target_bir_lowering=False, num_devices=1)
    I = {k[3:]: nc.dram_tensor(k, v.shape, mybir.dt.from_np(v.dtype), kind="ExternalInput").ap() for k, v in arrays.items()}
    out = nc.dram_tensor("out", (B, N1 * N2, E), F32, kind="ExternalOutput").ap()
    program(nc, I, out)
    r = run_bass_kernel_spmd(nc, [arrays], core_ids=[0])
    return r.results[0]["out"].reshape(B, N1, N2, E)
```

```python
from contextlib import ExitStack

import numpy as np

import concourse.bass as bass
from concourse import mybir

ALU = mybir.AluOpType
ACT = mybir.ActivationFunctionType
AX = mybir.AxisListType
F32 = mybir.dt.float32
F32R = mybir.dt.float32r


def layer0(nc, x, xT, wqT, wkT, wvT, woT, lng, lnb, window, rowscale, cosT, sinT, avg8, ident, x1):
    B, L, E = x.shape
    H, HD = 8, E // 8
    QC = 512
    KT = L // 128
    STEPS, PHASES = 4 * KT, 4
    ROWS = L // 32
    CROWS = QC // 32
    LN_EPS, GN_EPS = 1e-5, 1e-5
    SCALING = float(HD) ** -0.5
    STACK = 12 * 16

    A_HEAD = ["gn1", "gn2", "k", "v", "q", "v'", "k'"]
    A_MID = ["q0", "dT3'", "k0", "v0", "q1", "dT0", "k1", "v1", "q2", "dT1", "gn1", "gn2", "k2", "v2",
             "q3", "dT2", "k3", "v3"]
    A_FIRST = [t for t in A_MID if t != "dT3'"]
    A_LAST = [t for t in A_MID if t not in ("gn1", "gn2", "k2", "v2", "q3", "k3", "v3")] + ["dT3'"]
    B_MID = ["nT3'", "o1'", "zT3'", "o2'", "nT0", "o3'", "zT0", "nT1", "zT1", "nT2", "zT2", "o0"]
    B_FIRST = [t for t in B_MID if t[-1] != "'"]
    B_LAST = B_MID + [t for t in B_MID if t[-1] == "'"]

    def order(name, b, first, last, lists, head):
        one, mid, end = lists
        if first:
            return head + one.index(name)
        if last:
            n = len(end) - 1 - end[::-1].index(name) if last == "after" else end.index(name)
            return head + len(one) + len(mid) * (B - 2) + n
        return head + len(one) + len(mid) * (b - 1) + mid.index(name)

    def a_order(name, b, first, last):
        return order(name, b, first, last, (A_FIRST, A_MID, A_LAST), len(A_HEAD))

    def b_order(name, b, first, last):
        return order(name, b, first, last, (B_FIRST, B_MID, B_LAST), 0)

    def prep_order(name, b):
        return 3 + 8 * b + ["q0", "k0", "q1", "k1", "q2", "k2", "q3", "k3"].index(name)

    with ExitStack() as ctx:
        def sb(name, shape, dt=F32):
            return ctx.enter_context(nc.sbuf_tensor("l0_" + name, shape, dt))

        def sem(name):
            return ctx.enter_context(nc.semaphore("l0_" + name))

        win = sb("window", [128, H, (2 * ROWS - 4) * 32])
        rsc = sb("rowscale", [128, 2, ROWS])
        cos_sb, sin_sb = sb("cos", [128, L]), sb("sin", [128, L])
        wq, wk, wv, wo = (sb(n, [128, 2, E]) for n in ("wq", "wk", "wv", "wo"))
        avg, idn = sb("avg8", [128, 128]), sb("ident", [128, 128])
        ones = sb("ones", [128, HD])
        lngb = sb("lngb", [128, 2])
        raw, xn = sb("raw", [128, 2, L]), sb("xn", [128, 2, L])
        t1, t2 = sb("t1", [128, QC]), sb("t2", [128, QC])
        hi, lo = sb("hi", [128, QC], F32R), sb("lo", [128, QC], F32R)
        kst = [sb(f"kst{g}", [128, 4, L], F32R) for g in range(2)]
        qst = [sb(f"qst{c}", [128, 4, QC], F32R) for c in range(2)]
        vsb = [sb(f"v{g}", [128, KT, 128]) for g in range(2)]
        prod = [sb(f"prod{n}", [128, 2, QC]) for n in range(4)]
        absp = [sb(f"absp{n}", [128, 2, QC]) for n in range(4)]
        tA, tB = sb("tA", [128, 4, 128]), sb("tB", [128, 4, 128])
        z = sb("z", [128, 2, L])
        xo = [sb(f"xo{n}", [128, 2, E]) for n in range(2)]
        stats, mv = sb("stats", [128, 2, 2, 6]), sb("mv", [128, 2, 2])
        gmean, dmean, gvar, grstd = (sb(n, [128, 2]) for n in ("gmean", "dmean", "gvar", "grstd"))
        mhalf = sb("mhalf", [128, 16])
        nsum, dent, var, fac, epst = (sb(n, [128, 16]) for n in ("nsum", "den_t", "var", "fac", "eps"))

        def bank(name, shape):
            return ctx.enter_context(nc.psum_tensor("l0_" + name, shape, F32))

        sc = [bank(f"scores{j}", [128, 2, QC]) for j in range(2)]
        num, den = bank("num", [128, QC]), bank("den", [128, QC])
        pA, pB = bank("bankA", [128, QC]), bank("bankB", [128, QC])

        def sems(names):
            return (sem(n) for n in names.split())

        weights_in, tables_in, consts, made, x_in, waited, window_in = sems("weights_in tables_in consts made x_in waited window_in")
        stats_done, agg_done, gmean_ready, gvar_ready = sems("stats_done agg_done gmean_ready gvar_ready")
        geps_ready, grstd_ready, xn_ready = sems("geps_ready grstd_ready xn_ready")
        scores_ready, prod_ready, abs_ready, av_done, den_done = sems("scores_ready prod_ready abs_ready av_done den_done")
        a_ready, b_ready = sems("a_ready b_ready")
        t1_ready, shuffled, rot_ready, sum_ready = sems("t1_ready shuffled rot_ready sum_ready")
        cos_ready = sem("cos_ready")
        hi_ready, lo_ready, q_stacked, v_ready = sems("hi_ready lo_ready q_stacked v_ready")
        n_taken, d_taken, nsum_ready, centred = sems("n_taken d_taken nsum_ready centred")
        sq_ready, den_ready, var_ready, fac_step = sems("sq_ready den_ready var_ready fac_step")
        on_ready, z_ready, o_added = sems("on_ready z_ready o_added")
        k_stacked = [sem(f"k_stacked{c}") for c in range(2)]
        xo_in = [sem(f"xo_in{n}") for n in range(2)]
        xo_out = [sem(f"xo_out{n}") for n in range(2)]

        NWEIGHTS, NTABLES, NCONST = 4, 3, 5
        NMADE = 3

        def nphase(b, p, prev):
            return 4 * b - 1 if prev else 4 * b + p

        block = ctx.enter_context(nc.Block())

        @block.sync
        def _(sp):
            sp.dma_start(raw[:], xT[0].rearrange("(k p) t -> p k t", p=128)).then_inc(x_in, 16)
            for dst, src in ((avg[:], avg8), (wk[:], wkT.rearrange("(k p) n -> p k n", p=128)),
                             (wv[:], wvT.rearrange("(k p) n -> p k n", p=128)),
                             (wq[:], wqT.rearrange("(k p) n -> p k n", p=128))):
                sp.dma_start(dst, src).then_inc(weights_in, 16)
            for dst, src in ((sin_sb[:], sinT), (cos_sb[:], cosT), (rsc[:], rowscale)):
                sp.dma_start(dst, src).then_inc(tables_in, 16)
            for dst, src in ((win[:, 0:H // 2], window[:, 0:H // 2]), (idn[:], ident),
                             (lngb[:, 0:1], lng), (lngb[:, 1:2], lnb),
                             (wo[:], woT.rearrange("(k p) n -> p k n", p=128))):
                sp.dma_start(dst, src).then_inc(consts, 16)

            def stack(n, dst, quads, done):
                sp.wait_ge(hi_ready, n + 1)
                for part, tile, ready in (("hi", hi, None), ("lo", lo, lo_ready)):
                    if ready is not None:
                        sp.wait_ge(ready, n + 1)
                    for quad in range(3):
                        if quads[quad] == part:
                            for h in range(4):
                                sp.dma_start(dst[32 * quad:32 * quad + 32, h, :].bitcast(F32),
                                             tile[32 * h:32 * h + 32, :].bitcast(F32)).then_inc(done, 16)

            QUADS = {"q": ("hi", "hi", "lo"), "k": ("hi", "lo", "hi")}
            stack(0, kst[0][:, :, 0:QC], QUADS["k"], k_stacked[0])
            stack(1, qst[0][:, :, :], QUADS["q"], q_stacked)
            sp.dma_start(win[:, H // 2:H], window[:, H // 2:H]).then_inc(window_in, 16)
            stack(2, kst[0][:, :, QC:L], QUADS["k"], k_stacked[1])

            def load_x(n, bb, t0, count):
                if count is not None:
                    sp.wait_ge(xo_out[n], count)
                sp.dma_start(xo[n][:], x[bb, t0:t0 + 256, :].rearrange("(t p) e -> p t e", p=128)).then_inc(xo_in[n], 16)

            def store_x(n, bb, t0, added):
                sp.wait_ge(o_added, added)
                sp.dma_start(x1[bb, t0:t0 + 256, :].rearrange("(t p) e -> p t e", p=128), xo[n][:]).then_inc(xo_out[n], 16)

            def body(b, first, last):
                if not last:
                    sp.wait_ge(xn_ready, 2 * b + 2)
                    sp.dma_start(raw[:], xT[b + 1].rearrange("(k p) t -> p k t", p=128)).then_inc(x_in, 16)
                if not first:
                    store_x(0, b - 1, 0, 4 * b - 3)
                    load_x(0, b - 1, QC, 16 * (2 * b - 1))
                stack(prep_order("q0", b), qst[1][:, :, :], QUADS["q"], q_stacked)
                if not first:
                    store_x(1, b - 1, 256, 4 * b - 2)
                    load_x(1, b - 1, QC + 256, 16 * (2 * b - 1))
                stack(prep_order("k0", b), kst[1][:, :, 0:QC], QUADS["k"], k_stacked[0])
                if not first:
                    store_x(0, b - 1, QC, 4 * b - 1)
                stack(prep_order("q1", b), qst[0][:, :, :], QUADS["q"], q_stacked)
                if not first:
                    store_x(1, b - 1, QC + 256, 4 * b)
                stack(prep_order("k1", b), kst[1][:, :, QC:L], QUADS["k"], k_stacked[1])
                stack(prep_order("q2", b), qst[1][:, :, :], QUADS["q"], q_stacked)
                if not last:
                    stack(prep_order("k2", b), kst[0][:, :, 0:QC], QUADS["k"], k_stacked[0])
                for n in range(2):
                    load_x(n, b, 256 * n, None if first else 32 * b)
                if not last:
                    stack(prep_order("q3", b), qst[0][:, :, :], QUADS["q"], q_stacked)
                    stack(prep_order("k3", b), kst[0][:, :, QC:L], QUADS["k"], k_stacked[1])

            body(0, True, False)
            with sp.Fori(1, B - 1) as b:
                body(b, False, False)
            body(B - 1, False, True)
            for n in range(2):
                store_x(n, B - 1, 256 * n, 4 * B - 3 + n)
                load_x(n, B - 1, QC + 256 * n, 16 * (2 * B - 1))
            for n in range(2):
                store_x(n, B - 1, QC + 256 * n, 4 * B - 1 + n)
            for n in range(2):
                sp.wait_ge(xo_out[n], 32 * B)

        @block.tensor
        def _(pe):
            pe.wait_ge(weights_in, 16 * NWEIGHTS)
            pe.wait_ge(made, NMADE)

            def a_free(name, b, first, last):
                tasks = A_FIRST if first else (A_LAST if last else A_MID)
                k = len(tasks) - 1 if last == "after" else tasks.index(name)
                before = tasks[k - 1] if k > 0 else "v3'"
                if first and k == 0:
                    pe.wait_ge(t1_ready, 3)
                elif before[0] in "qk":
                    pe.wait_ge(t1_ready, prep_order(before, b) + 1)
                elif before == "v3'":
                    pe.wait_ge(v_ready, 4 * b + 2)
                elif before[0] == "v":
                    pe.wait_ge(v_ready, 4 * b + 3 + int(before[1]))
                elif before == "gn1":
                    pe.wait_ge(gmean_ready, 3 * b + 4)
                elif before == "gn2":
                    pe.wait_ge(geps_ready, b + 2)
                else:
                    pe.wait_ge(den_ready, 4 * b if before == "dT3'" else 4 * b + int(before[2]) + 1)

            def b_free(name, b, first, last):
                tasks = B_FIRST if first else (B_LAST if last else B_MID)
                k = len(tasks) - 1 - tasks[::-1].index(name) if last == "after" else tasks.index(name)
                if first and k == 0:
                    return
                before = tasks[k - 1] if k > 0 else "o0'"
                if k > len(B_MID):
                    b = b + 1
                if before[0] == "o":
                    pe.wait_ge(o_added, {"o0'": 4 * b - 3, "o1'": 4 * b - 2, "o2'": 4 * b - 1, "o3'": 4 * b,
                                         "o0": 4 * b + 1}[before])
                else:
                    taken = centred if before[0] == "n" else z_ready
                    pe.wait_ge(taken, 4 * b if before[2:] == "3'" else 4 * b + int(before[2]) + 1)

            def project(w, g, c, part=None):
                for k in range(2) if part is None else (part,):
                    mm = nc.tensor.matmul(pA[:], w[:, k, 128 * g:128 * g + 128], xn[:, k, QC * c:QC * c + QC],
                                          start=(k == 0), stop=(k == 1))
                if part != 0:
                    mm.then_inc(a_ready, 1)

            def project_v(g, half, part=None):
                for t in range(4) if part is None else range(2 * part, 2 * part + 2):
                    tok = QC * half + 128 * t
                    for k in range(2):
                        mm = nc.tensor.matmul(pA[:, 128 * t:128 * t + 128], xn[:, k, tok:tok + 128],
                                              wv[:, k, 128 * g:128 * g + 128], start=(k == 0), stop=(k == 1))
                if part != 0:
                    mm.then_inc(a_ready, 1)

            def group_sums(rhs, sem_, count):
                pe.wait_ge(sem_, count)
                nc.tensor.matmul(pA[:, 0:2], avg[:], rhs, start=True, stop=True).then_inc(a_ready, 1)

            def transpose_n(phase):
                pe.wait_ge(n_taken, phase + 1)
                for t in range(4):
                    mm = nc.tensor.transpose(pB[:, 128 * t:128 * t + 128], tA[:, t, :], idn[:])
                mm.then_inc(b_ready, 1)

            def transpose_d(phase):
                pe.wait_ge(d_taken, phase + 1)
                for t in range(4):
                    mm = nc.tensor.transpose(pA[:, 128 * t:128 * t + 128], tB[:, t, :], idn[:])
                mm.then_inc(a_ready, 1)

            def transpose_z(phase):
                pe.wait_ge(on_ready, phase + 1)
                for t in range(4):
                    mm = nc.tensor.transpose(pB[:, 128 * t:128 * t + 128], tA[:, t, :], idn[:])
                mm.then_inc(b_ready, 1)

            def out_proj(c, half, phases, part=None):
                if part != 1:
                    pe.wait_ge(z_ready, phases)
                for t in range(2) if part is None else (part,):
                    tok = QC * c + 256 * half + 128 * t
                    for g in range(2):
                        mm = nc.tensor.matmul(pB[:, 256 * t:256 * t + 256], z[:, g, tok:tok + 128], wo[:, g, :],
                                              start=(g == 0), stop=(g == 1))
                if part != 0:
                    mm.then_inc(b_ready, 1)

            def scores(b, i, j):
                p, kt = i // KT, i % KT
                g, c = p // 2, p % 2
                if kt == 0 and j == 0:
                    pe.wait_ge(q_stacked, STACK * (4 * b + p + 1))
                if c == 0 and kt % 4 == 0 and j == 0:
                    pe.wait_ge(k_stacked[kt // 4], STACK * (2 * b + g + 1))
                n = 2 * i + j
                if n >= 2 or not isinstance(b, int) or b > 0:
                    pe.wait_ge(prod_ready, 2 * STEPS * b + n - 1)
                for s in range(2):
                    h = 2 * j + s
                    mm = nc.tensor.matmul(sc[j][:, s, :], kst[g][0:96, h, 128 * kt:128 * kt + 128], qst[c][0:96, h, :],
                                          start=True, stop=True)
                mm.then_inc(scores_ready, 1)

            def weighted(b, i, first):
                p, kt = i // KT, i % KT
                g = p // 2
                if p % 2 == 0 and kt % 4 == 0:
                    pe.wait_ge(v_ready, 4 * b + 2 * g + kt // 4 + 1)
                if kt == 0 and not (first and p == 0):
                    pe.wait_ge(n_taken, 4 * b + p)
                pe.wait_ge(prod_ready, 2 * STEPS * b + 2 * i + 2)
                for h in range(4):
                    mm = nc.tensor.matmul(num[32 * h:32 * h + 32, :], vsb[g][:, kt, 32 * h:32 * h + 32],
                                          prod[2 * (i % 2) + h // 2][:, h % 2, :], start=(kt == 0), stop=(kt == KT - 1))
                mm.then_inc(av_done, 1)

            def sums(b, i, first):
                p, kt = i // KT, i % KT
                if kt == 0 and not (first and p == 0):
                    pe.wait_ge(d_taken, 4 * b + p)
                pe.wait_ge(abs_ready, 2 * STEPS * b + 2 * i + 2)
                for h in range(4):
                    mm = nc.tensor.matmul(den[32 * h:32 * h + 32, :], ones[:],
                                          absp[2 * (i % 2) + h // 2][:, h % 2, :], start=(kt == 0), stop=(kt == KT - 1))
                mm.then_inc(den_done, 1)

            group_sums(mv[:, :, 0], agg_done, 1)
            group_sums(gvar[:], gvar_ready, 1)
            pe.wait_ge(xn_ready, 2)
            project(wk, 0, 0)
            pe.wait_ge(t1_ready, 1)
            project_v(0, 0)
            pe.wait_ge(v_ready, 1)
            project(wq, 0, 0)
            pe.wait_ge(t1_ready, 2)
            project_v(0, 1)
            pe.wait_ge(v_ready, 2)
            project(wk, 0, 1)
            scores(0, 0, 0)
            scores(0, 0, 1)
            pe.wait_ge(consts, 16 * NCONST)

            def body(b, first, last):
                def A(name, task, *args):
                    if task not in (project, project_v) or args[-1] != 1:
                        a_free(name, b, first, last)
                    task(*args)

                def Bk(name, task, *args):
                    if task is not out_proj or args[-1] != 1:
                        b_free(name, b, first, last)
                    task(*args)

                for i in range(STEPS):
                    p, kt = i // KT, i % KT
                    prev = p == 0
                    post = not (prev and first)
                    tag = "3'" if prev else str(p - 1)
                    ph = nphase(b, p - 1, prev)
                    g, c = ((p + 1) // 2 % 2, (p + 1) % 2)
                    prep_q, prep_kv = p < 3 or not last, p < 2 or not last
                    nb, ni = (b, i + 1) if i + 1 < STEPS else (b + 1, 0)
                    more = i + 1 < STEPS or not last
                    if more:
                        scores(nb, ni, 0)
                    if i > 0:
                        sums(b, i - 1, first)
                    elif not first:
                        sums(b - 1, STEPS - 1, False)
                    if kt == 0 and prep_q:
                        A(f"q{p}", project, wq, g, c, 0)
                    if kt == 1 and post:
                        Bk("nT" + tag, transpose_n, ph)
                    if p != 2 and kt == 3 and prep_kv:
                        A(f"k{p}", project, wk, (1 - p // 2), p % 2, 0)
                    if p == 2 and kt == 6 and prep_kv:
                        pe.wait_ge(xn_ready, 2 * b + 4)
                        A(f"k{p}", project, wk, (1 - p // 2), p % 2, 1)
                    if kt == 6 and post:
                        Bk("zT" + tag, transpose_z, ph)
                    if kt == 7 and p == 3:
                        Bk("o0", out_proj, 0, 0, 4 * b + 3, 0)
                    if kt == 7 and prev and not first:
                        Bk("o2'", out_proj, 1, 0, 4 * b, 0)
                    if kt == 4 and p == 0 and not first:
                        Bk("o1'", out_proj, 0, 1, 4 * b - 1, 0)
                    if kt == 4 and p == 1 and not first:
                        Bk("o3'", out_proj, 1, 1, 4 * b, 0)
                    if kt == (7 if p == 2 else 6) and prep_kv:
                        A(f"v{p}", project_v, (1 - p // 2), p % 2, 0)
                    if more:
                        scores(nb, ni, 1)
                    weighted(b, i, first)
                    if kt == 0 and prep_q:
                        A(f"q{p}", project, wq, g, c, 1)
                    if kt == 1 and post:
                        A("dT" + tag, transpose_d, ph)
                    if p == 2 and kt == 2 and not last:
                        A("gn1", group_sums, mv[:, :, 0], agg_done, b + 2)
                    if p == 2 and kt == 3 and not last:
                        A("gn2", group_sums, gvar[:], gvar_ready, b + 2)
                    if p != 2 and kt == 3 and prep_kv:
                        A(f"k{p}", project, wk, (1 - p // 2), p % 2, 1)
                    if p == 2 and kt == 5 and prep_kv:
                        pe.wait_ge(xn_ready, 2 * b + 3)
                        A(f"k{p}", project, wk, (1 - p // 2), p % 2, 0)
                    if kt == (7 if p == 2 else 6) and prep_kv:
                        A(f"v{p}", project_v, (1 - p // 2), p % 2, 1)
                    if kt == 7 and p == 3:
                        Bk("o0", out_proj, 0, 0, 4 * b + 3, 1)
                    if kt == 7 and prev and not first:
                        Bk("o2'", out_proj, 1, 0, 4 * b, 1)
                    if kt == 4 and p == 0 and not first:
                        Bk("o1'", out_proj, 0, 1, 4 * b - 1, 1)
                    if kt == 4 and p == 1 and not first:
                        Bk("o3'", out_proj, 1, 1, 4 * b, 1)

            body(0, True, False)
            with pe.Fori(1, B - 1) as b:
                body(b, False, False)
            body(B - 1, False, True)
            sums(B - 1, STEPS - 1, False)
            b_free("nT3'", B - 1, False, "after")
            transpose_n(4 * B - 1)
            a_free("dT3'", B - 1, False, "after")
            transpose_d(4 * B - 1)
            b_free("o1'", B - 1, False, "after")
            out_proj(0, 1, 4 * B - 1)
            b_free("zT3'", B - 1, False, "after")
            transpose_z(4 * B - 1)
            b_free("o2'", B - 1, False, "after")
            out_proj(1, 0, 4 * B)
            b_free("o3'", B - 1, False, "after")
            out_proj(1, 1, 4 * B)

        @block.vector
        def _(dve):

            def q_rotate_in(n, a, g, c):
                if not isinstance(n, int) or n > 0:
                    dve.wait_ge(lo_ready, n)
                dve.wait_ge(a_ready, a + 1)
                nc.vector.tensor_tensor(t1[:].rearrange("p (a b) -> p a b", b=32), pA[:].rearrange("p (a b) -> p a b", b=32),
                                        rsc[:, g, CROWS * c:CROWS * c + CROWS].unsqueeze(2).to_broadcast([128, CROWS, 32]),
                                        ALU.mult).then_inc(t1_ready, 1)

            def shuffle(n):
                dve.wait_ge(t1_ready, n + 1)
                dve.sem_inc(waited, 1)
                nc.vector.stream_shuffle(t2[:], t1[:], [i ^ 1 for i in range(32)]).then_inc(shuffled, 1)

            def rotate_sin(n, c):
                dve.wait_ge(shuffled, n + 1)
                nc.vector.tensor_tensor(t2[:], t2[:], sin_sb[:, QC * c:QC * c + QC], ALU.mult).then_inc(rot_ready, 1)

            def products(b, i, j, first):
                p, kt = i // KT, i % KT
                g, c = p // 2, p % 2
                w0 = 32 * (CROWS * c - 4 * kt + ROWS - 4)
                n = 2 * i + j
                dve.wait_ge(scores_ready, 2 * STEPS * b + n + 1)
                if not (first and i < 2):
                    dve.wait_ge(av_done, STEPS * b + i - 1)
                    dve.wait_ge(abs_ready, 2 * STEPS * b + n - 3)
                nc.vector.tensor_tensor(prod[n % 4][:], sc[j][:], win[:, 4 * g + 2 * j:4 * g + 2 * j + 2, w0:w0 + QC],
                                        ALU.mult).then_inc(prod_ready, 1)

            nT = pB[:].rearrange("p (m d) -> p m d", d=32)

            def head_sums(n):
                dve.wait_ge(b_ready, n + 1)
                nc.vector.tensor_reduce(nsum[:], nT, AX.X, ALU.add).then_inc(nsum_ready, 1)

            def centre(phase):
                dve.wait_ge(nsum_ready, phase + 1)
                nc.vector.scalar_tensor_tensor(tA[:].rearrange("p t (h d) -> p (t h) d", d=32),
                                               nsum[:].unsqueeze(2).to_broadcast([128, 16, 32]), -1.0 / HD, nT,
                                               ALU.mult, ALU.add).then_inc(centred, 1)

            nT_A = pA[:].rearrange("p (m d) -> p m d", d=32)

            def take_den(a):
                dve.wait_ge(a_ready, a + 1)
                nc.vector.tensor_scalar(dent[:], nT_A[:, :, 0], 1.0, 50000.0, ALU.max, ALU.min).then_inc(den_ready, 1)

            def variance(phase):
                dve.wait_ge(sq_ready, phase + 1)
                nc.vector.tensor_reduce(var[:], tB[:].rearrange("p t (h d) -> p (t h) d", d=32), AX.X,
                                        ALU.add).then_inc(var_ready, 1)

            def statistics(b, quarters):
                if 0 in quarters:
                    dve.wait_ge(x_in, 16 * (b + 1))
                for n in quarters:
                    k, s = n // 2, n % 2
                    nc.vector.bn_stats(stats[:, k, s, :], raw[:, k, 512 * s:512 * s + 512]).then_inc(stats_done, 1)

            def aggregate(b):
                dve.wait_ge(stats_done, 4 * (b + 1))
                dve.sem_inc(waited, 1)
                for k in range(2):
                    ins = nc.vector.bn_aggr(mv[:, k, :], stats[:, k, :, :].rearrange("p s f -> p (s f)"))
                ins.then_inc(agg_done, 1)

            def group_mean(b, a):
                dve.wait_ge(a_ready, a + 1)
                nc.vector.tensor_copy(gmean[:], pA[:, 0:2]).then_inc(gmean_ready, 1)
                dve.wait_ge(gmean_ready, 3 * b + 1)
                nc.vector.tensor_tensor(dmean[:], mv[:, :, 0], gmean[:], ALU.subtract).then_inc(gmean_ready, 1)
                dve.wait_ge(gmean_ready, 3 * b + 2)
                nc.vector.tensor_tensor(dmean[:], dmean[:], dmean[:], ALU.mult).then_inc(gmean_ready, 1)
                dve.wait_ge(gmean_ready, 3 * b + 3)
                nc.vector.tensor_tensor(gvar[:], mv[:, :, 1], dmean[:], ALU.add).then_inc(gvar_ready, 1)

            def group_var(b, a):
                dve.wait_ge(a_ready, a + 1)
                nc.vector.tensor_scalar(dmean[:], pA[:, 0:2], GN_EPS, None, ALU.add).then_inc(geps_ready, 1)

            def normalise(b, parts):
                if 0 in parts:
                    dve.wait_ge(grstd_ready, b + 1)
                for k in parts:
                    nc.vector.tensor_scalar(xn[:, k, :], raw[:, k, :], gmean[:, k:k + 1], grstd[:, k:k + 1],
                                            ALU.subtract, ALU.mult).then_inc(xn_ready, 1)

            def add_residual(bn, n, k, count):
                dve.wait_ge(b_ready, bn + 1)
                dve.wait_ge(xo_in[n], count)
                nc.vector.tensor_tensor(xo[n][:].rearrange("p t e -> p (t e)"), pB[:], xo[n][:].rearrange("p t e -> p (t e)"),
                                        ALU.add).then_inc(o_added, 1)


            statistics(0, range(4))
            aggregate(0)
            group_mean(0, 0)
            group_var(0, 1)
            normalise(0, (0, 1))
            dve.wait_ge(tables_in, 16 * NTABLES)
            for n in range(3):
                if n == 1:
                    q_rotate_in(1, 4, 0, 0)
                shuffle(n)
                rotate_sin(n, n // 2)
            dve.wait_ge(consts, 16 * NCONST)

            def body(b, first, last):
                A = lambda name: a_order(name, b, first, last)
                Bn = lambda name: b_order(name, b, first, last)
                for i in range(STEPS):
                    p, kt = i // KT, i % KT
                    prev = p == 0
                    post = not (prev and first)
                    tag = "3'" if prev else str(p - 1)
                    ph = nphase(b, p - 1, prev)
                    g, c = ((p + 1) // 2 % 2, (p + 1) % 2)
                    prep_q, prep_k = p < 3 or not last, p < 2 or not last
                    nq, nk = prep_order(f"q{p}", b), prep_order(f"k{p}", b)
                    if first and i == 2 * KT:
                        dve.wait_ge(window_in, 16)
                    products(b, i, 0, first)
                    if kt == 2 and prep_q:
                        shuffle(nq)
                    if kt == 3 and post:
                        take_den(A("dT" + tag))
                        head_sums(Bn("nT" + tag))
                    if kt == (7 if p == 2 else 6) and prep_k:
                        shuffle(nk)
                    if not last:
                        if p == 1 and kt == 5:
                            statistics(b + 1, (1,))
                        if p == 1 and kt == 7:
                            statistics(b + 1, (3,))
                        if p == 2 and kt == 4:
                            group_var(b + 1, A("gn2"))
                        if p == 2 and kt == 5:
                            normalise(b + 1, (0,))
                    products(b, i, 1, first)
                    if kt == 5 and p == 1 and not first:
                        add_residual(Bn("o3'"), 1, 4 * b, 16 * 2 * b)
                    if kt == 5 and p == 0 and not first:
                        add_residual(Bn("o1'"), 1, 4 * b - 2, 16 * (2 * b - 1))
                    if kt == 1 and prep_q:
                        q_rotate_in(nq, A(f"q{p}"), g, c)
                    if kt == 2 and prep_q:
                        rotate_sin(nq, (p + 1) % 2)
                    if kt == 3 and post:
                        centre(ph)
                    if kt == 4 and post:
                        variance(ph)
                    if kt == (7 if p == 2 else 6) and prep_k:
                        rotate_sin(nk, p % 2)
                    if not last:
                        if p == 1 and kt == 4:
                            statistics(b + 1, (0,))
                        if p == 1 and kt == 5:
                            statistics(b + 1, (2,))
                        if p == 1 and kt == 7:
                            aggregate(b + 1)
                        if p == 2 and kt == 3:
                            group_mean(b + 1, A("gn1"))
                        if p == 2 and kt == 5:
                            normalise(b + 1, (1,))
                    if kt == 0 and p == 0 and not first:
                        add_residual(Bn("nT3'") - 1, 0, 4 * b - 3, 16 * (2 * b - 1))
                    if kt == 0 and p == 1 and not first:
                        add_residual(Bn("o2'"), 0, 4 * b - 1, 32 * b)

            body(0, True, False)
            with dve.Fori(1, B - 1) as b:
                body(b, False, False)
            body(B - 1, False, True)
            Bn = lambda name: b_order(name, B - 1, False, "after")
            add_residual(Bn("nT3'") - 1, 0, 4 * B - 3, 16 * (2 * B - 1))
            head_sums(Bn("nT3'"))
            centre(4 * B - 1)
            take_den(a_order("dT3'", B - 1, False, "after"))
            variance(4 * B - 1)
            add_residual(Bn("o1'"), 1, 4 * B - 2, 16 * (2 * B - 1))
            add_residual(Bn("o2'"), 0, 4 * B - 1, 32 * B)
            add_residual(Bn("o3'"), 1, 4 * B, 32 * B)

        @block.scalar
        def _(act):

            def k_take(n, a):
                if not isinstance(n, int) or n > 0:
                    act.wait_ge(lo_ready, n)
                act.wait_ge(a_ready, a + 1)
                nc.scalar.activation(t1[:], pA[:], ACT.Copy, scale=SCALING).then_inc(t1_ready, 1)

            def high(n, before, count):
                if before is not None:
                    act.wait_ge(before, count)
                act.wait_ge(sum_ready, n + 1)
                nc.scalar.activation(hi[:], t1[:], ACT.Copy).then_inc(hi_ready, 1)

            def v_take(a, g, half, n):
                act.wait_ge(a_ready, a + 1)
                nc.scalar.activation(vsb[g][:, 4 * half:4 * half + 4, :].rearrange("p t c -> p (t c)"), pA[:],
                                     ACT.Copy).then_inc(v_ready, 1)

            def absolutes(b, i, first):
                for j in range(2):
                    n = 2 * i + j
                    act.wait_ge(prod_ready, 2 * STEPS * b + n + 1)
                    if not (first and i < 2):
                        act.wait_ge(den_done, STEPS * b + i - 1)
                    nc.scalar.activation(absp[n % 4][:], prod[n % 4][:], ACT.Abs).then_inc(abs_ready, 1)

            def take_num(phase):
                act.wait_ge(av_done, KT * (phase + 1))
                nc.scalar.activation(tA[:].rearrange("p t c -> p (t c)"), num[:], ACT.Copy).then_inc(n_taken, 1)

            def take_den(phase):
                act.wait_ge(den_done, KT * (phase + 1))
                nc.scalar.activation(tB[:].rearrange("p t c -> p (t c)"), den[:], ACT.Copy).then_inc(d_taken, 1)

            def squares(a, phase):
                act.wait_ge(a_ready, a + 1)
                act.wait_ge(centred, phase + 1)
                nc.scalar.activation(tB[:], tA[:], ACT.Square, scale=HD ** -0.5).then_inc(sq_ready, 1)

            def gelu(n, phase, g, c):
                act.wait_ge(b_ready, n + 1)
                nc.scalar.activation(z[:, g, QC * c:QC * c + QC], pB[:], ACT.Gelu, bias=lngb[:, 1:2],
                                     scale=lngb[:, 0:1]).then_inc(z_ready, 1)

            def before(name, b):
                if name[0] == "q":
                    p = int(name[1])
                    return k_stacked[(p + 1) % 2], STACK * (2 * b + [1, 2, 2, 3][p])
                return q_stacked, STACK * (4 * b + int(name[1]) + 2)

            k_take(0, 2)
            v_take(3, 0, 0, 1)
            high(0, None, 0)
            v_take(5, 0, 1, 2)
            high(1, k_stacked[0], STACK)
            k_take(2, 6)
            high(2, q_stacked, STACK)
            act.wait_ge(consts, 16 * NCONST)

            def body(b, first, last):
                A = lambda name: a_order(name, b, first, last)
                Bn = lambda name: b_order(name, b, first, last)
                for i in range(STEPS):
                    p, kt = i // KT, i % KT
                    prev = p == 0
                    post = not (prev and first)
                    tag = "3'" if prev else str(p - 1)
                    ph = nphase(b, p - 1, prev)
                    if kt == 0 and post:
                        take_num(ph)
                    absolutes(b, i, first)
                    if kt == 0 and post:
                        take_den(ph)
                    if kt == 3 and post:
                        squares(A("dT" + tag), ph)
                    if kt == 3 and (p < 3 or not last):
                        high(prep_order(f"q{p}", b), *before(f"q{p}", b))
                    if (p < 2 or not last):
                        if kt == (6 if p == 2 else 5):
                            k_take(prep_order(f"k{p}", b), A(f"k{p}"))
                        if kt == 7:
                            if p != 2:
                                high(prep_order(f"k{p}", b), *before(f"k{p}", b))
                            v_take(A(f"v{p}"), 1 - p // 2, p % 2, 4 * b + 3 + p)
                    if p == 3 and kt == 0 and not last:
                        high(prep_order("k2", b), *before("k2", b))
                    if kt == 6 and post:
                        g, c = (1, 1) if prev else ((p - 1) // 2, (p - 1) % 2)
                        gelu(Bn("zT" + tag), ph, g, c)

            body(0, True, False)
            with act.Fori(1, B - 1) as b:
                body(b, False, False)
            body(B - 1, False, True)
            take_num(4 * B - 1)
            take_den(4 * B - 1)
            squares(a_order("dT3'", B - 1, False, "after"), 4 * B - 1)
            gelu(b_order("zT3'", B - 1, False, "after"), 4 * B - 1, 1, 1)

        @block.gpsimd
        def _(pool):
            nc.gpsimd.memset(ones[:], 1.0).then_inc(made, 1)
            nc.gpsimd.memset(mhalf[:], -0.5).then_inc(made, 1)
            nc.gpsimd.memset(epst[:], LN_EPS).then_inc(made, 1)
            pool.wait_ge(made, NMADE)

            def rotate_cos(n, c):
                pool.wait_ge(shuffled, n + 1)
                nc.gpsimd.tensor_tensor(t1[:], t1[:], cos_sb[:, QC * c:QC * c + QC], ALU.mult).then_inc(cos_ready, 1)

            def split(n):
                pool.wait_ge(cos_ready, n + 1)
                pool.wait_ge(rot_ready, n + 1)
                nc.gpsimd.tensor_tensor(t1[:], t1[:], t2[:], ALU.add).then_inc(sum_ready, 1)

            def low(n, before, count):
                if before is not None:
                    pool.wait_ge(before, count)
                pool.wait_ge(hi_ready, n + 1)
                nc.gpsimd.tensor_tensor(lo[:], t1[:], hi[:].bitcast(F32), ALU.subtract).then_inc(lo_ready, 1)

            def before(name, b):
                if name[0] == "q":
                    p = int(name[1])
                    return k_stacked[(p + 1) % 2], STACK * (2 * b + [1, 2, 2, 3][p])
                return q_stacked, STACK * (4 * b + int(name[1]) + 2)

            def group_rstd(b):
                pool.wait_ge(geps_ready, b + 1)
                nc.gpsimd.tensor_tensor(grstd[:], dmean[:], mhalf[:, 0:2], ALU.pow).then_inc(grstd_ready, 1)

            def scale_heads(phase):
                pool.wait_ge(den_ready, phase + 1)
                nc.gpsimd.tensor_tensor(fac[:], dent[:], dent[:], ALU.mult).then_inc(fac_step, 1)
                pool.wait_ge(fac_step, 4 * phase + 1)
                nc.gpsimd.tensor_tensor(fac[:], fac[:], epst[:], ALU.mult).then_inc(fac_step, 1)
                pool.wait_ge(fac_step, 4 * phase + 2)
                pool.wait_ge(var_ready, phase + 1)
                nc.gpsimd.tensor_tensor(fac[:], fac[:], var[:], ALU.add).then_inc(fac_step, 1)
                pool.wait_ge(fac_step, 4 * phase + 3)
                nc.gpsimd.tensor_tensor(fac[:], fac[:], mhalf[:], ALU.pow).then_inc(fac_step, 1)
                pool.wait_ge(fac_step, 4 * phase + 4)
                tv = tA[:].rearrange("p t (h d) -> p (t h) d", d=32)
                nc.gpsimd.tensor_tensor(tv, tv, fac[:].unsqueeze(2).to_broadcast([128, 16, 32]),
                                        ALU.mult).then_inc(on_ready, 1)

            group_rstd(0)
            pool.wait_ge(tables_in, 16 * NTABLES)
            rotate_cos(0, 0)
            split(0)
            low(0, None, 0)
            rotate_cos(1, 0)
            split(1)
            low(1, k_stacked[0], STACK)
            rotate_cos(2, 1)
            split(2)
            low(2, q_stacked, STACK)

            def body(b, first, last):
                for p in range(PHASES):
                    ph = nphase(b, p - 1, p == 0)
                    if p == 3 and not last:
                        low(prep_order("k2", b), *before("k2", b))
                    if p < 3 or not last:
                        rotate_cos(prep_order(f"q{p}", b), (p + 1) % 2)
                        split(prep_order(f"q{p}", b))
                        low(prep_order(f"q{p}", b), *before(f"q{p}", b))
                    if p == 2 and not last:
                        group_rstd(b + 1)
                    if not (first and p == 0):
                        scale_heads(ph)
                    if p < 2 or not last:
                        rotate_cos(prep_order(f"k{p}", b), p % 2)
                        split(prep_order(f"k{p}", b))
                        if p != 2:
                            low(prep_order(f"k{p}", b), *before(f"k{p}", b))

            body(0, True, False)
            with pool.Fori(1, B - 1) as b:
                body(b, False, False)
            body(B - 1, False, True)
            scale_heads(4 * B - 1)


def layer1_attention(nc, x1, wqT, wkT, wv, ident, causal, t2, xn2T, feat):
    B, L, E = x1.shape
    NT = L // 128
    LN_EPS = 1e-5
    SCALE = float(E) ** -0.5

    ORDER = [4, 5, 6, 7, 3, 2, 1, 0]
    assert sorted(ORDER) == list(range(NT))

    T_TASKS = ["T00", "T10", "T01", "T11"]
    QV_TASKS = ["Q00", "Q10", "V0", "V1", "Q01", "Q11", "V2", "V3"]
    X_TASKS = [f"X{k}{h}" for k in range(2) for h in range(2)]
    P_TASKS = [f"P{i}{h}" for i in range(NT) for h in range(ORDER[i] // 4 + 1)]
    LISTS = {"first": QV_TASKS + P_TASKS + T_TASKS, "mid": QV_TASKS + X_TASKS + P_TASKS + T_TASKS,
             "last": QV_TASKS + X_TASKS + P_TASKS}
    HEAD = ["A0", "A1"] + T_TASKS

    def place(name):
        if name[0] == "A":
            return 4 + int(name[1])
        if name[0] == "T":
            return T_TASKS.index(name)
        if name in QV_TASKS:
            return [4, 5, 0, 1, 2, 3, 4, 5][QV_TASKS.index(name)]
        return 4 + (X_TASKS if name[0] == "X" else P_TASKS).index(name) % 2

    def before(name, b, first, last, counts):
        of = lambda names: sum(1 for t in names if counts(t))
        one, mid = of(LISTS["first"]), of(LISTS["mid"])
        if name == "end":
            return of(HEAD) + one + mid * (B - 2) + of(LISTS["last"])
        if name in HEAD and isinstance(b, str):
            return of(HEAD[:HEAD.index(name)])
        tasks = LISTS["first" if first else "mid"]
        here = of(tasks[:tasks.index(name)])
        return of(HEAD) + here if first else of(HEAD) + one + mid * (b - 1) + here

    def number(name, b, first):
        return before(name, b, first, False, lambda t: True)

    def earlier(name, b, first):
        return before(name, b, first, False, lambda t: place(t) == place(name))

    def split_number(name, b, first):
        return before(name, b, first, False, lambda t: t[0] != "X")

    with ExitStack() as ctx:
        def sb(name, shape, dt=F32):
            return ctx.enter_context(nc.sbuf_tensor("l1_" + name, shape, dt))

        def sem(name):
            return ctx.enter_context(nc.semaphore("l1_" + name))

        idn, mask = sb("ident", [128, 128]), sb("causal", [128, 128])
        wq_in, wk_in, wv_in = (sb(n, [128, 2, E]) for n in ("wq_in", "wk_in", "wv_in"))
        ahi, alo, vhw, vlw = (sb(n, [128, 2, E], F32R) for n in ("ahi", "alo", "wvhi", "wvlo"))
        xa, xr = sb("xa", [128, NT, E]), sb("xr", [128, NT, E])
        xn, xn2 = sb("xn", [128, NT, E]), sb("xn2", [128, NT, E])
        t2s = sb("t2s", [128, NT, E])
        xt2 = sb("xt2", [128, 2, L])
        xhi, xlo, qhi, qlo = (sb(n, [128, 2, L], F32R) for n in ("xhi", "xlo", "qhi", "qlo"))
        vhi, vlo = (sb(n, [128, NT, E], F32R) for n in ("vhi", "vlo"))
        prob = [sb(f"prob{n}", [128, L]) for n in range(2)]
        phi = [sb(f"phi{n}", [128, NT, 128], F32R) for n in range(2)]
        plo = [sb(f"plo{n}", [128, NT, 128], F32R) for n in range(2)]
        st1, st2 = sb("st1", [128, NT, 6]), sb("st2", [128, NT, 6])
        mv1, mv2 = sb("mv1", [128, NT, 2]), sb("mv2", [128, NT, 2])
        eps1, eps2, rstd1, rstd2, mhalf = (sb(n, [128, NT]) for n in ("eps1", "eps2", "rstd1", "rstd2", "mhalf"))
        shift1, shift2, minus = (sb(n, [128, NT]) for n in ("shift1", "shift2", "minus"))
        nmax, rsum, rinv = sb("nmax", [128, NT]), sb("rsum", [128, NT]), sb("rinv", [128, NT])

        def bank(name, shape):
            return ctx.enter_context(nc.psum_tensor("l1_" + name, shape, F32))

        sc = [bank(f"scores{n}", [128, L]) for n in range(2)]
        av = [bank(f"av{n}", [128, 512]) for n in range(2)]
        ring = [sc[n // 2][:, 512 * (n % 2):512 * (n % 2) + 512] for n in range(4)] + [bank(f"ring{n}", [128, 512])[:]
                                                                                     for n in range(2)]

        consts, wqk_in, xa_in, xr_in, made = (sem(n) for n in ("consts", "wqk_in", "xa_in", "xr_in", "made"))
        xa_head = [sem(f"xa_head{h}") for h in range(2)]
        waited = sem("waited")
        ring_ready, hi_ready = sem("ring_ready"), sem("hi_ready")
        ring_read = [sem(f"ring_read{n}") for n in range(6)]
        wv_hi, wv_split = sem("wv_hi"), sem("wv_split")
        stats1, agg1, eps1_ready, rstd1_ready, xn_ready = (sem(n) for n in ("stats1", "agg1", "eps1_ready", "rstd1_ready",
                                                                            "xn_ready"))
        stats2, agg2, eps2_ready, rstd2_ready, xn2_ready = (sem(n) for n in ("stats2", "agg2", "eps2_ready", "rstd2_ready",
                                                                             "xn2_ready"))
        feat_added, xn_high, xn2_high = sem("feat_added"), sem("xn_high"), sem("xn2_high")
        scores_ready, masked, max_ready, prob_ready = (sem(n) for n in ("scores_ready", "masked", "max_ready", "prob_ready"))
        av_ready, rinv_ready, out_ready = sem("av_ready"), sem("rinv_ready"), sem("out_ready")
        xt2_out, t2_out = sem("xt2_out"), sem("t2_out")
        NCONST = 3

        block = ctx.enter_context(nc.Block())

        @block.sync
        def _(sp):
            tiles = lambda a: a.rearrange("(t p) e -> p t e", p=128)
            sp.sem_inc(xt2_out, 16)
            for h in range(2):
                half = slice(NT // 2 * h, NT // 2 * (h + 1))
                sp.dma_start(xa[:, half, :], tiles(x1[0])[:, half, :]).then_inc(xa_head[h], 16)
                dst, src = ((wq_in, wqT), (wk_in, wkT))[h]
                sp.dma_start(dst[:], src.rearrange("(k p) n -> p k n", p=128)).then_inc(wqk_in, 16)
            for dst, src in ((wv_in[:], wv.rearrange("(k p) n -> p k n", p=128)),
                             (idn[:], ident), (mask[:], causal)):
                sp.dma_start(dst, src).then_inc(consts, 16)

            def body(b, first, last):
                if not first:
                    sp.wait_ge(out_ready, NT * b)
                    sp.dma_start(tiles(t2[b - 1]), t2s[:]).then_inc(t2_out, 16)
                sp.dma_start(xr[:], tiles(x1[b])).then_inc(xr_in, 16)
                if not last:
                    sp.wait_ge(xn_ready, b + 1)
                    if first:
                        sp.wait_ge(xn_high, NT // 2)
                    sp.dma_start(xa[:], tiles(x1[b + 1])).then_inc(xa_in, 16)
                if not first:
                    for name in X_TASKS[2:]:
                        sp.wait_ge(ring_read[place(name)], earlier(name, b, first) + 1)
                    sp.dma_start(xn2T[b - 1].rearrange("(k p) t -> p k t", p=128), xt2[:]).then_inc(xt2_out, 16)

            body(0, True, False)
            with sp.Fori(1, B - 1) as b:
                body(b, False, False)
            body(B - 1, False, True)
            sp.wait_ge(out_ready, NT * B)
            sp.dma_start(tiles(t2[B - 1]), t2s[:]).then_inc(t2_out, 16)
            for k in range(2):
                for n in (4, 5):
                    sp.wait_ge(ring_read[n], before("end", 0, False, False, lambda t: place(t) == n) + k + 1)
                sp.dma_start(xn2T[B - 1, 128 * k:128 * k + 128, :], xt2[:, k, :]).then_inc(xt2_out, 16)
            sp.wait_ge(t2_out, 16 * B)
            sp.wait_ge(xt2_out, 16 * (B + 2))

        @block.tensor
        def _(pe):
            def three(out, a, b, start, stop):
                nc.tensor.matmul(out, a[0], b[0], start=start, stop=False)
                nc.tensor.matmul(out, a[0], b[1], start=False, stop=False)
                return nc.tensor.matmul(out, a[1], b[0], start=False, stop=stop)

            def whole(names, b, first):
                latest = {place(name): name for name in names}
                for n, name in latest.items():
                    pe.wait_ge(ring_read[n], earlier(name, b, first) + 1)

            def begin(name, b, first):
                n = place(name)
                if not (isinstance(b, str) and n < 4):
                    pe.wait_ge(ring_read[n], earlier(name, b, first))
                return ring[n]

            pe.wait_ge(wqk_in, 16 * 2)
            for i in range(2):
                for k in range(2):
                    mm = nc.tensor.matmul(ring[4 + i][:, 0:E], wq_in[:, k, 128 * i:128 * i + 128], wk_in[:, k, :],
                                          start=(k == 0), stop=(k == 1))
                mm.then_inc(ring_ready, 1)

            def xn_transposes(b, first, count):
                pe.wait_ge(xn_ready, count)
                for name in T_TASKS:
                    bk, k, h = begin(name, b, first), int(name[1]), int(name[2])
                    if isinstance(b, str) and h == 1:
                        pe.wait_ge(xn_high, NT // 2)
                    for t in range(4):
                        mm = nc.tensor.transpose(bk[:, 128 * t:128 * t + 128], xn[:, 4 * h + t, 128 * k:128 * k + 128],
                                                 idn[:])
                    mm.then_inc(ring_ready, 1)

            def xn2_transposes(count, befores, end=False):
                for n, before_ in befores:
                    if n == 0:
                        pe.wait_ge(xn2_ready, count)
                    if n == 1 and end:
                        pe.wait_ge(xn2_high, NT // 2)
                    bk = 4 + n % 2
                    pe.wait_ge(ring_read[bk], before_)
                    for t in range(4):
                        mm = nc.tensor.transpose(ring[bk][:, 128 * t:128 * t + 128],
                                                 xn2[:, 4 * (n % 2) + t, 128 * (n // 2):128 * (n // 2) + 128], idn[:])
                    mm.then_inc(ring_ready, 1)

            def xn_whole(b, first, h):
                for k in range(2):
                    name = f"T{k}{h}"
                    after = {"T00": "V0", "T10": "V1", "T01": "Q01", "T11": "Q11"}[name]
                    assert place(after) == place(name)
                    pe.wait_ge(ring_read[place(name)], earlier(after, b, first))

            def body(b, first, last):
                if first:
                    pe.wait_ge(ring_read[4], 1)
                    pe.wait_ge(ring_read[5], 1)
                for name in QV_TASKS:
                    if name in ("Q00", "Q01"):
                        xn_whole(b, first, int(name[2]))
                    if first and name == "V0":
                        pe.wait_ge(wv_split, 2)
                    bk = begin(name, b, first)
                    if name[0] == "Q":
                        j, h = int(name[1]), int(name[2])
                        tok = slice(512 * h, 512 * h + 512)
                        for k in range(2):
                            mm = three(bk, (ahi[:, k, 128 * j:128 * j + 128], alo[:, k, 128 * j:128 * j + 128]),
                                       (xhi[:, k, tok], xlo[:, k, tok]), k == 0, k == 1)
                    else:
                        n = int(name[1])
                        for t in range(2):
                            tok = slice(256 * n + 128 * t, 256 * n + 128 * t + 128)
                            for k in range(2):
                                mm = three(bk[:, E * t:E * t + E], (xhi[:, k, tok], xlo[:, k, tok]),
                                           (vhw[:, k, :], vlw[:, k, :]), k == 0, k == 1)
                    mm.then_inc(ring_ready, 1)
                whole(QV_TASKS[2:6], b, first)
                for i in range(NT + 2):
                    if i < NT:
                        t = ORDER[i]
                        if i >= 2:
                            pe.wait_ge(prob_ready, NT * b + i - 1)
                        for c0 in range(0, 128 * (t + 1), 512):
                            c1 = min(c0 + 512, 128 * (t + 1))
                            for k in range(2):
                                tok = slice(128 * t, 128 * t + 128)
                                mm = three(sc[i % 2][:, c0:c1], (qhi[:, k, tok], qlo[:, k, tok]),
                                           (xhi[:, k, c0:c1], xlo[:, k, c0:c1]), k == 0, k == 1)
                        mm.then_inc(scores_ready, 1)
                    if i < 2 and not first:
                        xn2_transposes(b, [(n, earlier(X_TASKS[n], b, first)) for n in (2 * i, 2 * i + 1)])
                    if 1 <= i <= NT:
                        q = ORDER[i - 1]
                        pe.wait_ge(prob_ready, NT * b + i)
                        for h in range(q // 4 + 1):
                            bk = begin(f"P{i - 1}{h}", b, first)
                            for kb in range(4 * h, min(4 * h + 4, q + 1)):
                                mm = nc.tensor.transpose(bk[:, 128 * (kb % 4):128 * (kb % 4) + 128],
                                                         prob[(i - 1) % 2][:, 128 * kb:128 * kb + 128], idn[:])
                            mm.then_inc(ring_ready, 1)
                    if i == NT and not last:
                        xn_transposes(b, first, b + 2)
                    if i >= 2:
                        q, n = ORDER[i - 2], i % 2
                        whole([f"P{i - 2}{h}" for h in range(q // 4 + 1)], b, first)
                        if i >= 4 or not first:
                            pe.wait_ge(out_ready, NT * b + i - 3)
                        for kb in range(q + 1):
                            mm = three(av[n][:, 0:E], (phi[n][:, kb, :], plo[n][:, kb, :]),
                                       (vhi[:, kb, :], vlo[:, kb, :]), kb == 0, kb == q)
                        mm.then_inc(av_ready, 1)

            pe.wait_ge(consts, 16 * NCONST)
            xn_transposes("head", False, 1)
            body(0, True, False)
            with pe.Fori(1, B - 1) as b:
                body(b, False, False)
            body(B - 1, False, True)
            e = [before("end", 0, False, False, lambda t: place(t) == 4 + n) for n in range(2)]
            xn2_transposes(B, [(n, e[n % 2] + n // 2) for n in range(4)], True)

        def parts(name):
            if name[0] in "TQ":
                k, h = int(name[1]), int(name[2])
                hi, lo = (xhi, xlo) if name[0] == "T" else (qhi, qlo)
                return hi[:, k, 512 * h:512 * h + 512], lo[:, k, 512 * h:512 * h + 512], 512
            if name[0] == "V":
                n = int(name[1])
                flat = lambda a: a[:, 2 * n:2 * n + 2, :].rearrange("p t e -> p (t e)")
                return flat(vhi), flat(vlo), 512
            i, h = int(name[1]), int(name[2])
            kb = min(4 * h + 4, ORDER[i] + 1)
            flat = lambda a: a[:, 4 * h:kb, :].rearrange("p t e -> p (t e)")
            return flat(phi[i % 2]), flat(plo[i % 2]), 128 * (kb - 4 * h)

        @block.scalar
        def _(act):
            def ln1_apply(b, tiles, head=False):
                if 0 in tiles:
                    act.wait_ge(rstd1_ready, 3 * (b + 1))
                for t in tiles:
                    ins = nc.scalar.activation(xn[:, t, :], xa[:, t, :], ACT.Identity, bias=shift1[:, t:t + 1],
                                               scale=rstd1[:, t:t + 1])
                if NT - 1 in tiles or head:
                    ins.then_inc(xn_ready, 1)

            def ln2_apply(b, tiles, end=False):
                if 0 in tiles:
                    act.wait_ge(rstd2_ready, 3 * b)
                    act.wait_ge(feat_added, b)
                for t in tiles:
                    ins = nc.scalar.activation(xn2[:, t, :], t2s[:, t, :], ACT.Identity, bias=shift2[:, t:t + 1],
                                               scale=rstd2[:, t:t + 1])
                if NT - 1 in tiles or end:
                    ins.then_inc(xn2_ready, 1)

            act.wait_ge(consts, 16 * NCONST)
            nc.scalar.activation(vhw[:], wv_in[:], ACT.Copy).then_inc(wv_hi, 1)
            for i in range(2):
                act.wait_ge(ring_ready, i + 1)
                nc.scalar.activation(ahi[:, i, :], ring[4 + i][:, 0:E], ACT.Copy, scale=SCALE).then_inc(hi_ready, 1)
            ln1_apply(0, range(NT // 2), True)

            def high(name, b, first):
                hi, lo, w = parts(name)
                if name[0] == "P" and (int(name[1]) >= 2 or not first):
                    act.wait_ge(av_ready, NT * b + int(name[1]) - 1)
                act.wait_ge(ring_ready, number(name, b, first) + 1)
                nc.scalar.activation(hi, ring[place(name)][:, 0:w], ACT.Copy).then_inc(hi_ready, 1)

            def take_x(n, num, b, count):
                k, h = n // 2, n % 2
                bk = 4 + n % 2
                if n == 0:
                    act.wait_ge(xt2_out, count)
                act.wait_ge(ring_ready, num + 1)
                nc.scalar.activation(xt2[:, k, 512 * h:512 * h + 512], ring[bk], ACT.Copy).then_inc(ring_read[bk], 1)

            def body(b, first, last):
                for n, name in enumerate(QV_TASKS):
                    high(name, b, first)
                    if not first and 4 <= n <= 7:
                        ln2_apply(b, (2 * n - 8, 2 * n - 7))
                for i in range(NT + 1):
                    if i < 2 and not first:
                        for n in (2 * i, 2 * i + 1):
                            take_x(n, number(X_TASKS[n], b, first), b, 16 * b)
                    if i >= 1:
                        for h in range(ORDER[i - 1] // 4 + 1):
                            high(f"P{i - 1}{h}", b, first)
                    if i < NT:
                        t = ORDER[i]
                        act.wait_ge(max_ready, NT * b + i + 1)
                        nc.scalar.activation(prob[i % 2][:, 0:128 * (t + 1)], sc[i % 2][:, 0:128 * (t + 1)], ACT.Exp,
                                             bias=nmax[:, t:t + 1], accum_out=rsum[:, t:t + 1]).then_inc(prob_ready, 1)
                    if not last and 4 <= i <= 6:
                        ln1_apply(b + 1, {4: range(0, 3), 5: range(3, 6), 6: range(6, NT)}[i])
                if not last:
                    for name in T_TASKS:
                        high(name, b, first)

            for name in T_TASKS:
                high(name, "head", False)
            body(0, True, False)
            with act.Fori(1, B - 1) as b:
                body(b, False, False)
            body(B - 1, False, True)
            ln2_apply(B, range(NT // 2), True)
            for n in range(4):
                take_x(n, number("end", 0, False) + n, B, 16 * B)

        @block.vector
        def _(dve):

            def ln1_stats(b, t):
                if isinstance(b, str):
                    if t % (NT // 2) == 0:
                        dve.wait_ge(xa_head[t // (NT // 2)], 16)
                elif t == 0:
                    dve.wait_ge(xa_in, 16 * b)
                nc.vector.bn_stats(st1[:, t, :], xa[:, t, :]).then_inc(stats1, 1)

            def ln1_eps(b):
                dve.wait_ge(stats1, NT * (b + 1))
                dve.sem_inc(waited, 1)
                for t in range(NT):
                    nc.vector.bn_aggr(mv1[:, t, :], st1[:, t, :]).then_inc(agg1, 1)
                dve.wait_ge(agg1, NT * (b + 1))
                nc.vector.tensor_scalar(eps1[:], mv1[:, :, 1], LN_EPS, None, ALU.add).then_inc(eps1_ready, 1)

            def ln2_eps(b):
                dve.wait_ge(stats2, NT * b)
                dve.sem_inc(waited, 1)
                for t in range(NT):
                    nc.vector.bn_aggr(mv2[:, t, :], st2[:, t, :]).then_inc(agg2, 1)
                dve.wait_ge(agg2, NT * b)
                nc.vector.tensor_scalar(eps2[:], mv2[:, :, 1], LN_EPS, None, ALU.add).then_inc(eps2_ready, 1)

            def low(name, b, first):
                hi, lo, w = parts(name)
                bk = place(name)
                dve.wait_ge(hi_ready, split_number(name, b, first) + 1)
                nc.vector.tensor_tensor(lo, ring[bk][:, 0:w], hi.bitcast(F32), ALU.subtract).then_inc(ring_read[bk], 1)

            for t in range(NT):
                ln1_stats("head", t)
            ln1_eps(0)
            dve.wait_ge(consts, 16 * NCONST)
            for i in range(2):
                dve.wait_ge(hi_ready, i + 1)
                nc.vector.scalar_tensor_tensor(out=alo[:, i, :], in0=ring[4 + i][:, 0:E], scalar=SCALE,
                                               in1=ahi[:, i, :].bitcast(F32), op0=ALU.mult,
                                               op1=ALU.subtract).then_inc(ring_read[4 + i], 1)
            dve.wait_ge(wv_hi, 1)
            nc.vector.tensor_tensor(vlw[:], wv_in[:], vhw[:].bitcast(F32), ALU.subtract).then_inc(wv_split, 2)
            dve.wait_ge(rstd1_ready, 3)
            for t in range(NT // 2, NT):
                nc.vector.tensor_scalar(xn[:, t, :], xa[:, t, :], rstd1[:, t:t + 1], shift1[:, t:t + 1], ALU.mult,
                                        ALU.add).then_inc(xn_high, 1)
            for name in T_TASKS:
                low(name, "head", False)

            def output(b, i, last):
                q = ORDER[i]
                if i == 0:
                    dve.wait_ge(xr_in, 16 * (b + 1))
                    if not isinstance(b, int) or b > 0:
                        dve.wait_ge(t2_out, 16 * b)
                nc.vector.reciprocal(rinv[:, q:q + 1], rsum[:, q:q + 1]).then_inc(rinv_ready, 1)
                dve.wait_ge(rinv_ready, NT * b + i + 1)
                dve.wait_ge(av_ready, NT * b + i + 1)
                nc.vector.scalar_tensor_tensor(out=t2s[:, q, :], in0=av[i % 2][:, 0:E], scalar=rinv[:, q:q + 1],
                                               in1=xr[:, q, :], op0=ALU.mult, op1=ALU.add).then_inc(out_ready, 1)

            def body(b, first, last):
                for name in QV_TASKS:
                    low(name, b, first)
                    if name == "Q00" and not first:
                        ln2_eps(b)
                for i in range(NT + 2):
                    if i < NT:
                        t = ORDER[i]
                        w = 128 * (t + 1)
                        dve.wait_ge(scores_ready, NT * b + i + 1)
                        nc.vector.tensor_tensor(sc[i % 2][:, w - 128:w], sc[i % 2][:, w - 128:w], mask[:],
                                                ALU.add).then_inc(masked, 1)
                        dve.wait_ge(masked, NT * b + i + 1)
                        nc.vector.tensor_reduce(nmax[:, t:t + 1], sc[i % 2][:, 0:w], AX.X, ALU.max,
                                                negate=True).then_inc(max_ready, 1)
                    if 1 <= i <= NT:
                        for h in range(ORDER[i - 1] // 4 + 1):
                            if (i >= 3 or not first) and h == 0:
                                dve.wait_ge(av_ready, NT * b + i - 2)
                            low(f"P{i - 1}{h}", b, first)
                    if i == NT and not last:
                        for name in T_TASKS:
                            low(name, b, first)
                    if i >= 2:
                        output(b, i - 2, last)
                    if not last and i < 3:
                        for t in range(3 * i, min(3 * i + 3, NT)):
                            ln1_stats(b + 1, t)
                    if not last and i == 3:
                        ln1_eps(b + 1)
                    if i >= 2:
                        q = ORDER[i - 2]
                        dve.wait_ge(out_ready, NT * b + i - 1)
                        nc.vector.bn_stats(st2[:, q, :], t2s[:, q, :]).then_inc(stats2, 1)

            body(0, True, False)
            with dve.Fori(1, B - 1) as b:
                body(b, False, False)
            body(B - 1, False, True)
            ln2_eps(B)
            dve.wait_ge(rstd2_ready, 3 * B)
            dve.wait_ge(feat_added, B)
            for t in range(NT // 2, NT):
                nc.vector.tensor_scalar(xn2[:, t, :], t2s[:, t, :], rstd2[:, t:t + 1], shift2[:, t:t + 1], ALU.mult,
                                        ALU.add).then_inc(xn2_high, 1)
            dve.wait_ge(xn2_high, NT // 2)
            nc.vector.tensor_tensor(feat[:, NT // 2:, :], feat[:, NT // 2:, :], xn2[:, NT // 2:, :], ALU.add).then_inc(feat_added, 1)
            dve.wait_ge(xn2_ready, B)
            nc.vector.tensor_tensor(feat[:, 0:NT // 2, :], feat[:, 0:NT // 2, :], xn2[:, 0:NT // 2, :], ALU.add).then_inc(feat_added, 1)

        @block.gpsimd
        def _(pool):
            nc.gpsimd.memset(mhalf[:], -0.5).then_inc(made, 1)
            nc.gpsimd.memset(minus[:], -1.0).then_inc(made, 1)
            nc.gpsimd.memset(feat[:], 0.0).then_inc(feat_added, 1)
            pool.wait_ge(made, 2)

            def rstd(ready, eps, out, done, count, mv, shift):
                pool.wait_ge(ready, count)
                nc.gpsimd.tensor_tensor(out[:], eps[:], mhalf[:], ALU.pow).then_inc(done, 1)
                pool.wait_ge(done, 3 * count - 2)
                nc.gpsimd.tensor_tensor(shift[:], mv[:, :, 0], out[:], ALU.mult).then_inc(done, 1)
                pool.wait_ge(done, 3 * count - 1)
                nc.gpsimd.tensor_tensor(shift[:], shift[:], minus[:], ALU.mult).then_inc(done, 1)

            def ln1(b):
                rstd(eps1_ready, eps1, rstd1, rstd1_ready, b + 1, mv1, shift1)

            def ln2(b, end=False):
                rstd(eps2_ready, eps2, rstd2, rstd2_ready, b, mv2, shift2)
                if end:
                    return
                pool.wait_ge(xn2_ready, b)
                pool.wait_ge(feat_added, b)
                nc.gpsimd.tensor_tensor(feat[:], feat[:], xn2[:], ALU.add).then_inc(feat_added, 1)

            def body(b, first, last):
                if not first:
                    ln2(b)
                if not last:
                    ln1(b + 1)

            ln1(0)
            body(0, True, False)
            with pool.Fori(1, B - 1) as b:
                body(b, False, False)
            body(B - 1, False, True)
            ln2(B, True)


def layer1_experts(nc, t2, xn2T, feat, wr, br, w1, w2, wo, bo, bn, ident, routerD, out):
    B, L, D = t2.shape
    NE = w1.shape[0]
    NT = L // 128
    CH = 512
    U = 2 * NE
    BN_EPS = 1e-3
    NS = 4
    NW = 3 * NE

    with ExitStack() as ctx:
        def sb(name, shape, dt=F32):
            return ctx.enter_context(nc.sbuf_tensor("e_" + name, shape, dt))

        def sem(name):
            return ctx.enter_context(nc.semaphore("e_" + name))

        whi, wlo = sb("whi", [128, NE, 3, 2, D], F32R), sb("wlo", [128, NE, 3, 2, D], F32R)
        xhi = [sb(f"xhi{c}", [128, 2, CH], F32R) for c in range(2)]
        xlo = [sb(f"xlo{c}", [128, 2, CH], F32R) for c in range(2)]
        wbc_rows = sb("wbc", [128, NE - 2, L])
        feat_rows = feat[:].rearrange("p t e -> p (t e)").rearrange("p (a l) -> p a l", l=L)
        wbc = [wbc_rows[:, e, :] if e < NE - 2 else feat_rows[:, e - NE + 2, :] for e in range(NE)]
        featT = wbc_rows[:, NE - 4:NE - 2, :]
        r1 = [sb(f"r1{m}", [128, CH]) for m in range(2)]
        r2 = [sb(f"r2{m}", [128, CH]) for m in range(2)]
        h1hi, h1lo, h2hi, h2lo = ([sb(f"{n}{c}", [128, 2, CH], F32R) for c in range(2)]
                                  for n in ("h1hi", "h1lo", "h2hi", "h2lo"))
        res = [sb(f"res{c}", [128, 4, D]) for c in range(2)]
        bias = [sb(f"bias{c}", [128, 4, D]) for c in range(2)]
        wT = bias[1][0:NE, :, :].rearrange("p t e -> p (t e)")
        stage = [res[n // 2][:, 2 * (n % 2):2 * (n % 2) + 2, :] for n in range(NS)]
        xraw = sb("xraw", [128, 2, CH])
        idn = sb("ident", [128, 128])
        wr_sb, br_sb, bo_sb = sb("wr", [128, 2, NE]), sb("br", [NE, 1]), sb("bo", [NE, D])
        bn_sb = sb("bn", [128, 10, 2, NE])
        bn_ = [[bn_sb[:, 5 * n + q] for q in range(5)] for n in range(2)]
        mhalf, rs = sb("mhalf", [128, 2, NE]), [sb(f"rs{n}", [128, 2, NE]) for n in range(2)]
        nm, sm, rsm = sb("nm", [128, NT]), sb("sm", [128, NT]), sb("rsm", [128, NT])
        lg, wt = sb("lg", [128, NT, NE]), sb("wt", [128, NT, NE])

        def bank(name, shape):
            return ctx.enter_context(nc.psum_tensor("e_" + name, shape, F32))

        p1 = [bank(f"h1_{m}", [128, CH]) for m in range(2)]
        p2 = [bank(f"h2_{m}", [128, CH]) for m in range(2)]
        py = [bank(f"y_{c}", [128, 4, D]) for c in range(2)]
        four = [p1[0], p1[1], p2[0], p2[1]]
        logitsT = py[0][0:NE, :, :].rearrange("p a b -> p (a b)").rearrange("p (h n) -> p h n", n=CH)
        logits = py[1][:, 0, 0:NT * NE].rearrange("p (t e) -> p t e", e=NE)
        wT_psum = logitsT

        consts, router_in, made, waited = sem("consts"), sem("router_in"), sem("made"), sem("waited")
        x_in = sem("x_in")
        stage_in = [sem(f"stage_in{n}") for n in range(NS)]
        wsplit_hi, wsplit = sem("wsplit_hi"), sem("wsplit")
        x_split_hi, x_split = sem("x_split_hi"), sem("x_split")
        bn_step, bn_eps, bn_rs, bn_ready = sem("bn_step"), sem("bn_eps"), sem("bn_rs"), sem("bn_ready")
        featT_made, featT_ready, logitsT_made, logitsT_ready = (sem(n) for n in ("featT_made", "featT_ready", "logitsT_made",
                                                                                 "logitsT_ready"))
        logits_made, soft, exp_ready, wT_made, wT_ready = (sem(n) for n in ("logits_made", "soft", "exp_ready", "wT_made",
                                                                           "wT_ready"))
        wT_out, bias_made, bias_ready = sem("wT_out"), sem("bias_made"), sem("bias_ready")
        wbc_in = [sem(f"wbc_in{e}") for e in range(NE)]
        h1_ready, r1_ready, hi1_ready, lo1_ready = sem("h1_ready"), sem("r1_ready"), sem("hi1_ready"), sem("lo1_ready")
        h2_ready, r2_ready, w2_ready = sem("h2_ready"), sem("r2_ready"), sem("w2_ready")
        hi2_ready, lo2_ready, y_ready, y_read = sem("hi2_ready"), sem("lo2_ready"), sem("y_ready"), sem("y_read")
        res_in = [sem(f"res_in{c}") for c in range(2)]
        res_out = [sem(f"res_out{c}") for c in range(2)]
        biased = [sem(f"biased{c}") for c in range(2)]

        block = ctx.enter_context(nc.Block())

        @block.sync
        def _(sp):
            cols = lambda a: a.rearrange("(k p) n -> p k n", p=128)

            def rows(a, b, c):
                return a[b, CH * c:CH * c + CH, :].rearrange("(t p) e -> p t e", p=128)

            def load_x(b, c):
                sp.dma_start(xraw[:], cols(xn2T[b])[:, :, CH * c:CH * c + CH]).then_inc(x_in, 16)

            def load_weights(i):
                if i >= NS:
                    sp.wait_ge(wsplit, i - NS + 1)
                sp.dma_start(stage[i % NS], cols((w1, w2, wo)[i % 3][i // 3])).then_inc(stage_in[i % NS], 16)

            for dst, src in ((idn[:], ident), (wr_sb[:], cols(wr)), (br_sb[:], br)):
                sp.dma_start(dst, src).then_inc(router_in, 16)
            load_x(0, 0)
            for i in range(NS):
                load_weights(i)
            sp.dma_start(bn_sb[:], bn).then_inc(consts, 16)
            sp.dma_start(bo_sb[:], bo).then_inc(consts, 16)
            load_weights(4)
            load_weights(5)
            sp.wait_ge(wT_ready, 1)
            sp.dma_start(routerD, wT).then_inc(wT_out, 16)
            for i in range(6, 9):
                load_weights(i)
            sp.wait_ge(wT_out, 16)
            sp.wait_ge(logitsT_made, 1)
            for e in range(NE):
                sp.dma_start(wbc[e], routerD[e:e + 1, :].to_broadcast([128, L])).then_inc(wbc_in[e], 16)
                for i in range(9 + 2 * e, min(11 + 2 * e, NW)):
                    load_weights(i)
                if e == 2:
                    sp.wait_ge(x_split, 1)
                    load_x(0, 1)
            for c in range(2):
                sp.wait_ge(wsplit, NW - 2 * (1 - c))
                sp.dma_start(res[c][:], rows(t2, 0, c)).then_inc(res_in[c], 16)

            def body(b, first, last):
                if not first:
                    sp.wait_ge(y_read, 2 * b)
                    sp.dma_start(rows(out, b - 1, 1), res[1][:]).then_inc(res_out[1], 16)
                    sp.wait_ge(res_out[1], 16 * b)
                    sp.sem_inc(waited, 1)
                    sp.dma_start(res[1][:], rows(t2, b, 1)).then_inc(res_in[1], 16)
                if not last:
                    sp.wait_ge(x_split, 2 * b + 2)
                    sp.sem_inc(waited, 1)
                    load_x(b + 1, 0)
                sp.wait_ge(y_read, 2 * b + 1)
                sp.sem_inc(waited, 1)
                sp.dma_start(rows(out, b, 0), res[0][:]).then_inc(res_out[0], 16)
                if not last:
                    sp.wait_ge(res_out[0], 16 * (b + 1))
                    sp.sem_inc(waited, 1)
                    sp.dma_start(res[0][:], rows(t2, b + 1, 0)).then_inc(res_in[0], 16)
                    sp.wait_ge(x_split, 2 * b + 3)
                    sp.sem_inc(waited, 1)
                    load_x(b + 1, 1)

            body(0, True, False)
            with sp.Fori(1, B - 1) as b:
                body(b, False, False)
            body(B - 1, False, True)
            sp.wait_ge(y_read, 2 * B)
            sp.dma_start(rows(out, B - 1, 1), res[1][:]).then_inc(res_out[1], 16)
            for c in range(2):
                sp.wait_ge(res_out[c], 16 * B)

        @block.tensor
        def _(pe):
            def three(o, a, b, start, stop):
                nc.tensor.matmul(o, a[0], b[0], start=start, stop=False, skip_group_check=True)
                nc.tensor.matmul(o, a[0], b[1], start=False, stop=False, skip_group_check=True)
                return nc.tensor.matmul(o, a[1], b[0], start=False, stop=stop, skip_group_check=True)

            def router_logits():
                pe.wait_ge(router_in, 16 * 3)
                for k in range(2):
                    for h in range(2):
                        for t in range(4):
                            mm = nc.tensor.transpose(four[2 * k + h][:, 128 * t:128 * t + 128],
                                                     feat[:, 4 * h + t, 128 * k:128 * k + 128], idn[:])
                        mm.then_inc(featT_made, 1)
                pe.wait_ge(featT_ready, 4)
                for h in range(2):
                    for k in range(2):
                        mm = nc.tensor.matmul(logitsT[:, h, :], wr_sb[:, k, :], featT[:, k, CH * h:CH * h + CH],
                                              start=(k == 0), stop=(k == 1))
                mm.then_inc(logitsT_made, 1)

            def router_turn():
                pe.wait_ge(logitsT_ready, 1)
                for t in range(NT):
                    mm = nc.tensor.transpose(logits[:, t, :], wT[:, 128 * t:128 * t + 128], idn[0:NE, 0:NE])
                mm.then_inc(logits_made, 1)

            def router_weights():
                pe.wait_ge(soft, 5)
                for t in range(NT):
                    mm = nc.tensor.transpose(wT_psum[:, t // 4, 128 * (t % 4):128 * (t % 4) + 128], wt[:, t, :], idn[:])
                mm.then_inc(wT_made, 1)

            def output_biases():
                pe.wait_ge(consts, 16 * 2)
                pe.wait_ge(wT_ready, 1)
                for t in range(NT):
                    mm = nc.tensor.matmul(py[t // 4][:, t % 4, :], wT[:, 128 * t:128 * t + 128], bo_sb[:],
                                          start=True, stop=True)
                    if t % 4 == 3:
                        mm.then_inc(bias_made, 1)

            def hidden1(b, u, first):
                c, e = u // NE, u % NE
                if e == 0:
                    pe.wait_ge(x_split, 2 * b + c + 1)
                if first:
                    if c == 0:
                        pe.wait_ge(wsplit, 3 * e + 1)
                for m in range(2):
                    if u > 0 or not first:
                        pe.wait_ge(r1_ready, 2 * (U * b + u) + m - 1)
                    for k in range(2):
                        cut = slice(128 * m, 128 * m + 128)
                        mm = three(p1[m][:], (whi[:, e, 0, k, cut], wlo[:, e, 0, k, cut]),
                                   (xhi[c][:, k, :], xlo[c][:, k, :]), k == 0, k == 1)
                    mm.then_inc(h1_ready, 1)

            def hidden2(b, u, first):
                c, e = u // NE, u % NE
                if first and c == 0:
                    pe.wait_ge(wsplit, 3 * e + 2)
                pe.wait_ge(lo1_ready, 2 * (U * b + u) + 2)
                for m in range(2):
                    if u > 0 or not first:
                        pe.wait_ge(r2_ready, 2 * (U * b + u) + m - 1)
                    for k in range(2):
                        cut = slice(128 * m, 128 * m + 128)
                        mm = three(p2[m][:], (whi[:, e, 1, k, cut], wlo[:, e, 1, k, cut]),
                                   (h1hi[u % 2][:, k, :], h1lo[u % 2][:, k, :]), k == 0, k == 1)
                    mm.then_inc(h2_ready, 1)

            def output(b, u, first):
                c, e = u // NE, u % NE
                if e == 0:
                    if first:
                        if c == 0:
                            pe.wait_ge(bias_ready, 2)
                    else:
                        pe.wait_ge(y_read, 2 * b + c - 1)
                if first and c == 0:
                    pe.wait_ge(wsplit, 3 * e + 3)
                pe.wait_ge(lo2_ready, 2 * (U * b + u) + 2)
                for t in range(4):
                    cut = slice(128 * t, 128 * t + 128)
                    for k in range(2):
                        mm = three(py[c][:, t, :], (h2hi[u % 2][:, k, cut], h2lo[u % 2][:, k, cut]),
                                   (whi[:, e, 2, k, :], wlo[:, e, 2, k, :]),
                                   e == 0 and k == 0 and t % 2 == 0, e == NE - 1 and k == 1)
                mm.then_inc(y_ready, 1)

            router_logits()
            router_turn()
            hidden1(0, 0, True)
            router_weights()

            def body(b, first, last):
                for s in range(U):
                    if s + 1 < U:
                        hidden1(b, s + 1, first)
                    elif not last:
                        hidden1(b + 1, 0, False)
                    hidden2(b, s, first)
                    if first and s == 0:
                        output_biases()
                    if s > 0:
                        output(b, s - 1, first)
                    elif not first:
                        output(b - 1, U - 1, False)

            body(0, True, False)
            with pe.Fori(1, B - 1) as b:
                body(b, False, False)
            body(B - 1, False, True)
            output(B - 1, U - 1, False)

        def flat(a):
            return a.rearrange("p k n -> p (k n)")

        @block.scalar
        def _(act):
            def weights_high(e):
                for j in range(3):
                    i = 3 * e + j
                    act.wait_ge(stage_in[i % NS], 16 * (i // NS + 1))
                    nc.scalar.activation(flat(whi[:, e, j]), flat(stage[i % NS]), ACT.Copy).then_inc(wsplit_hi, 1)

            act.wait_ge(router_in, 16 * 3)
            for n in range(4):
                act.wait_ge(featT_made, n + 1)
                nc.scalar.activation(featT[:, n // 2, 512 * (n % 2):512 * (n % 2) + 512], four[n][:], ACT.Copy,
                                     scale=1.0 / B).then_inc(featT_ready, 1)
            weights_high(0)
            act.wait_ge(logitsT_made, 1)
            nc.scalar.activation(wT, logitsT.rearrange("p h n -> p (h n)"), ACT.Identity,
                                 bias=br_sb[:]).then_inc(logitsT_ready, 1)
            act.wait_ge(soft, 2)
            nc.scalar.activation(flat(wt[:]), flat(lg[:]), ACT.Exp).then_inc(exp_ready, 1)
            weights_high(1)
            act.wait_ge(bn_ready, 2)

            def relu(b, u, layer, first):
                e = u % NE
                ready, done, lo_done, p, r = ((h1_ready, r1_ready, lo1_ready, p1, r1),
                                              (h2_ready, r2_ready, lo2_ready, p2, r2))[layer]
                for m in range(2):
                    n = 2 * (U * b + u) + m
                    act.wait_ge(ready, n + 1)
                    if u > 0 or not first:
                        act.wait_ge(lo_done, n - 1)
                    nc.scalar.activation(r[m][:], p[m][:], ACT.Relu, bias=bn_[layer][1][:, m, e:e + 1],
                                         scale=rs[layer][:, m, e:e + 1]).then_inc(done, 1)

            def high2(b, u, first):
                for m in range(2):
                    n = 2 * (U * b + u) + m
                    if m == 0 and (u >= 2 or not first):
                        act.wait_ge(y_ready, U * b + u - 1)
                    act.wait_ge(w2_ready, n + 1)
                    nc.scalar.activation(h2hi[u % 2][:, m, :], r2[m][:], ACT.Copy).then_inc(hi2_ready, 1)

            relu(0, 0, 0, True)

            def body(b, first, last):
                for s in range(U):
                    if s > 0:
                        high2(b, s - 1, first)
                    elif not first:
                        high2(b - 1, U - 1, False)
                    if s + 1 < U:
                        relu(b, s + 1, 0, first)
                    elif not last:
                        relu(b + 1, 0, 0, False)
                    relu(b, s, 1, first)
                    if first and s + 2 < NE:
                        weights_high(s + 2)

            body(0, True, False)
            with act.Fori(1, B - 1) as b:
                body(b, False, False)
            body(B - 1, False, True)
            high2(B - 1, U - 1, False)

        @block.vector
        def _(dve):
            def weights_low(e):
                for j in range(3):
                    i = 3 * e + j
                    dve.wait_ge(wsplit_hi, i + 1)
                    nc.vector.tensor_tensor(flat(wlo[:, e, j]), flat(stage[i % NS]), flat(whi[:, e, j]).bitcast(F32), ALU.subtract).then_inc(wsplit, 1)

            def split_x(b, c, first=False):
                dve.wait_ge(x_in, 16 * (2 * b + c + 1))
                if not first:
                    dve.wait_ge(h1_ready, 2 * (U * b + NE * c - NE))
                nc.vector.tensor_copy(flat(xhi[c][:]), flat(xraw[:])).then_inc(x_split_hi, 1)
                dve.wait_ge(x_split_hi, 2 * b + c + 1)
                nc.vector.tensor_tensor(flat(xlo[c][:]), flat(xraw[:]), flat(xhi[c][:]).bitcast(F32),
                                        ALU.subtract).then_inc(x_split, 1)

            split_x(0, 0, True)
            weights_low(0)
            dve.wait_ge(consts, 16 * 2)
            for n in range(2):
                g, bb, be, m, v = (flat(a) for a in bn_[n])
                nc.vector.tensor_scalar(v, v, BN_EPS, None, ALU.add).then_inc(bn_eps, 1)
                nc.vector.tensor_tensor(bb, bb, m, ALU.subtract).then_inc(bn_step, 1)
            dve.wait_ge(logits_made, 1)
            nc.vector.tensor_reduce(nm[:], logits, AX.X, ALU.max, negate=True).then_inc(soft, 1)
            dve.wait_ge(soft, 1)
            nc.vector.tensor_tensor(lg[:], logits, nm[:].unsqueeze(2).to_broadcast([128, NT, NE]), ALU.add).then_inc(soft, 1)
            dve.wait_ge(exp_ready, 1)
            nc.vector.tensor_reduce(sm[:], wt[:], AX.X, ALU.add).then_inc(soft, 1)
            dve.wait_ge(soft, 3)
            nc.vector.reciprocal(rsm[:], sm[:]).then_inc(soft, 1)
            dve.wait_ge(soft, 4)
            nc.vector.tensor_tensor(wt[:], wt[:], rsm[:].unsqueeze(2).to_broadcast([128, NT, NE]), ALU.mult).then_inc(soft, 1)
            for n in range(2):
                g, bb, be, m, v = (flat(a) for a in bn_[n])
                dve.wait_ge(bn_rs, n + 1)
                nc.vector.tensor_tensor(flat(rs[n][:]), flat(rs[n][:]), g, ALU.mult).then_inc(bn_step, 1)
                dve.wait_ge(bn_step, 3 + 2 * n)
                nc.vector.tensor_tensor(bb, bb, flat(rs[n][:]), ALU.mult).then_inc(bn_step, 1)
                dve.wait_ge(bn_step, 4 + 2 * n)
                nc.vector.tensor_tensor(bb, bb, be, ALU.add).then_inc(bn_ready, 1)
            dve.wait_ge(wT_made, 1)
            nc.vector.tensor_copy(wT, wT_psum.rearrange("p h n -> p (h n)")).then_inc(wT_ready, 1)
            weights_low(1)

            def take_biases():
                for c in range(2):
                    dve.wait_ge(bias_made, c + 1)
                    if c == 1:
                        dve.wait_ge(wT_out, 16)
                    nc.vector.tensor_copy(flat(bias[c][:]), flat(py[c][:])).then_inc(bias_ready, 1)

            def split1(b, u, first):
                for m in range(2):
                    n = 2 * (U * b + u) + m
                    dve.wait_ge(r1_ready, n + 1)
                    if m == 0 and (u >= 2 or not first):
                        dve.wait_ge(h2_ready, 2 * (U * b + u) - 2)
                    nc.vector.tensor_copy(h1hi[u % 2][:, m, :], r1[m][:]).then_inc(hi1_ready, 1)
                    dve.wait_ge(hi1_ready, n + 1)
                    nc.vector.tensor_tensor(h1lo[u % 2][:, m, :], r1[m][:], h1hi[u % 2][:, m, :].bitcast(F32),
                                            ALU.subtract).then_inc(lo1_ready, 1)

            def weigh(b, u, first):
                c, e = u // NE, u % NE
                if first and c == 0:
                    dve.wait_ge(wbc_in[e], 16)
                for m in range(2):
                    dve.wait_ge(r2_ready, 2 * (U * b + u) + m + 1)
                    nc.vector.tensor_tensor(r2[m][:], r2[m][:], wbc[e][:, CH * c:CH * c + CH], ALU.mult).then_inc(w2_ready, 1)

            def low2(b, u):
                for m in range(2):
                    dve.wait_ge(hi2_ready, 2 * (U * b + u) + m + 1)
                    nc.vector.tensor_tensor(h2lo[u % 2][:, m, :], r2[m][:], h2hi[u % 2][:, m, :].bitcast(F32),
                                            ALU.subtract).then_inc(lo2_ready, 1)

            def finish(b, c):
                dve.wait_ge(y_ready, U * b + NE * c + NE)
                dve.wait_ge(biased[c], b + 1)
                nc.vector.tensor_tensor(flat(res[c][:]), flat(py[c][:]), flat(res[c][:]), ALU.add).then_inc(y_read, 1)

            split1(0, 0, True)

            def body(b, first, last):
                for s in range(U):
                    if s > 0:
                        low2(b, s - 1)
                    elif not first:
                        low2(b - 1, U - 1)
                    if s + 1 < U:
                        split1(b, s + 1, first)
                    elif not last:
                        split1(b + 1, 0, False)
                    if first and s == 0:
                        take_biases()
                    weigh(b, s, first)
                    if first and s + 2 < NE:
                        weights_low(s + 2)
                    if s == 1 and not first:
                        finish(b - 1, 1)
                    if s == NE + 1:
                        finish(b, 0)
                    if s == 4:
                        split_x(b, 1, first)
                    if s == NE + 4 and not last:
                        split_x(b + 1, 0)

            body(0, True, False)
            with dve.Fori(1, B - 1) as b:
                body(b, False, False)
            body(B - 1, False, True)
            low2(B - 1, U - 1)
            finish(B - 1, 1)

        @block.gpsimd
        def _(pool):
            nc.gpsimd.memset(mhalf[:], -0.5).then_inc(made, 1)
            pool.wait_ge(made, 1)
            for n in range(2):
                pool.wait_ge(bn_eps, n + 1)
                nc.gpsimd.tensor_tensor(flat(rs[n][:]), flat(bn_[n][4]), flat(mhalf[:]), ALU.pow).then_inc(bn_rs, 1)
            pool.wait_ge(bias_ready, 2)

            def add_biases(b):
                for c in range(2):
                    pool.wait_ge(res_in[c], 16 * (b + 1))
                    nc.gpsimd.tensor_tensor(flat(res[c][:]), flat(res[c][:]), flat(bias[c][:]), ALU.add).then_inc(biased[c], 1)

            add_biases(0)
            with pool.Fori(1, B) as b:
                add_biases(b)


def program(nc, I, out):
    B, L, E = I["x"].shape
    x1 = nc.dram_tensor("x1_scratch", (B, L, E), F32, kind="Internal").ap()
    t2 = nc.dram_tensor("t2_scratch", (B, L, E), F32, kind="Internal").ap()
    xn2T = nc.dram_tensor("xn2T_scratch", (B, E, L), F32, kind="Internal").ap()
    router = nc.dram_tensor("router_scratch", (I["wr"].shape[1], L), F32, kind="Internal").ap()
    layer0(nc, I["x"], I["xT"], I["wqT0"], I["wkT0"], I["wvT0"], I["woT0"], I["ln_g"], I["ln_b"], I["window"],
           I["rowscale"], I["cosT"], I["sinT"], I["avg8"], I["ident"], x1)
    with nc.sbuf_tensor("feat", [128, L // 128, E], F32) as feat:
        layer1_attention(nc, x1, I["wqT1"], I["wkT1"], I["wv1"], I["ident"], I["causal"], t2, xn2T, feat)
        layer1_experts(nc, t2, xn2T, feat, I["wr"], I["br"], I["w1"], I["w2"], I["wo"], I["bo"], I["bn"], I["ident"],
                       router, out)


def shape_constants(H=8, R=32):
    gamma = 1.0 - 2.0 ** (-2.0 - 5.0 * np.arange(H) / H)
    i = np.arange(R)
    factor = 1 / np.sqrt((gamma[:, None, None] ** np.abs(i[:, None] - i[None, :])).sum(-1))
    r, j2, u = np.arange(128) // R, np.arange(128) % R, np.arange(4 - R, R)
    dist = np.abs(u[None, None, :, None] - r[:, None, None, None]) + np.abs(i[None, None, None, :] - j2[:, None, None, None])
    window = gamma[None, :, None, None] ** dist * factor[None, :, None, :]
    rowscale = np.stack([factor[4 * g + np.arange(128) // 32] for g in range(2)], 1)
    angle = np.repeat(1.0 / 10000.0 ** np.linspace(0.0, 1.0, 16), 2)
    turn = (i[:, None] + i[None, :]).reshape(-1)[None, :] * angle[:, None]
    sine = np.sin(turn)
    sine[0::2] *= -1
    tri = np.arange(128)
    out = {
        "window": window.reshape(128, H, -1), "rowscale": rowscale, "cosT": np.tile(np.cos(turn), (4, 1)),
        "sinT": np.tile(sine, (4, 1)), "avg8": np.kron(np.eye(16), np.full((8, 8), 1 / 8)), "ident": np.eye(128),
        "causal": np.where(tri[None, :] > tri[:, None], -3e38, 0.0),
    }
    return {k: np.ascontiguousarray(v, dtype=np.float32) for k, v in out.items()}


def kernel(**inputs):
    import concourse.bacc as bacc
    from concourse.bass_utils import run_bass_kernel_spmd

    a = {k: np.asarray(v) for k, v in inputs.items()}
    B, N1, N2, E = a["x"].shape
    x = a["x"].reshape(B, N1 * N2, E)
    arrays = {"x": x, "xT": x.transpose(0, 2, 1)}
    for n, k in (("wqT0", "Wq"), ("wkT0", "Wk"), ("wvT0", "Wv"), ("woT0", "Wo")):
        arrays[n] = a["L0_conv_" + k].T
    for n in ("g", "b"):
        arrays["ln_" + n] = np.tile(a["L0_conv_ln_" + n], 4)[:, None]
    arrays |= {"wqT1": a["L1_attn_Wq"].T, "wkT1": a["L1_attn_Wk"].T, "wv1": a["L1_attn_Wv"]}
    for n in ("Wr", "W1", "W2", "Wo", "bo"):
        arrays[n.lower()] = a["L1_ffn_" + n]
    arrays["br"] = a["L1_ffn_br"][:, None]
    bn = np.stack([a["L1_ffn_" + n + layer].T for layer in "12" for n in ("g", "b", "be", "m", "v")])
    arrays["bn"] = bn.reshape(10, -1, 128, bn.shape[-1]).transpose(2, 0, 1, 3)
    arrays |= shape_constants()
    arrays = {"in_" + k: np.ascontiguousarray(v) for k, v in arrays.items()}

    nc = bacc.Bacc("TRN2", target_bir_lowering=False, num_devices=1)
    I = {k[3:]: nc.dram_tensor(k, v.shape, mybir.dt.from_np(v.dtype), kind="ExternalInput").ap() for k, v in arrays.items()}
    out = nc.dram_tensor("out", (B, N1 * N2, E), F32, kind="ExternalOutput").ap()
    program(nc, I, out)
    r = run_bass_kernel_spmd(nc, [arrays], core_ids=[0])
    return r.results[0]["out"].reshape(B, N1, N2, E)
```
